# Optimizing a Trainium2 kernel written in Bass

```python
import numpy as np
import jax
import jax.numpy as jnp

def _softmax(x, axis=-1):
    return jax.nn.softmax(x, axis=axis)

def _gelu(x):
    return jax.nn.gelu(x, approximate=True)

def _silu(x):
    return jax.nn.silu(x)

def _sigmoid(x):
    return jax.nn.sigmoid(x)

def _layernorm(x, axis=-1, eps=1e-05):
    m = jnp.mean(x, axis=axis, keepdims=True)
    v = jnp.var(x, axis=axis, keepdims=True)
    return (x - m) / jnp.sqrt(v + eps)

def _scatter_add(tgt, idx, src, axis=0):
    return tgt.at[idx].add(src)

def _segment_sum(src, seg, n):
    return jax.ops.segment_sum(src, seg, n)
kernel_name = 'mk_decoder_postln_d4_seqx_r8_118ecd'

def setup_inputs(seed: int=0):
    np.random.seed(seed)
    _w = jnp.asarray

    def _rec_inputs():
        import jax
        import jax.numpy as jnp
        _rk = jax.random.key(seed)
        x = 7.22e-05 + 1 * jax.random.normal(jax.random.fold_in(_rk, 1), (16, 64, 512), jnp.float32)
        _lenS = 64 - jax.random.randint(jax.random.fold_in(_rk, 7), (16,), 0, max(1, 64 // 4) + 1, jnp.int32)
        _lenS2 = 64 - jax.random.randint(jax.random.fold_in(_rk, 8), (16,), 0, max(1, 64 // 4) + 1, jnp.int32)
        _ctx_4096P = jax.random.normal(jax.random.fold_in(_rk, 11), (16, 16, 512), jnp.float32)
        _ctx_4096c = jax.random.dirichlet(jax.random.fold_in(_rk, 511), 0.3 * jnp.ones((16,), jnp.float32), (16, 64))
        _ctx_4096t = jnp.einsum('bsk,bkd->bsd', _ctx_4096c, _ctx_4096P)
        _ctx_4096t = _ctx_4096t * jax.lax.rsqrt(jnp.mean(jnp.square(_ctx_4096t)) + 1e-12) * 0.953939
        ctx_4096 = 4.13588e-05 + 0.999923 * (_ctx_4096t + 0.3 * jax.random.normal(jax.random.fold_in(_rk, 611), (16, 64, 512), jnp.float32))
        fside_Bx32xSxS2_0 = 1.74963e-06 + 0.0200011 * jax.random.normal(jax.random.fold_in(_rk, 14), (16, 32, 64, 64), jnp.float32)
        _validS = jnp.arange(64)[None, :] < _lenS[:, None]
        _validS2 = jnp.arange(64)[None, :] < _lenS2[:, None]
        _causal = jnp.tril(jnp.ones((64, 64), dtype=bool))
        mask_1x1xSxS2_ff0 = jnp.where(jnp.ones((1, 1, 64, 64), dtype=bool), 0.0, -1000000000.0).astype(jnp.float32)
        mask_BxSxS2_bk0 = jnp.logical_not(jnp.broadcast_to(_validS2[:, None, :], (16, 64, 64)))
        return (x, ctx_4096, fside_Bx32xSxS2_0, mask_1x1xSxS2_ff0, mask_BxSxS2_bk0)
    x, ctx_4096, fside_Bx32xSxS2_0, mask_1x1xSxS2_ff0, mask_BxSxS2_bk0 = _rec_inputs()

    def _L0_attn_setup():
        import jax, jax.numpy as jnp
        import numpy as np
        import math
        NH, NKV, D = (32, 8, 128)

        def _alibi_slopes(n):
            cp2 = 2 ** math.floor(math.log2(n))
            base = 2.0 ** (-8.0 / cp2)
            slopes = base ** np.arange(1, cp2 + 1, dtype=np.float32)
            if cp2 != n:
                extra_base = 2.0 ** (-4.0 / cp2)
                extra = extra_base ** np.arange(1, 1 + 2 * (n - cp2), 2, dtype=np.float32)
                slopes = np.concatenate([slopes, extra])
            return slopes.astype(np.float32)
        key = jax.random.key(seed)
        k1, k2, k3 = jax.random.split(key, 3)
        B, S, H = (4, 128, 512)
        qkv_out = NH * D + 2 * NKV * D
        return {'hidden_states': jax.random.normal(k1, (B, S, H), jnp.float32) * 0.02, 'w_qkv': jax.random.normal(k2, (H, qkv_out), jnp.float32) * 0.02, 'w_o': jax.random.normal(k3, (NH * D, H), jnp.float32) * 0.02}
    _L0_attn_all = _L0_attn_setup()
    _L0_attn_in = {k: v for k, v in _L0_attn_all.items() if k in ('w_qkv', 'w_o')}
    del _L0_attn_all

    def _L0_xattn_setup():
        import jax, jax.numpy as jnp
        import numpy as np
        DIM = 512
        NUM_HEADS = 32
        NUM_KV_HEADS = 8
        HEAD_DIM = DIM // NUM_HEADS
        KV_DIM = DIM // (NUM_HEADS // NUM_KV_HEADS)
        B, S = (1, 256)
        key = jax.random.key(seed)
        ks = jax.random.split(key, 7)
        w_scale = DIM ** (-0.5)
        return {'query': jax.random.normal(ks[0], (B, S, DIM), jnp.float32), 'key': jax.random.normal(ks[1], (B, S, DIM), jnp.float32), 'value': jax.random.normal(ks[2], (B, S, DIM), jnp.float32), 'Wq': jax.random.normal(ks[3], (DIM, DIM), jnp.float32) * w_scale, 'Wk': jax.random.normal(ks[4], (DIM, KV_DIM), jnp.float32) * w_scale, 'Wv': jax.random.normal(ks[5], (DIM, KV_DIM), jnp.float32) * w_scale, 'Wo': jax.random.normal(ks[6], (DIM, DIM), jnp.float32) * w_scale}
    _L0_xattn_all = _L0_xattn_setup()
    _L0_xattn_in = {k: v for k, v in _L0_xattn_all.items() if k in ('Wq', 'Wk', 'Wv', 'Wo')}
    del _L0_xattn_all

    def _L0_ffn_setup():
        import jax, jax.numpy as jnp
        import numpy as np
        NUM_EXPERTS = 4
        HIDDEN = 512
        RANK = 8
        ALPHA = 8.0
        SCALE = ALPHA / RANK
        key = jax.random.key(seed)
        ks = jax.random.split(key, 6)
        B, T, H, E, R = (4, 512, HIDDEN, NUM_EXPERTS, RANK)
        x = jax.random.normal(ks[0], (B, T, H), dtype=jnp.float32)
        W_up = jax.random.normal(ks[1], (H, H), dtype=jnp.float32) / np.sqrt(H)
        gate_w = jax.random.normal(ks[2], (E, H), dtype=jnp.float32) / np.sqrt(H)
        expert_bias = jnp.zeros((E,), dtype=jnp.float32)
        lora_A = jax.random.normal(ks[3], (E, R, H), dtype=jnp.float32) / np.sqrt(H)
        lora_B = jax.random.normal(ks[4], (E, H, R), dtype=jnp.float32) * 0.01
        return {'x': x, 'W_up': W_up, 'gate_w': gate_w, 'expert_bias': expert_bias, 'lora_A': lora_A, 'lora_B': lora_B}
    _L0_ffn_all = _L0_ffn_setup()
    _L0_ffn_in = {k: v for k, v in _L0_ffn_all.items() if k in ('W_up', 'gate_w', 'expert_bias', 'lora_A', 'lora_B')}
    del _L0_ffn_all

    def _L1_attn_setup():
        import jax, jax.numpy as jnp
        import numpy as np
        B, C, L = (32, 64, 512)
        key = jax.random.key(seed)
        k1, = jax.random.split(key, 1)
        minibatch = jax.random.normal(k1, (B, C, L), dtype=jnp.float32)
        eta = jnp.zeros((1,), dtype=jnp.float32)
        return {'minibatch': minibatch, 'eta': eta}
    _L1_attn_all = _L1_attn_setup()
    _L1_attn_in = {k: v for k, v in _L1_attn_all.items() if k in ('eta',)}
    del _L1_attn_all

    def _L1_xattn_setup():
        import jax, jax.numpy as jnp
        import numpy as np
        import math
        HIDDEN = 512
        N_HEADS = 32
        HEAD_DIM = 128
        N_KV_HEADS = 4
        N_GROUPS = N_HEADS // N_KV_HEADS
        key = jax.random.key(seed)
        ks = jax.random.split(key, 6)
        B, NL, S = (8, 64, 512)
        latents = jax.random.normal(ks[0], (B, NL, HIDDEN), dtype=jnp.float32)
        context = jax.random.normal(ks[1], (B, S, HIDDEN), dtype=jnp.float32)
        scale = 1.0 / math.sqrt(HIDDEN)
        Wq = jax.random.normal(ks[2], (HIDDEN, N_HEADS * HEAD_DIM), dtype=jnp.float32) * scale
        Wk = jax.random.normal(ks[3], (HIDDEN, N_KV_HEADS * HEAD_DIM), dtype=jnp.float32) * scale
        Wv = jax.random.normal(ks[4], (HIDDEN, N_KV_HEADS * HEAD_DIM), dtype=jnp.float32) * scale
        Wo = jax.random.normal(ks[5], (N_HEADS * HEAD_DIM, HIDDEN), dtype=jnp.float32) * scale
        return {'latents': latents, 'context': context, 'Wq': Wq, 'Wk': Wk, 'Wv': Wv, 'Wo': Wo}
    _L1_xattn_all = _L1_xattn_setup()
    _L1_xattn_in = {k: v for k, v in _L1_xattn_all.items() if k in ('Wq', 'Wk', 'Wv', 'Wo')}
    del _L1_xattn_all

    def _L1_ffn_setup():
        import jax, jax.numpy as jnp
        import numpy as np
        NUM_EXPERTS = 8
        TOP_K = 2
        RANK = 16
        LORA_ALPHA = 32
        SCALING = LORA_ALPHA / RANK
        key = jax.random.key(seed)
        ks = jax.random.split(key, 6)
        B, S, D_IN, D_OUT = (4, 256, 512, 512)
        x = jax.random.normal(ks[0], (B, S, D_IN), dtype=jnp.float32)
        W_base = jax.random.normal(ks[1], (D_OUT, D_IN), dtype=jnp.float32) * 0.02
        b_base = jax.random.normal(ks[2], (D_OUT,), dtype=jnp.float32) * 0.02
        W_router = jax.random.normal(ks[3], (NUM_EXPERTS, D_IN), dtype=jnp.float32) * 0.02
        A = jax.random.normal(ks[4], (NUM_EXPERTS, RANK, D_IN), dtype=jnp.float32) * 0.02
        Bm = jax.random.normal(ks[5], (D_OUT, RANK), dtype=jnp.float32) * 0.02
        Bm = jnp.broadcast_to(Bm, (NUM_EXPERTS, D_OUT, RANK)) * jnp.arange(1, NUM_EXPERTS + 1, dtype=jnp.float32)[:, None, None] * 0.2
        return {'x': x, 'W_base': W_base, 'b_base': b_base, 'W_router': W_router, 'A': A, 'B': Bm}
    _L1_ffn_all = _L1_ffn_setup()
    _L1_ffn_in = {k: v for k, v in _L1_ffn_all.items() if k in ('W_base', 'b_base', 'W_router', 'A', 'B')}
    del _L1_ffn_all

    def _L2_attn_setup():
        import jax, jax.numpy as jnp
        import numpy as np
        EMBED = 512
        H = 32
        KV = 8
        D = EMBED // H
        REP = H // KV

        def _rope(t, cos, sin):
            t = t.reshape(*t.shape[:-1], 2, D // 2)
            t1, t2 = (t[..., 0, :], t[..., 1, :])
            return jnp.concatenate([t1 * cos - t2 * sin, t1 * sin + t2 * cos], axis=-1)
        key = jax.random.key(seed)
        ks = jax.random.split(key, 7)
        B, S = (1, 256)
        x = jax.random.normal(ks[0], (B, S, EMBED), dtype=jnp.float32)
        wq = jax.random.normal(ks[1], (EMBED, EMBED), dtype=jnp.float32) * 0.02
        bq = jax.random.normal(ks[2], (EMBED,), dtype=jnp.float32) * 0.02
        wk = jax.random.normal(ks[3], (EMBED, KV * D), dtype=jnp.float32) * 0.02
        bk = jax.random.normal(ks[4], (KV * D,), dtype=jnp.float32) * 0.02
        wv = jax.random.normal(ks[5], (EMBED, KV * D), dtype=jnp.float32) * 0.02
        bv = jax.random.normal(ks[6], (KV * D,), dtype=jnp.float32) * 0.02
        return {'x': x, 'wq': wq, 'bq': bq, 'wk': wk, 'bk': bk, 'wv': wv, 'bv': bv}
    _L2_attn_all = _L2_attn_setup()
    _L2_attn_in = {k: v for k, v in _L2_attn_all.items() if k in ('wq', 'bq', 'wk', 'bk', 'wv', 'bv')}
    del _L2_attn_all

    def _L2_xattn_setup():
        import jax, jax.numpy as jnp
        import numpy as np
        NUM_HEADS = 32
        NUM_KV_HEADS = 8
        HEAD_DIM = 128
        HIDDEN = 512
        EPS = 1e-05

        def rmsnorm(x, w, eps=EPS):
            xf = x.astype(jnp.float32)
            var = jnp.mean(xf * xf, axis=-1, keepdims=True)
            return w * (xf * jax.lax.rsqrt(var + eps)).astype(x.dtype)
        key = jax.random.key(seed)
        ks = jax.random.split(key, 10)
        B, Q, KV = (1, 128, 6404)
        s = 1.0 / np.sqrt(HIDDEN)
        return {'hidden_states': jax.random.normal(ks[0], (B, Q, HIDDEN), jnp.float32), 'cross_attention_states': jax.random.normal(ks[1], (B, KV, HIDDEN), jnp.float32), 'attention_mask': jnp.zeros((B, 1, Q, KV), jnp.float32), 'q_proj_w': jax.random.normal(ks[2], (NUM_HEADS * HEAD_DIM, HIDDEN), jnp.float32) * s, 'k_proj_w': jax.random.normal(ks[3], (NUM_KV_HEADS * HEAD_DIM, HIDDEN), jnp.float32) * s, 'v_proj_w': jax.random.normal(ks[4], (NUM_KV_HEADS * HEAD_DIM, HIDDEN), jnp.float32) * s, 'o_proj_w': jax.random.normal(ks[5], (HIDDEN, NUM_HEADS * HEAD_DIM), jnp.float32) * s, 'q_norm_w': jnp.ones((HEAD_DIM,), jnp.float32), 'k_norm_w': jnp.ones((HEAD_DIM,), jnp.float32)}
    _L2_xattn_all = _L2_xattn_setup()
    _L2_xattn_in = {k: v for k, v in _L2_xattn_all.items() if k in ('q_proj_w', 'k_proj_w', 'v_proj_w', 'o_proj_w', 'q_norm_w', 'k_norm_w')}
    del _L2_xattn_all

    def _L2_ffn_setup():
        import jax, jax.numpy as jnp
        import numpy as np
        HID, BOT, RDIM, NSLOT, K, VB = (512, 64, 48, 128, 8, 32)
        TAU_LOW, TAU_HIGH, EARLY_EXIT = (0.5, 2.0, 0.05)

        def _uncertainty(h, Wu1, bu1, Wu2, bu2):
            var = jnp.var(h, axis=-1)
            log_var = jnp.log1p(var)
            norm_var = log_var / (jnp.mean(log_var) + 1e-06)
            learned = (jax.nn.gelu(h @ Wu1.T + bu1) @ Wu2.T + bu2)[..., 0]
            return jnp.clip(norm_var * 0.5 + jax.nn.sigmoid(learned) * 2.5, 0.0, 5.0)
        key = jax.random.key(seed)
        ks = jax.random.split(key, 12)
        B, S = (2, 256)
        return {'hidden_states': jax.random.normal(ks[0], (B, S, HID), dtype=jnp.float32), 'Wq': jax.random.normal(ks[1], (BOT, HID), dtype=jnp.float32) / np.sqrt(HID), 'Wr': jax.random.normal(ks[2], (RDIM, BOT), dtype=jnp.float32) / np.sqrt(BOT), 'aux_keys': jax.random.normal(ks[3], (NSLOT, BOT), dtype=jnp.float32) * 0.01, 'aux_values': jax.random.normal(ks[4], (NSLOT, HID), dtype=jnp.float32) * 0.02, 'Wvd': jax.random.normal(ks[5], (VB, HID), dtype=jnp.float32) * 0.1 / np.sqrt(HID), 'Wvu': jax.random.normal(ks[6], (HID, VB), dtype=jnp.float32) * 0.1 / np.sqrt(VB), 'Wu1': jax.random.normal(ks[7], (HID // 4, HID), dtype=jnp.float32) / np.sqrt(HID), 'bu1': jnp.zeros((HID // 4,), dtype=jnp.float32), 'Wu2': jax.random.normal(ks[8], (1, HID // 4), dtype=jnp.float32) * 0.01, 'bu2': jnp.zeros((1,), dtype=jnp.float32), 'gate_w1': jnp.float32(0.5), 'gate_bias': jnp.float32(-1.0), 'log_rel': jnp.zeros((NSLOT,), dtype=jnp.float32)}
    _L2_ffn_all = _L2_ffn_setup()
    _L2_ffn_in = {k: v for k, v in _L2_ffn_all.items() if k in ('Wq', 'Wr', 'aux_keys', 'aux_values', 'Wvd', 'Wvu', 'Wu1', 'bu1', 'Wu2', 'bu2', 'gate_w1', 'gate_bias', 'log_rel')}
    del _L2_ffn_all

    def _L3_attn_setup():
        import math
        import jax, jax.numpy as jnp
        import numpy as np
        NUM_HEADS = 32
        HIDDEN = 512
        HEAD_DIM = HIDDEN // NUM_HEADS
        NEG_INF = -1e+30

        def _alibi_slopes(n: int) -> jnp.ndarray:
            cp2 = 2 ** math.floor(math.log2(n))
            base = 2.0 ** (-2.0 ** (-(math.log2(cp2) - 3)))
            slopes = base ** np.arange(1, cp2 + 1, dtype=np.float64)
            if cp2 != n:
                extra_base = 2.0 ** (-2.0 ** (-(math.log2(2 * cp2) - 3)))
                rem = min(cp2, n - cp2)
                extra = extra_base ** np.arange(1, 1 + 2 * rem, 2, dtype=np.float64)
                slopes = np.concatenate([slopes, extra])
            return jnp.asarray(slopes, dtype=jnp.float32)
        key = jax.random.key(seed)
        k1, k2, k3 = jax.random.split(key, 3)
        B, S = (2, 256)
        hidden_states = jax.random.normal(k1, (B, S, HIDDEN), dtype=jnp.float32)
        Wqkv = jax.random.normal(k2, (HIDDEN, NUM_HEADS * HEAD_DIM + 2 * HEAD_DIM), dtype=jnp.float32) * 0.02
        Wo = jax.random.normal(k3, (HIDDEN, HIDDEN), dtype=jnp.float32) * 0.02
        return {'hidden_states': hidden_states, 'Wqkv': Wqkv, 'Wo': Wo}
    _L3_attn_all = _L3_attn_setup()
    _L3_attn_in = {k: v for k, v in _L3_attn_all.items() if k in ('Wqkv', 'Wo')}
    del _L3_attn_all

    def _L3_xattn_setup():
        import jax, jax.numpy as jnp
        import numpy as np
        B, S, D, H, DH = (2, 128, 512, 32, 128)
        key = jax.random.key(seed)
        ks = jax.random.split(key, 7)
        hidden_q = jax.random.normal(ks[0], (B, S, D), dtype=jnp.float32)
        hidden_kv = jax.random.normal(ks[1], (B, S, D), dtype=jnp.float32)
        attention_mask = jnp.tril(jnp.ones((B, S, S), dtype=bool))
        position_bias = jax.random.normal(ks[2], (B, H, S, S), dtype=jnp.float32) * 0.02
        Wq = jax.random.normal(ks[3], (D, H * DH), dtype=jnp.float32) * 0.02
        Wk = jax.random.normal(ks[4], (D, H * DH), dtype=jnp.float32) * 0.02
        Wv = jax.random.normal(ks[5], (D, H * DH), dtype=jnp.float32) * 0.02
        Wo = jax.random.normal(ks[6], (H * DH, D), dtype=jnp.float32) * 0.02
        return {'hidden_q': hidden_q, 'hidden_kv': hidden_kv, 'attention_mask': attention_mask, 'position_bias': position_bias, 'Wq': Wq, 'Wk': Wk, 'Wv': Wv, 'Wo': Wo}
    _L3_xattn_all = _L3_xattn_setup()
    _L3_xattn_in = {k: v for k, v in _L3_xattn_all.items() if k in ('Wq', 'Wk', 'Wv', 'Wo')}
    del _L3_xattn_all

    def _L3_ffn_setup():
        import jax, jax.numpy as jnp
        import numpy as np
        import math
        B, S, IN, OUT = (4, 256, 512, 512)
        E, R, K = (8, 64, 128)
        SCALE = 64.0 / 64.0
        MULTIPLIER = 1.0
        key = jax.random.key(seed)
        ks = jax.random.split(key, 6)
        return {'x': jax.random.normal(ks[0], (B, S, IN), jnp.float32), 'W_org': jax.random.normal(ks[1], (OUT, IN), jnp.float32) * 0.02, 'lora_down': jax.random.normal(ks[2], (E, IN, R), jnp.float32) * 0.02, 'lora_up': jax.random.normal(ks[3], (E, R, OUT), jnp.float32) * 0.02, 'lora_keys': jax.random.normal(ks[4], (E, K), jnp.float32), 'Wq': jax.random.normal(ks[5], (K, IN), jnp.float32) * 0.02}
    _L3_ffn_all = _L3_ffn_setup()
    _L3_ffn_in = {k: v for k, v in _L3_ffn_all.items() if k in ('W_org', 'lora_down', 'lora_up', 'lora_keys', 'Wq')}
    del _L3_ffn_all
    return {'x': x, 'ctx_4096': ctx_4096, 'fside_Bx32xSxS2_0': fside_Bx32xSxS2_0, 'mask_1x1xSxS2_ff0': mask_1x1xSxS2_ff0, 'mask_BxSxS2_bk0': mask_BxSxS2_bk0, 'L0_attn_w_qkv': _L0_attn_in['w_qkv'], 'L0_attn_w_o': _L0_attn_in['w_o'], 'L0_xattn_Wq': _L0_xattn_in['Wq'], 'L0_xattn_Wk': _L0_xattn_in['Wk'], 'L0_xattn_Wv': _L0_xattn_in['Wv'], 'L0_xattn_Wo': _L0_xattn_in['Wo'], 'L0_ffn_W_up': _L0_ffn_in['W_up'], 'L0_ffn_gate_w': _L0_ffn_in['gate_w'], 'L0_ffn_expert_bias': _L0_ffn_in['expert_bias'], 'L0_ffn_lora_A': _L0_ffn_in['lora_A'], 'L0_ffn_lora_B': _L0_ffn_in['lora_B'], 'L1_attn_eta': _L1_attn_in['eta'], 'L1_xattn_Wq': _L1_xattn_in['Wq'], 'L1_xattn_Wk': _L1_xattn_in['Wk'], 'L1_xattn_Wv': _L1_xattn_in['Wv'], 'L1_xattn_Wo': _L1_xattn_in['Wo'], 'L1_ffn_W_base': _L1_ffn_in['W_base'], 'L1_ffn_b_base': _L1_ffn_in['b_base'], 'L1_ffn_W_router': _L1_ffn_in['W_router'], 'L1_ffn_A': _L1_ffn_in['A'], 'L1_ffn_B': _L1_ffn_in['B'], 'L2_attn_wq': _L2_attn_in['wq'], 'L2_attn_bq': _L2_attn_in['bq'], 'L2_attn_wk': _L2_attn_in['wk'], 'L2_attn_bk': _L2_attn_in['bk'], 'L2_attn_wv': _L2_attn_in['wv'], 'L2_attn_bv': _L2_attn_in['bv'], 'L2_xattn_q_proj_w': _L2_xattn_in['q_proj_w'], 'L2_xattn_k_proj_w': _L2_xattn_in['k_proj_w'], 'L2_xattn_v_proj_w': _L2_xattn_in['v_proj_w'], 'L2_xattn_o_proj_w': _L2_xattn_in['o_proj_w'], 'L2_xattn_q_norm_w': _L2_xattn_in['q_norm_w'], 'L2_xattn_k_norm_w': _L2_xattn_in['k_norm_w'], 'L2_ffn_Wq': _L2_ffn_in['Wq'], 'L2_ffn_Wr': _L2_ffn_in['Wr'], 'L2_ffn_aux_keys': _L2_ffn_in['aux_keys'], 'L2_ffn_aux_values': _L2_ffn_in['aux_values'], 'L2_ffn_Wvd': _L2_ffn_in['Wvd'], 'L2_ffn_Wvu': _L2_ffn_in['Wvu'], 'L2_ffn_Wu1': _L2_ffn_in['Wu1'], 'L2_ffn_bu1': _L2_ffn_in['bu1'], 'L2_ffn_Wu2': _L2_ffn_in['Wu2'], 'L2_ffn_bu2': _L2_ffn_in['bu2'], 'L2_ffn_gate_w1': _L2_ffn_in['gate_w1'], 'L2_ffn_gate_bias': _L2_ffn_in['gate_bias'], 'L2_ffn_log_rel': _L2_ffn_in['log_rel'], 'L3_attn_Wqkv': _L3_attn_in['Wqkv'], 'L3_attn_Wo': _L3_attn_in['Wo'], 'L3_xattn_Wq': _L3_xattn_in['Wq'], 'L3_xattn_Wk': _L3_xattn_in['Wk'], 'L3_xattn_Wv': _L3_xattn_in['Wv'], 'L3_xattn_Wo': _L3_xattn_in['Wo'], 'L3_ffn_W_org': _L3_ffn_in['W_org'], 'L3_ffn_lora_down': _L3_ffn_in['lora_down'], 'L3_ffn_lora_up': _L3_ffn_in['lora_up'], 'L3_ffn_lora_keys': _L3_ffn_in['lora_keys'], 'L3_ffn_Wq': _L3_ffn_in['Wq']}

def reference(x, ctx_4096, fside_Bx32xSxS2_0, mask_1x1xSxS2_ff0, mask_BxSxS2_bk0, L0_attn_w_qkv, L0_attn_w_o, L0_xattn_Wq, L0_xattn_Wk, L0_xattn_Wv, L0_xattn_Wo, L0_ffn_W_up, L0_ffn_gate_w, L0_ffn_expert_bias, L0_ffn_lora_A, L0_ffn_lora_B, L1_attn_eta, L1_xattn_Wq, L1_xattn_Wk, L1_xattn_Wv, L1_xattn_Wo, L1_ffn_W_base, L1_ffn_b_base, L1_ffn_W_router, L1_ffn_A, L1_ffn_B, L2_attn_wq, L2_attn_bq, L2_attn_wk, L2_attn_bk, L2_attn_wv, L2_attn_bv, L2_xattn_q_proj_w, L2_xattn_k_proj_w, L2_xattn_v_proj_w, L2_xattn_o_proj_w, L2_xattn_q_norm_w, L2_xattn_k_norm_w, L2_ffn_Wq, L2_ffn_Wr, L2_ffn_aux_keys, L2_ffn_aux_values, L2_ffn_Wvd, L2_ffn_Wvu, L2_ffn_Wu1, L2_ffn_bu1, L2_ffn_Wu2, L2_ffn_bu2, L2_ffn_gate_w1, L2_ffn_gate_bias, L2_ffn_log_rel, L3_attn_Wqkv, L3_attn_Wo, L3_xattn_Wq, L3_xattn_Wk, L3_xattn_Wv, L3_xattn_Wo, L3_ffn_W_org, L3_ffn_lora_down, L3_ffn_lora_up, L3_ffn_lora_keys, L3_ffn_Wq):
    import jax
    import jax.numpy as jnp

    def _L0_attn_ref(hidden_states, w_qkv, w_o):
        import jax, jax.numpy as jnp
        import numpy as np
        import math
        NH, NKV, D = (32, 8, 128)

        def _alibi_slopes(n):
            cp2 = 2 ** math.floor(math.log2(n))
            base = 2.0 ** (-8.0 / cp2)
            slopes = base ** np.arange(1, cp2 + 1, dtype=np.float32)
            if cp2 != n:
                extra_base = 2.0 ** (-4.0 / cp2)
                extra = extra_base ** np.arange(1, 1 + 2 * (n - cp2), 2, dtype=np.float32)
                slopes = np.concatenate([slopes, extra])
            return slopes.astype(np.float32)
        B, S, H = hidden_states.shape
        G = NH // NKV
        scale = D ** (-0.5)
        qkv = hidden_states @ w_qkv
        q = qkv[..., :NH * D].reshape(B, S, NKV, G, D)
        k = qkv[..., NH * D:NH * D + NKV * D].reshape(B, S, NKV, D)
        v = qkv[..., NH * D + NKV * D:].reshape(B, S, NKV, D)
        scores = jnp.einsum('bqhgd,bkhd->bhgqk', q, k) * scale
        slopes = jnp.asarray(_alibi_slopes(NH)).reshape(NKV, G)
        pos = jnp.arange(S)
        rel = pos[:, None] - pos[None, :]
        sqrt_dist = jnp.sqrt(jnp.maximum(rel, 0).astype(jnp.float32))
        bias = -slopes[:, :, None, None] * sqrt_dist
        bias = jnp.where(rel[None, None] >= 0, bias, -jnp.inf)
        attn = jax.nn.softmax(scores + bias[None], axis=-1)
        out = jnp.einsum('bhgqk,bkhd->bqhgd', attn, v).reshape(B, S, NH * D)
        return out @ w_o

    def _L0_xattn_ref(query, key, value, Wq, Wk, Wv, Wo):
        import jax, jax.numpy as jnp
        import numpy as np
        DIM = 512
        NUM_HEADS = 32
        NUM_KV_HEADS = 8
        HEAD_DIM = DIM // NUM_HEADS
        KV_DIM = DIM // (NUM_HEADS // NUM_KV_HEADS)
        B, S = (1, 256)
        b, sq, _ = query.shape
        _, sk, _ = key.shape
        rep = NUM_HEADS // NUM_KV_HEADS
        q = (query @ Wq).reshape(b, sq, NUM_HEADS, HEAD_DIM).transpose(0, 2, 1, 3)
        k = (key @ Wk).reshape(b, sk, NUM_KV_HEADS, HEAD_DIM).transpose(0, 2, 1, 3)
        v = (value @ Wv).reshape(b, sk, NUM_KV_HEADS, HEAD_DIM).transpose(0, 2, 1, 3)
        k = jnp.repeat(k, rep, axis=1)
        v = jnp.repeat(v, rep, axis=1)
        scale = HEAD_DIM ** (-0.5)
        scores = jnp.einsum('bhqd,bhkd->bhqk', q, k) * scale
        probs = jax.nn.softmax(scores, axis=-1)
        out = jnp.einsum('bhqk,bhkd->bhqd', probs, v)
        out = out.transpose(0, 2, 1, 3).reshape(b, sq, DIM)
        return out @ Wo

    def _L0_ffn_ref(x, W_up, gate_w, expert_bias, lora_A, lora_B):
        import jax, jax.numpy as jnp
        import numpy as np
        NUM_EXPERTS = 4
        HIDDEN = 512
        RANK = 8
        ALPHA = 8.0
        SCALE = ALPHA / RANK
        B, T, H = x.shape
        E = gate_w.shape[0]
        x_flat = x.reshape(-1, H)
        logits = x_flat @ gate_w.T + expert_bias
        top1 = jnp.argmax(logits, axis=-1)
        one_hot = jax.nn.one_hot(top1, E, dtype=x_flat.dtype)
        base_out = jnp.einsum('bth,oh->bto', x, W_up)
        z = jnp.einsum('nh,erh->ner', x_flat, lora_A)
        d = jnp.einsum('ner,ehr->neh', z, lora_B) * SCALE
        delta = jnp.einsum('neh,ne->nh', d, one_hot)
        return base_out + delta.reshape(B, T, H)

    def _L1_attn_ref(minibatch, eta):
        import jax, jax.numpy as jnp
        import numpy as np
        B, C, L = (32, 64, 512)
        logits = jnp.einsum('bcl,bdl->bcd', minibatch, minibatch)
        logits_new = jnp.max(logits, axis=-1, keepdims=True) - logits
        probs = jax.nn.softmax(logits_new, axis=-1)
        read = jnp.einsum('bcd,bdl->bcl', probs, minibatch)
        return eta * read + minibatch

    def _L1_xattn_ref(latents, context, Wq, Wk, Wv, Wo):
        import jax, jax.numpy as jnp
        import numpy as np
        import math
        HIDDEN = 512
        N_HEADS = 32
        HEAD_DIM = 128
        N_KV_HEADS = 4
        N_GROUPS = N_HEADS // N_KV_HEADS
        b, q_len, _ = latents.shape
        kv_len = q_len + context.shape[1]
        hidden_states = jnp.concatenate([context, latents], axis=1)
        q = (latents @ Wq).reshape(b, q_len, N_KV_HEADS, N_GROUPS, HEAD_DIM)
        k = (hidden_states @ Wk).reshape(b, kv_len, N_KV_HEADS, HEAD_DIM)
        v = (hidden_states @ Wv).reshape(b, kv_len, N_KV_HEADS, HEAD_DIM)
        scale = 1.0 / math.sqrt(HEAD_DIM)
        scores = jnp.einsum('bqhgd,bkhd->bhgqk', q, k) * scale
        attn = jax.nn.softmax(scores.astype(jnp.float32), axis=-1).astype(q.dtype)
        out = jnp.einsum('bhgqk,bkhd->bqhgd', attn, v)
        out = out.reshape(b, q_len, N_HEADS * HEAD_DIM)
        return out @ Wo

    def _L1_ffn_ref(x, W_base, b_base, W_router, A, B):
        import jax, jax.numpy as jnp
        import numpy as np
        NUM_EXPERTS = 8
        TOP_K = 2
        RANK = 16
        LORA_ALPHA = 32
        SCALING = LORA_ALPHA / RANK
        bs, seq, d_in = x.shape
        T = bs * seq
        xf = x.reshape(T, d_in)
        base = xf @ W_base.T + b_base
        logits = xf @ W_router.T
        rw, sel = jax.lax.top_k(logits, TOP_K)
        rw = jax.nn.softmax(rw, axis=-1)
        onehot = jax.nn.one_hot(sel, NUM_EXPERTS, dtype=rw.dtype)
        w = jnp.einsum('tk,tke->te', rw, onehot)
        h = jnp.einsum('td,erd->ter', xf, A)
        lora = jnp.einsum('ter,te,eor->to', h, w, B) * SCALING
        return (base + lora).reshape(bs, seq, -1)

    def _L2_attn_ref(x, wq, bq, wk, bk, wv, bv):
        import jax, jax.numpy as jnp
        import numpy as np
        EMBED = 512
        H = 32
        KV = 8
        D = EMBED // H
        REP = H // KV

        def _rope(t, cos, sin):
            t = t.reshape(*t.shape[:-1], 2, D // 2)
            t1, t2 = (t[..., 0, :], t[..., 1, :])
            return jnp.concatenate([t1 * cos - t2 * sin, t1 * sin + t2 * cos], axis=-1)
        B, S, E = x.shape
        xq = (x @ wq + bq).reshape(B, S, H, D)
        xk = (x @ wk + bk).reshape(B, S, KV, D)
        xv = (x @ wv + bv).reshape(B, S, KV, D)
        inv_freq = 1.0 / 10000.0 ** (jnp.arange(0, D, 2, dtype=jnp.float32) / D)
        ang = jnp.arange(S, dtype=jnp.float32)[:, None] * inv_freq[None, :]
        cos, sin = (jnp.cos(ang)[:, None, :], jnp.sin(ang)[:, None, :])
        q = _rope(xq, cos, sin)
        k = _rope(xk, cos, sin)
        k = jnp.repeat(k, REP, axis=2)
        v = jnp.repeat(xv, REP, axis=2)
        scores = jnp.einsum('bqhd,bkhd->bhqk', q, k) / jnp.sqrt(jnp.float32(D))
        probs = jax.nn.softmax(scores.astype(jnp.float32), axis=-1)
        out = jnp.einsum('bhqk,bkhd->bqhd', probs, v).reshape(B, S, E)
        return out

    def _L2_xattn_ref(hidden_states, cross_attention_states, attention_mask, q_proj_w, k_proj_w, v_proj_w, o_proj_w, q_norm_w, k_norm_w):
        import jax, jax.numpy as jnp
        import numpy as np
        NUM_HEADS = 32
        NUM_KV_HEADS = 8
        HEAD_DIM = 128
        HIDDEN = 512
        EPS = 1e-05

        def rmsnorm(x, w, eps=EPS):
            xf = x.astype(jnp.float32)
            var = jnp.mean(xf * xf, axis=-1, keepdims=True)
            return w * (xf * jax.lax.rsqrt(var + eps)).astype(x.dtype)
        B, Q, _ = hidden_states.shape
        KV = cross_attention_states.shape[1]
        n_rep = NUM_HEADS // NUM_KV_HEADS
        q = (hidden_states @ q_proj_w.T).reshape(B, Q, NUM_HEADS, HEAD_DIM).transpose(0, 2, 1, 3)
        k = (cross_attention_states @ k_proj_w.T).reshape(B, KV, NUM_KV_HEADS, HEAD_DIM).transpose(0, 2, 1, 3)
        v = (cross_attention_states @ v_proj_w.T).reshape(B, KV, NUM_KV_HEADS, HEAD_DIM).transpose(0, 2, 1, 3)
        q = rmsnorm(q, q_norm_w)
        k = jnp.repeat(k, n_rep, axis=1)
        v = jnp.repeat(v, n_rep, axis=1)
        k = rmsnorm(k, k_norm_w)
        scale = 1.0 / np.sqrt(HEAD_DIM)
        scores = jnp.einsum('bhqd,bhkd->bhqk', q, k) * scale + attention_mask
        attn = jax.nn.softmax(scores.astype(jnp.float32), axis=-1).astype(q.dtype)
        out = jnp.einsum('bhqk,bhkd->bhqd', attn, v)
        out = out.transpose(0, 2, 1, 3).reshape(B, Q, NUM_HEADS * HEAD_DIM)
        return out @ o_proj_w.T

    def _L2_ffn_ref(hidden_states, Wq, Wr, aux_keys, aux_values, Wvd, Wvu, Wu1, bu1, Wu2, bu2, gate_w1, gate_bias, log_rel):
        import jax, jax.numpy as jnp
        import numpy as np
        HID, BOT, RDIM, NSLOT, K, VB = (512, 64, 48, 128, 8, 32)
        TAU_LOW, TAU_HIGH, EARLY_EXIT = (0.5, 2.0, 0.05)

        def _uncertainty(h, Wu1, bu1, Wu2, bu2):
            var = jnp.var(h, axis=-1)
            log_var = jnp.log1p(var)
            norm_var = log_var / (jnp.mean(log_var) + 1e-06)
            learned = (jax.nn.gelu(h @ Wu1.T + bu1) @ Wu2.T + bu2)[..., 0]
            return jnp.clip(norm_var * 0.5 + jax.nn.sigmoid(learned) * 2.5, 0.0, 5.0)
        query = hidden_states @ Wq.T
        rq = query @ Wr.T
        rk = aux_keys @ Wr.T
        router_scores = jnp.einsum('bsr,nr->bsn', rq, rk) / np.sqrt(RDIM) + log_rel
        top_scores, top_idx = jax.lax.top_k(router_scores, K)
        sel_keys = aux_keys[top_idx]
        attn = jnp.einsum('bsd,bskd->bsk', query, sel_keys) / np.sqrt(BOT) + log_rel[top_idx]
        w = jax.nn.softmax(attn, axis=-1)
        sel_vals = aux_values[top_idx]
        aux_out = jnp.einsum('bsk,bskh->bsh', w, sel_vals)
        aux_out = aux_out @ Wvd.T @ Wvu.T
        u = _uncertainty(hidden_states, Wu1, bu1, Wu2, bu2)
        u_norm = jnp.clip((u - TAU_LOW) / (TAU_HIGH - TAU_LOW), 0.0, 1.0)
        gate = jax.nn.sigmoid(gate_w1 * u_norm + gate_bias)
        gate = jnp.where(gate < EARLY_EXIT, 0.0, gate)
        return hidden_states + gate[..., None] * aux_out

    def _L3_attn_ref(hidden_states, Wqkv, Wo):
        import math
        import jax, jax.numpy as jnp
        import numpy as np
        NUM_HEADS = 32
        HIDDEN = 512
        HEAD_DIM = HIDDEN // NUM_HEADS
        NEG_INF = -1e+30

        def _alibi_slopes(n: int) -> jnp.ndarray:
            cp2 = 2 ** math.floor(math.log2(n))
            base = 2.0 ** (-2.0 ** (-(math.log2(cp2) - 3)))
            slopes = base ** np.arange(1, cp2 + 1, dtype=np.float64)
            if cp2 != n:
                extra_base = 2.0 ** (-2.0 ** (-(math.log2(2 * cp2) - 3)))
                rem = min(cp2, n - cp2)
                extra = extra_base ** np.arange(1, 1 + 2 * rem, 2, dtype=np.float64)
                slopes = np.concatenate([slopes, extra])
            return jnp.asarray(slopes, dtype=jnp.float32)
        B, S, H = hidden_states.shape
        nH, d = (NUM_HEADS, HEAD_DIM)
        scale = d ** (-0.5)
        qkv = hidden_states @ Wqkv
        q = qkv[..., :nH * d].reshape(B, S, nH, d)
        k = qkv[..., nH * d:nH * d + d]
        v = qkv[..., nH * d + d:]
        scores = jnp.einsum('bqhd,bkd->bhqk', q, k) * scale
        pos_q = jnp.arange(S)[:, None]
        pos_k = jnp.arange(S)[None, :]
        slopes = _alibi_slopes(nH)
        alibi = slopes[:, None, None] * (pos_k - pos_q).astype(jnp.float32)
        causal = pos_k <= pos_q
        scores = jnp.where(causal[None, None], scores + alibi[None], NEG_INF)
        probs = jax.nn.softmax(scores, axis=-1)
        attn = jnp.einsum('bhqk,bkd->bqhd', probs, v).reshape(B, S, H)
        return attn @ Wo

    def _L3_xattn_ref(hidden_q, hidden_kv, attention_mask, position_bias, Wq, Wk, Wv, Wo):
        import jax, jax.numpy as jnp
        import numpy as np
        B, S, D, H, DH = (2, 128, 512, 32, 128)
        b, lq, _ = hidden_q.shape
        lk = hidden_kv.shape[1]
        h, dh = (H, DH)
        q = (hidden_q @ Wq).reshape(b, lq, h, dh)
        k = (hidden_kv @ Wk).reshape(b, lk, h, dh)
        v = (hidden_kv @ Wv).reshape(b, lk, h, dh)
        scale = 1.0 / jnp.sqrt(jnp.asarray(dh, dtype=q.dtype))
        score = jnp.einsum('bqhd,bkhd->bhqk', q, k) * scale + position_bias
        mask = attention_mask[:, None, :, :]
        neg_inf = jnp.asarray(-jnp.inf, dtype=score.dtype)
        score = jnp.where(mask, score, neg_inf)
        probs = jax.nn.softmax(score, axis=-1)
        probs = jnp.where(mask, probs, jnp.asarray(0, dtype=probs.dtype))
        ctx = jnp.einsum('bhqk,bkhd->bqhd', probs, v).reshape(b, lq, h * dh)
        return ctx @ Wo

    def _L3_ffn_ref(x, W_org, lora_down, lora_up, lora_keys, Wq):
        import jax, jax.numpy as jnp
        import numpy as np
        import math
        B, S, IN, OUT = (4, 256, 512, 512)
        E, R, K = (8, 64, 128)
        SCALE = 64.0 / 64.0
        MULTIPLIER = 1.0
        base = jnp.einsum('bsi,oi->bso', x, W_org)
        q = jnp.einsum('bi,ki->bk', x.mean(axis=1), Wq)
        scores = jnp.einsum('bk,ek->be', q, lora_keys) / math.sqrt(K)
        coeffs = jax.nn.softmax(scores, axis=-1)
        h = jnp.einsum('bsi,eir->bser', x, lora_down)
        delta = jnp.einsum('be,bser,ero->bso', coeffs, h, lora_up)
        return base + delta * (SCALE * MULTIPLIER)
    x = _layernorm(x + _L0_attn_ref(x, L0_attn_w_qkv, L0_attn_w_o), axis=-1)
    x = _layernorm(x + _L0_xattn_ref(x, ctx_4096, ctx_4096, L0_xattn_Wq, L0_xattn_Wk, L0_xattn_Wv, L0_xattn_Wo), axis=-1)
    x = _layernorm(x + _L0_ffn_ref(x, L0_ffn_W_up, L0_ffn_gate_w, L0_ffn_expert_bias, L0_ffn_lora_A, L0_ffn_lora_B), axis=-1)
    x = _layernorm(x + _L1_attn_ref(x, L1_attn_eta), axis=-1)
    x = _layernorm(x + _L1_xattn_ref(x, ctx_4096, L1_xattn_Wq, L1_xattn_Wk, L1_xattn_Wv, L1_xattn_Wo), axis=-1)
    x = _layernorm(x + _L1_ffn_ref(x, L1_ffn_W_base, L1_ffn_b_base, L1_ffn_W_router, L1_ffn_A, L1_ffn_B), axis=-1)
    x = _layernorm(x + _L2_attn_ref(x, L2_attn_wq, L2_attn_bq, L2_attn_wk, L2_attn_bk, L2_attn_wv, L2_attn_bv), axis=-1)
    x = _layernorm(x + _L2_xattn_ref(x, ctx_4096, mask_1x1xSxS2_ff0, L2_xattn_q_proj_w, L2_xattn_k_proj_w, L2_xattn_v_proj_w, L2_xattn_o_proj_w, L2_xattn_q_norm_w, L2_xattn_k_norm_w), axis=-1)
    x = _layernorm(x + _L2_ffn_ref(x, L2_ffn_Wq, L2_ffn_Wr, L2_ffn_aux_keys, L2_ffn_aux_values, L2_ffn_Wvd, L2_ffn_Wvu, L2_ffn_Wu1, L2_ffn_bu1, L2_ffn_Wu2, L2_ffn_bu2, L2_ffn_gate_w1, L2_ffn_gate_bias, L2_ffn_log_rel), axis=-1)
    x = _layernorm(x + _L3_attn_ref(x, L3_attn_Wqkv, L3_attn_Wo), axis=-1)
    x = _layernorm(x + _L3_xattn_ref(x, ctx_4096, mask_BxSxS2_bk0, fside_Bx32xSxS2_0, L3_xattn_Wq, L3_xattn_Wk, L3_xattn_Wv, L3_xattn_Wo), axis=-1)
    x = _layernorm(x + _L3_ffn_ref(x, L3_ffn_W_org, L3_ffn_lora_down, L3_ffn_lora_up, L3_ffn_lora_keys, L3_ffn_Wq), axis=-1)
    return x

_drawn_inputs = setup_inputs


def setup_inputs(seed=0):
    import zlib

    import numpy as np

    out = dict(_drawn_inputs(seed))
    spreads = {'L0_ffn_expert_bias': (0.0, 0.8),
     'L2_xattn_q_norm_w': (1.0, 0.2),
     'L2_xattn_k_norm_w': (1.0, 0.2),
     'L2_ffn_bu1': (0.0, 2.0),
     'L2_ffn_log_rel': (0.0, 2.0)}
    factors = {'fside_Bx32xSxS2_0': 8.0,
     'L0_ffn_gate_w': 7.248,
     'L0_ffn_lora_A': 6.246,
     'L0_ffn_lora_B': 6.083,
     'L1_ffn_b_base': 5.646,
     'L1_ffn_W_router': 2.712,
     'L2_attn_wq': 8.0,
     'L2_attn_bq': 25.129,
     'L2_attn_wk': 8.0,
     'L2_attn_bk': 31.394,
     'L2_attn_bv': 4.799,
     'L2_ffn_Wq': 63.946,
     'L2_ffn_Wr': 64.0,
     'L2_ffn_aux_keys': 64.0,
     'L2_ffn_aux_values': 62.23,
     'L2_ffn_Wvd': 58.075,
     'L2_ffn_Wvu': 61.106,
     'L2_ffn_Wu1': 64.0,
     'L2_ffn_Wu2': 64.0,
     'L3_ffn_lora_keys': 6.893,
     'L3_ffn_Wq': 6.879}
    for name, (base, spread) in spreads.items():
        noise = np.random.default_rng([zlib.crc32(name.encode()), seed]).standard_normal(out[name].shape)
        drawn = base * np.exp(spread * noise) if base else spread * noise
        out[name] = jnp.asarray(drawn.astype(out[name].dtype))
    for name, factor in factors.items():
        out[name] = (out[name] * factor).astype(out[name].dtype)
    return out
```

```python
from contextlib import ExitStack
import math

import numpy as np

import concourse.bass as bass
from concourse import mybir

F32 = mybir.dt.float32
U8 = mybir.dt.uint8
ALU = mybir.AluOpType
ACT = mybir.ActivationFunctionType
AX = mybir.AxisListType

P = 128
BATCH, SEQ, DIM = 16, 64, 512
TOKENS = BATCH * SEQ
CH = DIM // P
TILES = TOKENS // P
HEADS = 32
HD = 128
ND = DIM // HEADS
GH = 4
GROUPS = HEADS // GH
UB = 4
UNITS = BATCH // UB
BODY = 2 * UNITS
UT = UB * SEQ
KV = 8
NR = HEADS // KV
NEG = -1.0e30
LN_EPS = 1e-5
CTX, SELF = 0, 1
CREDIT = 8


class Record:
    pass


class Signal:

    def __init__(self, sem, begin):
        self.sem, self.begin = sem, begin

    def at(self, n):
        return self.begin + n


class Signals:

    def __init__(self, nc, ctx):
        self.all, self.credited = [], []

        def plain(name):
            self.all.append(ctx.enter_context(nc.semaphore(name)))
            return Signal(self.all[-1], 0)

        def released(name):
            sig = plain(name)
            self.credited.append(sig.sem)
            return Signal(sig.sem, CREDIT)

        self.q_done = released("q_done")
        self.k_done = released("k_done")
        self.v_done = released("v_done")
        self.s_read = released("s_read")
        self.shifted = released("shifted")
        self.pt_done = released("pt_done")
        self.o_done = released("o_done")
        self.added = released("added")
        self.staged = released("staged")
        self.kd_done = released("kd_done")
        self.keys_taken = released("keys_taken")
        self.squared = released("squared")
        self.attn_taken = released("attn_taken")
        self.wide_a = plain("wide_a")
        self.wide_b = plain("wide_b")
        self.kv_in = plain("kv_in")
        self.small_in = plain("small_in")
        self.q_ready = plain("q_ready")
        self.k_ready = plain("k_ready")
        self.v_ready = plain("v_ready")
        self.s_ready = plain("s_ready")
        self.exp_done = plain("exp_done")
        self.p_ready = plain("p_ready")
        self.pt_ready = plain("pt_ready")
        self.o_ready = plain("o_ready")
        self.y_ready = plain("y_ready")
        self.dve_step = plain("dve_step")
        self.act_step = plain("act_step")
        self.pool_step = plain("pool_step")
        self.rms_done = plain("rms_done")
        self.rms_sum = plain("rms_sum")
        self.rms_var = plain("rms_var")
        self.rms_power = plain("rms_power")
        self.norm_step = plain("norm_step")
        self.var_ready = plain("var_ready")
        self.rstd_ready = plain("rstd_ready")
        self.normed = plain("normed")
        self.turned = plain("turned")
        self.turn_read = plain("turn_read")
        self.keys_turned = plain("keys_turned")
        self.rotated = plain("rotated")
        self.attn_turned = plain("attn_turned")
        self.prepared = plain("prepared")
        self.logits_ready = plain("logits_ready")
        self.z_ready = plain("z_ready")
        self.z_weighted = plain("z_weighted")
        self.z_turning = plain("z_turning")
        self.z_turned = plain("z_turned")
        self.zeroed = plain("zeroed")
        self.least = plain("least")
        self.y_squared = plain("y_squared")
        self.inner_done = plain("inner_done")
        self.tanh_done = plain("tanh_done")
        self.gelu_done = plain("gelu_done")
        self.x_read = plain("x_read")
        self.log_done = plain("log_done")
        self.log_summed = plain("log_summed")
        self.rq_ready = plain("rq_ready")
        self.rq_done = plain("rq_done")
        self.hidden_ready = plain("hidden_ready")
        self.learned_ready = plain("learned_ready")
        self.logistic_in = plain("logistic_in")
        self.logistic = plain("logistic")
        self.h_ready = plain("h_ready")
        self.h_done = plain("h_done")
        self.sums_done = plain("sums_done")
        self.coef_done = plain("coef_done")
        self.rows_ready = plain("rows_ready")


class Steps:

    def __init__(self, signal, before=0):
        self.of, self.before, self.n = signal, before, 0

    def count(self):
        self.n += 1
        return self.of.sem

    def so_far(self):
        return self.of.at(self.before + self.n)


def over(ap, *dims):
    for axis, size in dims:
        ap = ap.unsqueeze(axis)
        shape = list(ap.shape)
        shape[axis] = size
        ap = ap.to_broadcast(shape)
    return ap


def clear_signals(nc, g):
    with nc.Block() as block:
        @block.sync
        def _(sp):
            numbers = sorted(sem.num for sem in g.sig.all)
            sp.sem_clear(range(numbers[0], numbers[-1] + 1))
            for sem in g.sig.credited:
                sp.sem_inc(sem, CREDIT)



def norm_buffers(nc, ctx):
    norm = Record()
    norm.stats = ctx.enter_context(nc.sbuf_tensor("ln_stats", [P, TILES, 6], F32))
    norm.mv = ctx.enter_context(nc.sbuf_tensor("ln_mean_var", [P, TILES, 2], F32))
    norm.var = ctx.enter_context(nc.sbuf_tensor("ln_var", [P, TILES], F32))
    norm.rstd = ctx.enter_context(nc.sbuf_tensor("ln_rstd", [P, TILES], F32))
    return norm


def norm_vector(nc, dve, g):
    n, steps = g.norm, Steps(g.sig.norm_step)
    for t in range(TILES):
        nc.vector.bn_stats(n.stats[:, t, :], g.x[:, t, :]).then_inc(steps.count(), 1)
    dve.wait_ge(g.sig.norm_step.sem, steps.so_far())
    for t in range(TILES):
        nc.vector.bn_aggr(n.mv[:, t, :], n.stats[:, t, :]).then_inc(steps.count(), 1)
    dve.wait_ge(g.sig.norm_step.sem, steps.so_far())
    nc.vector.tensor_scalar(n.var[:], n.mv[:, :, 1], LN_EPS, None, ALU.add).then_inc(g.sig.var_ready.sem, 1)
    dve.wait_ge(g.sig.rstd_ready.sem, g.sig.rstd_ready.at(1))
    for t in range(TILES):
        nc.vector.tensor_scalar(g.x[:, t, :], g.x[:, t, :], n.mv[:, t, 0:1], n.rstd[:, t:t + 1],
                                ALU.subtract, ALU.mult).then_inc(g.sig.normed.sem, 1)


def norm_pool(nc, pool, g):
    pool.wait_ge(g.sig.var_ready.sem, g.sig.var_ready.at(1))
    nc.gpsimd.tensor_tensor(g.norm.rstd[:], g.norm.var[:], g.minus_half[:, 0:TILES], ALU.pow).then_inc(
        g.sig.rstd_ready.sem, 1)


def norm_tensor(nc, pe, g):
    for t in range(TILES):
        pe.wait_ge(g.sig.normed.sem, g.sig.normed.at(t + 1))
        if t >= 2:
            pe.wait_ge(g.sig.turn_read.sem, g.sig.turn_read.at(t - 1))
        bank = g.bank[t % 2]
        for c in range(CH):
            last = nc.tensor.transpose(bank[:, c * P:(c + 1) * P], g.x[:, t, c * P:(c + 1) * P], g.ident[:])
        last.then_inc(g.sig.turned.sem, 1)


def norm_scalar(nc, act, g):
    for t in range(TILES):
        act.wait_ge(g.sig.turned.sem, g.sig.turned.at(t + 1))
        src = g.bank[t % 2][:, :].rearrange("p (c b s) -> p c b s", c=CH, b=2)
        nc.scalar.copy(g.feat[:, SELF, :, 2 * t:2 * t + 2, :], src).then_inc(g.sig.turn_read.sem, 1)


def norm_sync(nc, sp, g):
    for t in range(TILES):
        sp.wait_ge(g.sig.normed.sem, g.sig.normed.at(t + 1))
        sp.dma_start(g.out[t * P:(t + 1) * P, :], g.x[:, t, :]).then_inc(g.out_written.sem, 16)
    sp.wait_ge(g.out_written.sem, 16 * TILES)



def wide_attention(nc, g, name, last, w_qo, w_kv, kv_heads, keys, scale, bias=None, mask=None,
                   q_norm=None, k_norm=None, key_mask=None):
    sig, feat, x, bank = g.sig, g.feat, g.x, g.bank
    both, rms = keys == "both", q_norm is not None
    klen = 2 * SEQ if both else SEQ
    halves = 2 if both else 1
    kbanks = 2 if kv_heads == GH else 1
    kdim = kv_heads * HD
    rounds = GROUPS // 2
    wq_cols = CH * GH * HD
    with ExitStack() as ctx:
        def sb(what, shape, dt=F32):
            return ctx.enter_context(nc.sbuf_tensor(f"{name}_{what}", shape, dt))
        wqo = sb("wqo", [P, 2, wq_cols + GH * DIM])
        wkv = sb("wkv", [P, 1 if both else 2, CH * kdim * 2])
        q_t = sb("q_t", [P, GH, UT])
        if both:
            joint = sb("joint", [P, CH, BATCH, 2, SEQ])
            k_t = sb("k_t", [P, UNITS, UB * klen])
            v = sb("v", [P, UNITS, UB, HD])
        else:
            k_t = sb("k_t", [P, kv_heads, UT])
            v = sb("v", [P, 2, 2, kdim])
        shifted = sb("shifted", [P, halves, 512])
        probs = sb("probs", [P, halves, 512])
        p_t = sb("p_t", [P, halves, 512])
        o_t = sb("o_t", [P, GH, UB, SEQ])
        ngr = 512 // klen
        mx = sb("mx", [P, halves, ngr])
        total = sb("total", [P, halves, ngr])
        recip = sb("recip", [P, halves, ngr])
        if bias is not None:
            bias_cols = bias.shape[2]
            bias_sb = sb("bias", [P, 2, bias_cols])
        if mask is not None:
            mask_sb = sb("mask", [P, SEQ])
        if key_mask is not None:
            km_u8 = sb("km_u8", [P, BATCH, SEQ], U8)
            km_one = sb("km_one", [P, BATCH, SEQ])
            km_neg = sb("km_neg", [P, BATCH, SEQ])
        if rms:
            q_sq = sb("q_sq", [P, UB, GH, SEQ])
            q_w = sb("q_w", [P, 1])
            k_w = sb("k_w", [P, 1])
            mean_col = sb("mean_col", [P, 1])
            k_rows = sb("k_rows", [P, 2, HD])
            k_junk = sb("k_junk", [P, HD])
            ssq = sb("ssq", [P, 2])
            k_var = sb("k_var", [P, 2])
            k_rstd = sb("k_rstd", [P, 2])
            q_var = sb("q_var", [P, 8])
            q_rstd = sb("q_rstd", [P, 8])

        def landed(n):
            return sig.wide_a if n % 2 == 0 else sig.wide_b
        small_loads = 16 * (2 * (mask is not None) + (key_mask is not None) + 2 * rms)
        score_bank_free = sig.s_read if (bias is not None or rms) else sig.shifted
        before_exp = 2 if (key_mask is not None or rms) else 1
        after_exp = 3 if key_mask is not None else 2
        score_banks = (bank[4], bank[3])
        value_bank = bank[2] if both else bank[3]
        per_group = 16 * (1 + (not both) + (bias is not None))

        def k_round(i, n):
            return UNITS * i + n if both else BODY * i + n

        with nc.Block() as block:
            @block.sync
            def _(sp):
                if mask is not None:
                    sp.dma_start(mask_sb[0:SEQ, :], mask).then_inc(sig.small_in.sem, 16)
                    sp.dma_start(mask_sb[SEQ:P, :], mask).then_inc(sig.small_in.sem, 16)
                if key_mask is not None:
                    sp.dma_start(km_u8[:], key_mask).then_inc(sig.small_in.sem, 16)
                if rms:
                    sp.dma_start(q_w[:], q_norm).then_inc(sig.small_in.sem, 16)
                    sp.dma_start(k_w[:], k_norm).then_inc(sig.small_in.sem, 16)

                def load(n, group):
                    if not both:
                        sp.dma_start(wkv[:, n % 2, :], w_kv[group]).then_inc(landed(n).sem, 16)
                    if bias is not None:
                        sp.dma_start(bias_sb[:, n % 2, :], bias[group]).then_inc(landed(n).sem, 16)
                    sp.dma_start(wqo[:, n % 2, :], w_qo[group]).then_inc(landed(n).sem, 16)
                if both:
                    sp.dma_start(wkv[:, 0, :], w_kv[0]).then_inc(sig.kv_in.sem, 16)
                for n in range(2):
                    load(n, n)
                with sp.Fori(0, rounds - 1) as i:
                    if both:
                        sp.wait_ge(sig.k_done.sem, sig.k_done.at(UNITS * i + UNITS))
                        sp.wait_ge(sig.v_done.sem, sig.v_done.at(UNITS * i + UNITS))
                        sp.dma_start(wkv[:, 0, :], w_kv[i + 1]).then_inc(sig.kv_in.sem, 16)
                    for n in range(2):
                        sp.wait_ge(sig.y_ready.sem, sig.y_ready.at(2 * (BODY * i + UNITS * (n + 1))))
                        load(n, 2 * i + 2 + n)
                if last:
                    norm_sync(nc, sp, g)

            @block.gpsimd
            def _(pool):
                if rms:
                    def unit(i, n):
                        uu = BODY * i + n
                        pool.wait_ge(sig.rms_var.sem, sig.rms_var.at(2 * uu + 1))
                        nc.gpsimd.tensor_tensor(k_rstd[:], k_var[:], g.minus_half[:, 0:2], ALU.pow).then_inc(
                            sig.rms_power.sem, 1)
                        pool.wait_ge(sig.rms_var.sem, sig.rms_var.at(2 * uu + 2))
                        nc.gpsimd.tensor_tensor(q_rstd[:], q_var[:], g.minus_half[:, 0:8], ALU.pow).then_inc(
                            sig.rms_power.sem, 1)
                    with pool.Fori(0, rounds) as i:
                        for n in range(BODY):
                            unit(i, n)
                norm_pool(nc, pool, g)

            @block.tensor
            def _(pe):
                def project_q(i, n):
                    uu, slot, u = BODY * i + n, n // UNITS, n % UNITS
                    if u == 0:
                        pe.wait_ge(landed(slot).sem, landed(slot).at(per_group * (i + 1)))
                    for j in range(2):
                        pe.wait_ge(sig.q_done.sem, sig.q_done.at(2 * uu - 1 + j))
                        for hh in range(2):
                            h = 2 * j + hh
                            for c in range(CH):
                                mm = nc.tensor.matmul(
                                    bank[j][:, hh * UT:(hh + 1) * UT].rearrange("p (b s) -> p b s", b=UB),
                                    wqo[:, slot, c * GH * HD + h * HD:c * GH * HD + (h + 1) * HD],
                                    feat[:, SELF, c, UB * u:UB * u + UB, :], start=(c == 0), stop=(c == CH - 1))
                        mm.then_inc(sig.q_ready.sem, 1)

                def project_k(i, n):
                    slot, u = (0 if both else n // UNITS), n % UNITS
                    kr = k_round(i, n)
                    if both and n == 0:
                        pe.wait_ge(sig.kv_in.sem, sig.kv_in.at(16 * (i + 1)))
                    if rms:
                        pe.wait_ge(sig.keys_taken.sem, sig.keys_taken.at(kr))
                    else:
                        pe.wait_ge(sig.k_done.sem, sig.k_done.at(kbanks * kr))
                    if both or kbanks == 2:
                        pe.wait_ge(sig.v_done.sem, sig.v_done.at(kbanks * kr))
                    if rms:
                        for tt in range(2):
                            for c in range(CH):
                                mm = nc.tensor.matmul(
                                    bank[2][:, tt * HD:(tt + 1) * HD],
                                    feat[:, keys, c, UB * u + 2 * tt:UB * u + 2 * tt + 2, :],
                                    wkv[:, slot, c * HD:(c + 1) * HD], start=(c == 0), stop=(c == CH - 1))
                        mm.then_inc(sig.k_ready.sem, 1)
                        return
                    for h in range(kv_heads):
                        for c in range(CH):
                            w = wkv[:, slot, c * kdim + h * HD:c * kdim + (h + 1) * HD]
                            if both:
                                mm = nc.tensor.matmul(bank[2][:, :], w,
                                                      joint[:, c, UB * u:UB * u + UB, :, :].rearrange(
                                                          "p b k s -> p (b k s)"),
                                                      start=(c == 0), stop=(c == CH - 1))
                            else:
                                out = bank[2 + h // 2][:, (h % 2) * UT:(h % 2 + 1) * UT]
                                mm = nc.tensor.matmul(out.rearrange("p (b s) -> p b s", b=UB), w,
                                                      feat[:, keys, c, UB * u:UB * u + UB, :],
                                                      start=(c == 0), stop=(c == CH - 1))
                        if h % 2 == 1 or kv_heads == 1:
                            mm.then_inc(sig.k_ready.sem, 1)

                def project_v(i, n):
                    slot, u = (0 if both else n // UNITS), n % UNITS
                    kr = k_round(i, n)
                    off = CH * kdim
                    if both or kbanks == 2:
                        pe.wait_ge(sig.k_done.sem, sig.k_done.at(kbanks * (kr + 1)))
                    else:
                        pe.wait_ge(sig.v_done.sem, sig.v_done.at(kr))
                    if both:
                        for b in range(UB):
                            for c in range(CH):
                                mm = nc.tensor.matmul(
                                    value_bank[:, b * HD:(b + 1) * HD],
                                    joint[:, c, UB * u + b, :, :].rearrange("p k s -> p (k s)"),
                                    wkv[:, slot, off + c * HD:off + (c + 1) * HD],
                                    start=(c == 0), stop=(c == CH - 1))
                        mm.then_inc(sig.v_ready.sem, 1)
                        return
                    for tt in range(2):
                        for c in range(CH):
                            out = bank[2 + tt][:, :] if kbanks == 2 else bank[3][:, tt * HD:(tt + 1) * HD]
                            mm = nc.tensor.matmul(
                                out, feat[:, keys, c, UB * u + 2 * tt:UB * u + 2 * tt + 2, :],
                                wkv[:, slot, off + c * kdim:off + (c + 1) * kdim],
                                start=(c == 0), stop=(c == CH - 1))
                        if kbanks == 2 or tt == 1:
                            mm.then_inc(sig.v_ready.sem, 1)

                def turn_keys(i, n):
                    uu = BODY * i + n
                    pe.wait_ge(sig.rms_done.sem, sig.rms_done.at(uu + 1))
                    for tt in range(2):
                        mm = nc.tensor.transpose(bank[2][:, tt * P:(tt + 1) * P], k_rows[:, tt, :], g.ident[:])
                    mm.then_inc(sig.keys_turned.sem, 1)

                def query_squares(i, n):
                    uu = BODY * i + n
                    pe.wait_ge(sig.squared.sem, sig.squared.at(2 * uu + 2))
                    for b in range(UB):
                        for j in range(2):
                            col = (b // 2) * 4 + j * 2 + b % 2
                            mm = nc.tensor.matmul(bank[5][:, col:col + 1],
                                                  q_sq[:, b, 2 * j:2 * j + 2, :].rearrange("p h s -> p (h s)"),
                                                  mean_col[:], start=True, stop=True)
                    mm.then_inc(sig.rms_sum.sem, 1)

                def scores(i, n):
                    uu, u = BODY * i + n, n % UNITS
                    pe.wait_ge(sig.q_done.sem, sig.q_done.at(2 * uu + 2))
                    if rms:
                        pe.wait_ge(sig.keys_taken.sem, sig.keys_taken.at(uu + 1))
                    elif n < UNITS or not both:
                        pe.wait_ge(sig.k_done.sem, sig.k_done.at(kbanks * (k_round(i, n) + 1)))
                    pe.wait_ge(score_bank_free.sem, score_bank_free.at(halves * uu))
                    for b in range(UB):
                        for h in range(GH):
                            j, h2 = h // 2, h % 2
                            if both:
                                dst = score_banks[b // 2][h2 * SEQ:(h2 + 1) * SEQ,
                                                            ((b % 2) * 2 + j) * klen:((b % 2) * 2 + j + 1) * klen]
                                key = k_t[:, u, b * klen:(b + 1) * klen]
                            else:
                                col = ((b // 2) * 4 + j * 2 + b % 2) * SEQ
                                dst = score_banks[0][h2 * SEQ:(h2 + 1) * SEQ, col:col + SEQ]
                                key = k_t[:, h if kv_heads == GH else 0, b * SEQ:(b + 1) * SEQ]
                            mm = nc.tensor.matmul(dst, q_t[:, h, b * SEQ:(b + 1) * SEQ], key,
                                                  start=True, stop=True)
                        if both and b % 2 == 1 or b == UB - 1 and not both:
                            mm.then_inc(sig.s_ready.sem, 1)

                def turn_probs(i, n):
                    uu = BODY * i + n
                    for half in range(halves):
                        pe.wait_ge(sig.p_ready.sem, sig.p_ready.at(halves * uu + half + 1))
                        pe.wait_ge(sig.pt_done.sem, sig.pt_done.at(halves * uu + half))
                        for blk in range(4):
                            mm = nc.tensor.transpose(bank[5][:, blk * P:(blk + 1) * P],
                                                     probs[:, half, blk * P:(blk + 1) * P], g.ident[:])
                        mm.then_inc(sig.pt_ready.sem, 1)

                def weighted_values(i, n):
                    uu, u, par = BODY * i + n, n % UNITS, n % 2
                    pe.wait_ge(sig.pt_done.sem, sig.pt_done.at(halves * (uu + 1)))
                    if n < UNITS or not both:
                        pe.wait_ge(sig.v_done.sem, sig.v_done.at(kbanks * (k_round(i, n) + 1)))
                    pe.wait_ge(sig.added.sem, sig.added.at(2 * uu))
                    for b2 in range(2):
                        for bp in range(2):
                            out = bank[6 + b2]
                            if both:
                                mm = nc.tensor.matmul(out[:, bp * UT:(bp + 1) * UT], v[:, u, 2 * bp + b2, :],
                                                      p_t[:, bp, b2 * UT:(b2 + 1) * UT], start=True, stop=True)
                                continue
                            rows = slice(b2 * SEQ, (b2 + 1) * SEQ)
                            if kv_heads == 1:
                                mm = nc.tensor.matmul(out[:, bp * UT:(bp + 1) * UT], v[rows, par, bp, :],
                                                      p_t[rows, 0, bp * UT:(bp + 1) * UT], start=True, stop=True)
                                continue
                            for h in range(GH):
                                mm = nc.tensor.matmul(
                                    out[:, bp * UT + h * SEQ:bp * UT + (h + 1) * SEQ],
                                    v[rows, par, bp, h * HD:(h + 1) * HD],
                                    p_t[rows, 0, bp * UT + h * SEQ:bp * UT + (h + 1) * SEQ], start=True, stop=True)
                        mm.then_inc(sig.o_ready.sem, 1)

                def project_out(i, n):
                    uu, slot, u = BODY * i + n, n // UNITS, n % UNITS
                    pe.wait_ge(sig.o_done.sem, sig.o_done.at(2 * (uu + 1)))
                    for tt in range(2):
                        for h in range(GH):
                            mm = nc.tensor.matmul(bank[6 + tt][:, :], o_t[:, h, 2 * tt:2 * tt + 2, :],
                                                  wqo[:, slot, wq_cols + h * DIM:wq_cols + (h + 1) * DIM],
                                                  start=(h == 0), stop=(h == GH - 1))
                        mm.then_inc(sig.y_ready.sem, 1)

                if both:
                    pe.wait_ge(sig.prepared.sem, sig.prepared.at(2 * CH))
                with pe.Fori(0, rounds) as i:
                    for n in range(BODY):
                        project_q(i, n)
                        if n < UNITS or not both:
                            project_k(i, n)
                        if n:
                            turn_probs(i, n - 1)
                        if n < UNITS or not both:
                            project_v(i, n)
                        if rms:
                            turn_keys(i, n)
                        if n:
                            weighted_values(i, n - 1)
                        if rms:
                            query_squares(i, n)
                        scores(i, n)
                        if n:
                            project_out(i, n - 1)
                    turn_probs(i, BODY - 1)
                    weighted_values(i, BODY - 1)
                    project_out(i, BODY - 1)
                if not last:
                    norm_tensor(nc, pe, g)

            @block.scalar
            def _(act):
                def queries(i, n):
                    uu = BODY * i + n
                    for j in range(2):
                        act.wait_ge(sig.q_ready.sem, sig.q_ready.at(2 * uu + j + 1))
                        if rms:
                            nc.scalar.activation(q_sq[:, :, 2 * j:2 * j + 2, :].rearrange("p b h s -> p h b s"),
                                                 bank[j][:, :].rearrange("p (h b s) -> p h b s", h=2, b=UB),
                                                 ACT.Square).then_inc(sig.squared.sem, 1)
                            nc.scalar.mul(q_t[:, 2 * j:2 * j + 2, :].rearrange("p h s -> p (h s)"),
                                          bank[j][:, :], q_w[:, 0:1]).then_inc(sig.q_done.sem, 1)
                        else:
                            nc.scalar.copy(q_t[:, 2 * j:2 * j + 2, :].rearrange("p h s -> p (h s)"),
                                           bank[j][:, :]).then_inc(sig.q_done.sem, 1)

                def keys_out(i, n):
                    kr = k_round(i, n)
                    if rms:
                        act.wait_ge(sig.k_ready.sem, sig.k_ready.at(kr + 1))
                        for tt in range(2):
                            if tt == 1:
                                act.wait_ge(sig.act_step.sem, sig.act_step.at(2 * kr + 1))
                            nc.scalar.activation(k_junk[:], bank[2][:, tt * HD:(tt + 1) * HD], ACT.Square,
                                                 accum_out=ssq[:, tt:tt + 1]).then_inc(sig.act_step.sem, 1)
                        return
                    for j in range(kbanks):
                        act.wait_ge(sig.k_ready.sem, sig.k_ready.at(kbanks * kr + j + 1))
                        if both:
                            dst, src = k_t[:, n % UNITS, :], bank[2][:, :]
                        elif kv_heads == 1:
                            dst, src = k_t[:, 0, :], bank[2][:, 0:UT]
                        else:
                            dst = k_t[:, 2 * j:2 * j + 2, :].rearrange("p h s -> p (h s)")
                            src = bank[2 + j][:, :]
                        nc.scalar.copy(dst, src).then_inc(sig.k_done.sem, 1)

                def turned_keys(i, n):
                    uu = BODY * i + n
                    act.wait_ge(sig.keys_turned.sem, sig.keys_turned.at(uu + 1))
                    nc.scalar.mul(k_t[:, 0, :], bank[2][:, 0:UT], k_w[:, 0:1]).then_inc(sig.keys_taken.sem, 1)

                def outputs(i, n):
                    uu = BODY * i + n
                    for b2 in range(2):
                        act.wait_ge(sig.o_ready.sem, sig.o_ready.at(2 * uu + b2 + 1))
                        dst = o_t[:, :, :, :].rearrange("p h (bp b2) s -> p bp b2 h s", b2=2)[:, :, b2, :, :]
                        src = bank[6 + b2][:, :].rearrange("p (bp h s) -> p bp h s", bp=2, h=GH)
                        nc.scalar.copy(dst, src).then_inc(sig.o_done.sem, 1)

                def exponentials(i, n):
                    uu = BODY * i + n
                    for half in range(halves):
                        act.wait_ge(sig.shifted.sem, sig.shifted.at(halves * uu + half + 1))
                        nc.scalar.activation(probs[:, half, :], shifted[:, half, :], ACT.Exp,
                                             scale=1.0 if (bias is not None or rms) else scale).then_inc(
                            sig.exp_done.sem, 1)

                if both:
                    for c in range(CH):
                        nc.scalar.copy(joint[:, c, :, SELF, :], feat[:, SELF, c, :, :]).then_inc(sig.prepared.sem, 1)
                if rms or key_mask is not None or mask is not None:
                    act.wait_ge(sig.small_in.sem, sig.small_in.at(small_loads))
                with act.Fori(0, rounds) as i:
                    for n in range(BODY):
                        queries(i, n)
                        if n < UNITS or not both:
                            keys_out(i, n)
                        if rms:
                            turned_keys(i, n)
                        if n:
                            outputs(i, n - 1)
                        exponentials(i, n)
                    outputs(i, BODY - 1)
                if not last:
                    norm_scalar(nc, act, g)

            @block.vector
            def _(dve):
                head_steps = Steps(sig.dve_step)
                if both:
                    for c in range(CH):
                        nc.vector.tensor_copy(joint[:, c, :, CTX, :], feat[:, CTX, c, :, :]).then_inc(
                            sig.prepared.sem, 1)
                if key_mask is not None:
                    dve.wait_ge(sig.small_in.sem, sig.small_in.at(small_loads))
                    nc.vector.tensor_copy(km_one[:], km_u8[:]).then_inc(head_steps.count(), 1)
                    dve.wait_ge(sig.dve_step.sem, head_steps.so_far())
                    nc.vector.tensor_scalar(km_neg[:], km_one[:], 1.0, -NEG, ALU.subtract, ALU.mult).then_inc(
                        head_steps.count(), 1)
                    dve.wait_ge(sig.dve_step.sem, head_steps.so_far())
                if mask is not None:
                    dve.wait_ge(sig.small_in.sem, sig.small_in.at(small_loads))
                if rms:
                    nc.vector.memset(mean_col[:], 1.0 / HD).then_inc(head_steps.count(), 1)
                    dve.wait_ge(sig.dve_step.sem, head_steps.so_far())
                head = head_steps.n
                per_unit = halves * (before_exp + after_exp)

                def turned(i, n):
                    uu = BODY * i + n
                    for half in range(halves):
                        dve.wait_ge(sig.pt_ready.sem, sig.pt_ready.at(halves * uu + half + 1))
                        nc.vector.tensor_copy(p_t[:, half, :], bank[5][:, :]).then_inc(sig.pt_done.sem, 1)

                def values(i, n):
                    kr = k_round(i, n)
                    for j in range(kbanks):
                        dve.wait_ge(sig.v_ready.sem, sig.v_ready.at(kbanks * kr + j + 1))
                        if both:
                            dst, src = v[:, n % UNITS, :, :].rearrange("p b d -> p (b d)"), value_bank[:, :]
                        elif kbanks == 2:
                            dst, src = v[:, n % 2, j, :], bank[2 + j][:, :]
                        else:
                            dst, src = v[:, n % 2, :, :].rearrange("p t d -> p (t d)"), bank[3][:, 0:2 * HD]
                        nc.vector.tensor_copy(dst, src).then_inc(sig.v_done.sem, 1)

                def rms_keys(i, n):
                    uu = BODY * i + n
                    dve.wait_ge(sig.act_step.sem, sig.act_step.at(2 * uu + 2))
                    nc.vector.tensor_scalar(k_var[:], ssq[:], 1.0 / HD, LN_EPS, ALU.mult, ALU.add).then_inc(
                        sig.rms_var.sem, 1)
                    dve.wait_ge(sig.rms_power.sem, sig.rms_power.at(2 * uu + 1))
                    for tt in range(2):
                        mm = nc.vector.tensor_scalar(k_rows[:, tt, :], bank[2][:, tt * HD:(tt + 1) * HD],
                                                     k_rstd[:, tt:tt + 1], None, ALU.mult)
                    mm.then_inc(sig.rms_done.sem, 1)

                def rms_queries(i, n):
                    uu = BODY * i + n
                    dve.wait_ge(sig.rms_sum.sem, sig.rms_sum.at(uu + 1))
                    nc.vector.tensor_scalar(q_var[:], bank[5][:, 0:8], LN_EPS, 1.0 / scale ** 2, ALU.add,
                                            ALU.mult).then_inc(sig.rms_var.sem, 1)

                def softmax(i, n):
                    uu = BODY * i + n
                    for half in range(halves):
                        steps = Steps(sig.dve_step, head + per_unit * uu + before_exp * half)
                        dve.wait_ge(sig.s_ready.sem, sig.s_ready.at(halves * uu + half + 1))
                        raw = score_banks[half][:, :]
                        sh = shifted[:, half, :]
                        rows = raw.rearrange("p (g k) -> p g k", k=klen)
                        sh_rows = sh.rearrange("p (g k) -> p g k", k=klen)
                        m = mx[:, half, :]
                        if bias is not None:
                            if bias_cols == BATCH * GH // 2 * SEQ:
                                u = n % UNITS
                                b_ap = bias_sb[:, n // UNITS, u * 512:(u + 1) * 512]
                                nc.vector.scalar_tensor_tensor(sh, raw, scale, b_ap, ALU.mult,
                                                               ALU.add).then_inc(sig.s_read.sem, 1)
                            else:
                                b_ap = over(bias_sb[:, n // UNITS, :], (1, 2))
                                nc.vector.scalar_tensor_tensor(
                                    sh.rearrange("p (a c) -> p a c", a=2), raw.rearrange("p (a c) -> p a c", a=2),
                                    scale, b_ap, ALU.mult, ALU.add).then_inc(sig.s_read.sem, 1)
                            dve.wait_ge(sig.s_read.sem, sig.s_read.at(uu + 1))
                            if key_mask is not None:
                                u = n % UNITS
                                km = km_neg[:, UB * u:UB * u + UB, :].rearrange("p (a b) s -> p a (b s)", a=2)
                                four = sh.rearrange("p (a j c) -> p a j c", a=2, j=2)
                                nc.vector.tensor_tensor(four, four, over(km, (2, 2)), ALU.add).then_inc(
                                    steps.count(), 1)
                                dve.wait_ge(sig.dve_step.sem, steps.so_far())
                            nc.vector.tensor_reduce(m, sh_rows, AX.X, ALU.max).then_inc(steps.count(), 1)
                            dve.wait_ge(sig.dve_step.sem, steps.so_far())
                            nc.vector.tensor_tensor(sh_rows, sh_rows, over(m, (2, klen)), ALU.subtract).then_inc(
                                sig.shifted.sem, 1)
                        elif rms:
                            dve.wait_ge(sig.rms_power.sem, sig.rms_power.at(2 * uu + 2))
                            nc.vector.tensor_tensor(sh_rows, rows, over(q_rstd[:], (2, klen)), ALU.mult).then_inc(
                                sig.s_read.sem, 1)
                            dve.wait_ge(sig.s_read.sem, sig.s_read.at(uu + 1))
                            nc.vector.tensor_tensor(sh_rows, sh_rows, over(mask_sb[:], (1, ngr)),
                                                    ALU.add).then_inc(steps.count(), 1)
                            dve.wait_ge(sig.dve_step.sem, steps.so_far())
                            nc.vector.tensor_reduce(m, sh_rows, AX.X, ALU.max).then_inc(steps.count(), 1)
                            dve.wait_ge(sig.dve_step.sem, steps.so_far())
                            nc.vector.tensor_tensor(sh_rows, sh_rows, over(m, (2, klen)), ALU.subtract).then_inc(
                                sig.shifted.sem, 1)
                        else:
                            nc.vector.tensor_reduce(m, rows, AX.X, ALU.max).then_inc(steps.count(), 1)
                            dve.wait_ge(sig.dve_step.sem, steps.so_far())
                            nc.vector.tensor_tensor(sh_rows, rows, over(m, (2, klen)), ALU.subtract).then_inc(
                                sig.shifted.sem, 1)
                    for half in range(halves):
                        steps = Steps(sig.dve_step, head + per_unit * uu + before_exp * halves + after_exp * half)
                        pr_rows = probs[:, half, :].rearrange("p (g k) -> p g k", k=klen)
                        t, r = total[:, half, :], recip[:, half, :]
                        dve.wait_ge(sig.exp_done.sem, sig.exp_done.at(halves * uu + half + 1))
                        nc.vector.tensor_reduce(t, pr_rows, AX.X, ALU.add).then_inc(steps.count(), 1)
                        dve.wait_ge(sig.dve_step.sem, steps.so_far())
                        nc.vector.reciprocal(r, t).then_inc(steps.count(), 1)
                        dve.wait_ge(sig.dve_step.sem, steps.so_far())
                        if key_mask is not None:
                            u = n % UNITS
                            nc.vector.tensor_tensor(pr_rows, pr_rows, over(r, (2, klen)), ALU.mult).then_inc(
                                steps.count(), 1)
                            dve.wait_ge(sig.dve_step.sem, steps.so_far())
                            km = km_one[:, UB * u:UB * u + UB, :].rearrange("p (a b) s -> p a (b s)", a=2)
                            four = probs[:, half, :].rearrange("p (a j c) -> p a j c", a=2, j=2)
                            nc.vector.tensor_tensor(four, four, over(km, (2, 2)), ALU.mult).then_inc(
                                sig.p_ready.sem, 1)
                        else:
                            nc.vector.tensor_tensor(pr_rows, pr_rows, over(r, (2, klen)), ALU.mult).then_inc(
                                sig.p_ready.sem, 1)

                def add(i, n):
                    uu, u = BODY * i + n, n % UNITS
                    for tt in range(2):
                        dve.wait_ge(sig.y_ready.sem, sig.y_ready.at(2 * uu + tt + 1))
                        t = 2 * u + tt
                        nc.vector.tensor_tensor(x[:, t, :], x[:, t, :], bank[6 + tt][:, :], ALU.add).then_inc(
                            sig.added.sem, 1)

                with dve.Fori(0, rounds) as i:
                    for n in range(BODY):
                        if n:
                            turned(i, n - 1)
                        if n < UNITS or not both:
                            values(i, n)
                        if rms:
                            rms_keys(i, n)
                            rms_queries(i, n)
                        softmax(i, n)
                        if n:
                            add(i, n - 1)
                    turned(i, BODY - 1)
                    add(i, BODY - 1)
                dve.wait_ge(sig.added.sem, sig.added.at(2 * rounds * BODY))
                norm_vector(nc, dve, g)



def narrow_attention(nc, g, name, last, weights, keys, scale, bias=None, rope=None, out_proj=True):
    sig, feat, x, bank = g.sig, g.feat, g.x, g.bank
    nbody = 4
    rounds = TILES // nbody
    blocks = KV // 2
    wk_at, wv_at, wo_at = CH * DIM, CH * (DIM + P), CH * (DIM + 2 * P)
    vcols = 2 * (ND + 1)
    with ExitStack() as ctx:
        def sb(what, shape, dt=F32):
            return ctx.enter_context(nc.sbuf_tensor(f"{name}_{what}", shape, dt))
        w = sb("w", [P, weights.shape[1]])
        xs = sb("xs", [P, CH, nbody * P])
        ks = sb("ks", [P, CH, nbody * P]) if keys == CTX else xs
        q_t = sb("q_t", [P, NR, P])
        k_t = sb("k_t", [P, P])
        k_diag = sb("k_diag", [P, 2, KV, SEQ])
        v_diag = sb("v_diag", [P, 2, 2, blocks, 2, ND + 1])
        v_sum = sb("v_sum", [P, 2 * P])
        head_of = sb("head_of", [P, KV])
        half_of = sb("half_of", [P, 2])
        shifted = sb("shifted", [P, 2, 512])
        probs = sb("probs", [P, 2, 512])
        p_t = sb("p_t", [P, 512])
        mx = sb("mx", [P, 2, KV])
        recip = sb("recip", [P, HEADS])
        attn = sb("attn", [P, HEADS, ND])
        attn_t = sb("attn_t", [P, NR, P])
        if bias is not None:
            bias_sb = sb("bias", [P, NR, 512])
        if rope is not None:
            consts = sb("consts", [P, rope.shape[1]])
            rot = consts[:, 0:P]
            cos, sin = consts[:, P:P + SEQ], consts[:, P + SEQ:P + 2 * SEQ]
            at = P + 2 * SEQ
            q_bias, k_bias, v_bias = consts[:, at:at + NR], consts[:, at + NR:at + NR + 1], \
                consts[:, at + NR + 1:at + NR + 1 + P]
            turned_q = sb("turned_q", [P, NR * P])
            turned_k = sb("turned_k", [P, P])
        loads = 16 * (3 + (bias is not None) + (rope is not None))
        score_bank_free = sig.s_read if bias is not None else sig.shifted
        o_banks = (bank[3], bank[7])

        def o_block(r, jj):
            n = r * blocks + jj
            return (o_banks[0], n) if r < NR - 1 else (o_banks[1], n - (NR - 1) * blocks)

        with nc.Block() as block:
            @block.sync
            def _(sp):
                sp.dma_start(head_of[:], g.t["head_of"]).then_inc(sig.small_in.sem, 16)
                sp.dma_start(half_of[:], g.t["half_of"]).then_inc(sig.small_in.sem, 16)
                if rope is not None:
                    sp.dma_start(consts[:], rope).then_inc(sig.small_in.sem, 16)
                sp.dma_start(w[:], weights).then_inc(sig.small_in.sem, 16)
                if bias is not None:
                    sp.dma_start(bias_sb[:].rearrange("p r c -> p (r c)"), bias).then_inc(sig.small_in.sem, 16)
                if last:
                    norm_sync(nc, sp, g)

            @block.gpsimd
            def _(pool):
                norm_pool(nc, pool, g)

            @block.tensor
            def _(pe):
                def projections(i, n):
                    uu = nbody * i + n
                    if n == 0:
                        pe.wait_ge(sig.staged.sem, sig.staged.at((1 + (keys == CTX)) * (i + 1)))
                    kv = bank[2]
                    pe.wait_ge(sig.kd_done.sem, sig.kd_done.at(uu))
                    pe.wait_ge(sig.v_done.sem, sig.v_done.at(uu))
                    for b in range(2):
                        for dup in range(2):
                            for c in range(CH):
                                mm = nc.tensor.matmul(
                                    kv[dup * SEQ:(dup + 1) * SEQ, 2 * P + b * P:2 * P + (b + 1) * P],
                                    ks[:, c, n * P + b * SEQ:n * P + (b + 1) * SEQ],
                                    w[:, wv_at + c * P:wv_at + (c + 1) * P], start=(c == 0), stop=(c == CH - 1))
                    for c in range(CH):
                        mm = nc.tensor.matmul(kv[:, 0:P], w[:, wk_at + c * P:wk_at + (c + 1) * P],
                                              ks[:, c, n * P:(n + 1) * P], start=(c == 0), stop=(c == CH - 1))
                    mm.then_inc(sig.k_ready.sem, 1)
                    if out_proj:
                        pe.wait_ge(sig.added.sem, sig.added.at(uu if n == 0 else uu - 1))
                    pe.wait_ge(sig.q_done.sem, sig.q_done.at(uu))
                    for r in range(NR):
                        for c in range(CH):
                            mm = nc.tensor.matmul(bank[0][:, r * P:(r + 1) * P],
                                                  w[:, c * DIM + r * P:c * DIM + (r + 1) * P],
                                                  xs[:, c, n * P:(n + 1) * P], start=(c == 0), stop=(c == CH - 1))
                    mm.then_inc(sig.q_ready.sem, 1)

                def rotate(i, n):
                    uu = nbody * i + n
                    pe.wait_ge(sig.q_done.sem, sig.q_done.at(uu + 1))
                    nc.tensor.matmul(bank[1][:, :], rot, q_t[:].rearrange("p r s -> p (r s)"),
                                     start=True, stop=True)
                    nc.tensor.matmul(bank[0][:, 0:P], rot, k_t[:], start=True, stop=True).then_inc(
                        sig.rotated.sem, 1)

                def scores(i, n, r):
                    uu = nbody * i + n
                    if r == 0:
                        pe.wait_ge(sig.kd_done.sem, sig.kd_done.at(uu + 1))
                        if rope is None:
                            pe.wait_ge(sig.q_done.sem, sig.q_done.at(uu + 1))
                    ss = NR * uu + r
                    pe.wait_ge(score_bank_free.sem, score_bank_free.at(ss - 1))
                    for b in range(2):
                        mm = nc.tensor.matmul(bank[4 + r % 2][b * SEQ:(b + 1) * SEQ, :],
                                              q_t[:, r, b * SEQ:(b + 1) * SEQ],
                                              k_diag[:, b, :, :].rearrange("p h k -> p (h k)"),
                                              start=True, stop=True)
                    mm.then_inc(sig.s_ready.sem, 1)

                def turn_probs(i, n, r):
                    ss = NR * (nbody * i + n) + r
                    pe.wait_ge(sig.exp_done.sem, sig.exp_done.at(ss + 1))
                    pe.wait_ge(sig.pt_done.sem, sig.pt_done.at(ss))
                    for jj in range(blocks):
                        mm = nc.tensor.transpose(bank[6][:, jj * P:(jj + 1) * P],
                                                 probs[:, r % 2, jj * P:(jj + 1) * P], g.ident[:])
                    mm.then_inc(sig.pt_ready.sem, 1)

                def weighted_values(i, n, r):
                    uu = nbody * i + n
                    ss = NR * uu + r
                    if r == 0:
                        pe.wait_ge(sig.v_done.sem, sig.v_done.at(uu + 1))
                        pe.wait_ge(sig.o_done.sem, sig.o_done.at(uu))
                    pe.wait_ge(sig.pt_done.sem, sig.pt_done.at(ss + 1))
                    for jj in range(blocks):
                        ob, at_block = o_block(r, jj)
                        for b in range(2):
                            mm = nc.tensor.matmul(
                                ob[b * SEQ:(b + 1) * SEQ, at_block * vcols:(at_block + 1) * vcols],
                                p_t[:, jj * P + b * SEQ:jj * P + (b + 1) * SEQ],
                                v_diag[:, n % 2, b, jj, :, :].rearrange("p h d -> p (h d)"),
                                start=True, stop=True)
                    if r == NR - 1:
                        mm.then_inc(sig.o_ready.sem, 1)

                def turn_output(i, n):
                    uu = nbody * i + n
                    pe.wait_ge(sig.o_done.sem, sig.o_done.at(uu + 1))
                    pe.wait_ge(sig.attn_taken.sem, sig.attn_taken.at(uu))
                    for r in range(NR):
                        mm = nc.tensor.transpose(bank[1][:, r * P:(r + 1) * P],
                                                 attn[:, r * KV:(r + 1) * KV, :].rearrange("p h d -> p (h d)"),
                                                 g.ident[:])
                    mm.then_inc(sig.attn_turned.sem, 1)

                def project_out(i, n, queries_too):
                    uu = nbody * i + n
                    pe.wait_ge(sig.attn_taken.sem, sig.attn_taken.at(uu + 1))
                    if queries_too:
                        pe.wait_ge(sig.q_done.sem, sig.q_done.at(uu + 2))
                    for r in range(NR):
                        mm = nc.tensor.matmul(bank[0][:, :], attn_t[:, r, :],
                                              w[:, wo_at + r * DIM:wo_at + (r + 1) * DIM],
                                              start=(r == 0), stop=(r == NR - 1))
                    mm.then_inc(sig.y_ready.sem, 1)

                pe.wait_ge(sig.small_in.sem, sig.small_in.at(loads))
                with pe.Fori(0, rounds) as i:
                    for n in range(nbody + 1):
                        if n < nbody:
                            projections(i, n)
                        if n:
                            turn_probs(i, n - 1, 2)
                            weighted_values(i, n - 1, 2)
                            turn_probs(i, n - 1, 3)
                        if n < nbody and rope is not None:
                            rotate(i, n)
                        if n:
                            weighted_values(i, n - 1, 3)
                            if out_proj:
                                turn_output(i, n - 1)
                        if n < nbody:
                            scores(i, n, 0)
                            scores(i, n, 1)
                        if n and out_proj:
                            project_out(i, n - 1, n < nbody)
                        if n < nbody:
                            turn_probs(i, n, 0)
                            scores(i, n, 2)
                            weighted_values(i, n, 0)
                            turn_probs(i, n, 1)
                            scores(i, n, 3)
                            weighted_values(i, n, 1)
                if not last:
                    norm_tensor(nc, pe, g)

            @block.scalar
            def _(act):
                def stage(i):
                    if keys == CTX:
                        nc.scalar.copy(ks[:].rearrange("p c (b s) -> p c b s", s=SEQ),
                                       feat[:, CTX, :, bass.ds(i * 2 * nbody, 2 * nbody), :]).then_inc(
                            sig.staged.sem, 1)
                    nc.scalar.copy(xs[:].rearrange("p c (b s) -> p c b s", s=SEQ),
                                   feat[:, SELF, :, bass.ds(i * 2 * nbody, 2 * nbody), :]).then_inc(
                        sig.staged.sem, 1)

                def queries(i, n):
                    uu = nbody * i + n
                    act.wait_ge(sig.q_ready.sem, sig.q_ready.at(uu + 1))
                    if rope is None:
                        nc.scalar.copy(q_t[:].rearrange("p r s -> p (r s)"), bank[0][:, :]).then_inc(
                            sig.q_done.sem, 1)
                        return
                    for r in range(NR):
                        nc.scalar.activation(q_t[:, r, :], bank[0][:, r * P:(r + 1) * P], ACT.Identity,
                                             bias=q_bias[:, r:r + 1])
                    nc.scalar.activation(k_t[:], bank[2][:, 0:P], ACT.Identity, bias=k_bias).then_inc(
                        sig.q_done.sem, 1)

                def exponentials(i, n, r):
                    ss = NR * (nbody * i + n) + r
                    act.wait_ge(sig.shifted.sem, sig.shifted.at(ss + 1))
                    nc.scalar.activation(probs[:, r % 2, :], shifted[:, r % 2, :], ACT.Exp,
                                         scale=1.0 if bias is not None else scale).then_inc(sig.exp_done.sem, 1)

                def turned(i, n, r):
                    ss = NR * (nbody * i + n) + r
                    act.wait_ge(sig.pt_ready.sem, sig.pt_ready.at(ss + 1))
                    nc.scalar.copy(p_t[:], bank[6][:, :]).then_inc(sig.pt_done.sem, 1)

                def output(i, n):
                    uu = nbody * i + n
                    act.wait_ge(sig.attn_turned.sem, sig.attn_turned.at(uu + 1))
                    nc.scalar.copy(attn_t[:].rearrange("p r s -> p (r s)"), bank[1][:, :]).then_inc(
                        sig.attn_taken.sem, 1)

                act.wait_ge(sig.small_in.sem, sig.small_in.at(loads))
                with act.Fori(0, rounds) as i:
                    stage(i)
                    for n in range(nbody + 1):
                        if n < nbody:
                            queries(i, n)
                        if n:
                            turned(i, n - 1, 2)
                            turned(i, n - 1, 3)
                            if out_proj:
                                output(i, n - 1)
                        if n < nbody:
                            exponentials(i, n, 0)
                            exponentials(i, n, 1)
                            turned(i, n, 0)
                            exponentials(i, n, 2)
                            turned(i, n, 1)
                            exponentials(i, n, 3)
                if not last:
                    norm_scalar(nc, act, g)

            @block.vector
            def _(dve):
                def spread(i, n, steps):
                    uu = nbody * i + n
                    dve.wait_ge(sig.k_ready.sem, sig.k_ready.at(uu + 1))
                    vals = bank[2][:, 2 * P:4 * P]
                    if rope is not None:
                        dve.wait_ge(sig.q_done.sem, sig.q_done.at(uu + 1))
                        nc.vector.tensor_tensor(v_sum[:].rearrange("p (b c) -> p b c", b=2),
                                                vals.rearrange("p (b c) -> p b c", b=2), over(v_bias, (1, 2)),
                                                ALU.add).then_inc(steps.count(), 1)
                        dve.wait_ge(sig.dve_step.sem, steps.so_far())
                        vals = v_sum[:]
                    nc.vector.tensor_tensor(
                        v_diag[:, n % 2, :, :, :, 0:ND].rearrange("p b j h d -> p (b j) h d"),
                        vals.rearrange("p (bj h d) -> p bj h d", h=2, d=ND),
                        over(half_of[:], (1, 2 * blocks), (3, ND)), ALU.mult).then_inc(sig.v_done.sem, 1)
                    key = bank[2][:, 0:P]
                    if rope is not None:
                        dve.wait_ge(sig.rotated.sem, sig.rotated.at(uu + 1))
                        nc.vector.tensor_tensor(turned_q[:].rearrange("p (a s) -> p a s", s=SEQ),
                                                bank[1][:, :].rearrange("p (a s) -> p a s", s=SEQ),
                                                over(sin, (1, 2 * NR)), ALU.mult).then_inc(steps.count(), 1)
                        nc.vector.tensor_tensor(turned_k[:].rearrange("p (a s) -> p a s", s=SEQ),
                                                bank[0][:, 0:P].rearrange("p (a s) -> p a s", s=SEQ),
                                                over(sin, (1, 2)), ALU.mult).then_inc(steps.count(), 1)
                        q_rows = q_t[:].rearrange("p r (b s) -> p (r b) s", s=SEQ)
                        k_rows = k_t[:].rearrange("p (b s) -> p b s", s=SEQ)
                        nc.vector.tensor_tensor(q_rows, q_rows, over(cos, (1, 2 * NR)), ALU.mult).then_inc(
                            steps.count(), 1)
                        nc.vector.tensor_tensor(k_rows, k_rows, over(cos, (1, 2)), ALU.mult).then_inc(
                            steps.count(), 1)
                        dve.wait_ge(sig.dve_step.sem, steps.so_far())
                        q_flat = q_t[:].rearrange("p r s -> p (r s)")
                        nc.vector.tensor_tensor(q_flat, q_flat, turned_q[:], ALU.add).then_inc(steps.count(), 1)
                        nc.vector.tensor_tensor(k_t[:], k_t[:], turned_k[:], ALU.add).then_inc(steps.count(), 1)
                        dve.wait_ge(sig.dve_step.sem, steps.so_far())
                        key = k_t[:]
                    for b in range(2):
                        ins = nc.vector.tensor_tensor(k_diag[:, b, :, :], over(key[:, b * SEQ:(b + 1) * SEQ], (1, KV)),
                                                      over(head_of[:], (2, SEQ)), ALU.mult)
                    ins.then_inc(sig.kd_done.sem, 1)

                def softmax(i, n, r, steps):
                    ss = NR * (nbody * i + n) + r
                    dve.wait_ge(sig.s_ready.sem, sig.s_ready.at(ss + 1))
                    raw = bank[4 + r % 2][:, :]
                    sh = shifted[:, r % 2, :]
                    m = mx[:, r % 2, :]
                    src = raw
                    if bias is not None:
                        nc.vector.scalar_tensor_tensor(sh, raw, scale, bias_sb[:, r, :], ALU.mult, ALU.add).then_inc(
                            sig.s_read.sem, 1)
                        dve.wait_ge(sig.s_read.sem, sig.s_read.at(ss + 1))
                        src = sh
                    rows = src.rearrange("p (h k) -> p h k", k=SEQ)
                    nc.vector.tensor_reduce(m, rows, AX.X, ALU.max).then_inc(steps.count(), 1)
                    dve.wait_ge(sig.dve_step.sem, steps.so_far())
                    nc.vector.tensor_tensor(sh.rearrange("p (h k) -> p h k", k=SEQ), rows, over(m, (2, SEQ)),
                                            ALU.subtract).then_inc(sig.shifted.sem, 1)

                def normalise(i, n, steps):
                    uu = nbody * i + n
                    dve.wait_ge(sig.o_ready.sem, sig.o_ready.at(uu + 1))
                    first = (NR - 1) * KV
                    parts = [(o_banks[0][:, 0:first * (ND + 1)], 0, first),
                             (o_banks[1][:, 0:KV * (ND + 1)], first, HEADS)]
                    for ob, lo, hi in parts:
                        rows = ob.rearrange("p (h d) -> p h d", d=ND + 1)
                        nc.vector.reciprocal(recip[:, lo:hi], rows[:, :, ND]).then_inc(steps.count(), 1)
                    dve.wait_ge(sig.dve_step.sem, steps.so_far())
                    for ob, lo, hi in parts:
                        rows = ob.rearrange("p (h d) -> p h d", d=ND + 1)
                        ins = nc.vector.tensor_tensor(attn[:, lo:hi, :], rows[:, :, 0:ND],
                                                      over(recip[:, lo:hi], (2, ND)), ALU.mult)
                    ins.then_inc(sig.o_done.sem, 1)
                    if not out_proj:
                        dve.wait_ge(sig.o_done.sem, sig.o_done.at(uu + 1))
                        tile = x[:, bass.ds(uu, 1), :].rearrange("p t (k r d) -> p (t r) k d", k=KV, r=NR)
                        nc.vector.tensor_tensor(tile, tile, attn[:].rearrange("p (r k) d -> p r k d", r=NR),
                                                ALU.add).then_inc(sig.added.sem, 1)

                def add(i, n):
                    uu = nbody * i + n
                    dve.wait_ge(sig.y_ready.sem, sig.y_ready.at(uu + 1))
                    tile = x[:, bass.ds(uu, 1), :].rearrange("p t c -> p (t c)")
                    nc.vector.tensor_tensor(tile, tile, bank[0][:, :], ALU.add).then_inc(sig.added.sem, 1)

                head = Steps(sig.dve_step)
                dve.wait_ge(sig.small_in.sem, sig.small_in.at(loads))
                nc.vector.memset(v_diag[:], 0.0).then_inc(head.count(), 1)
                dve.wait_ge(sig.dve_step.sem, head.so_far())
                for par in range(2):
                    for h in range(2):
                        nc.vector.tensor_copy(v_diag[:, par, :, :, h, ND:ND + 1].rearrange("p b j d -> p (b j) d"),
                                              over(half_of[:, h:h + 1], (1, 2 * blocks))).then_inc(head.count(), 1)
                dve.wait_ge(sig.dve_step.sem, head.so_far())
                per_body = nbody * ((7 if rope is not None else 0) + NR + 2)
                with dve.Fori(0, rounds) as i:
                    steps = Steps(sig.dve_step, head.n + per_body * i)
                    for n in range(nbody + 1):
                        if n < nbody:
                            spread(i, n, steps)
                        if n:
                            normalise(i, n - 1, steps)
                        if n < nbody:
                            softmax(i, n, 0, steps)
                            softmax(i, n, 1, steps)
                        if n and out_proj:
                            add(i, n - 1)
                        if n < nbody:
                            softmax(i, n, 2, steps)
                            softmax(i, n, 3, steps)
                    assert steps.n == per_body
                dve.wait_ge(sig.added.sem, sig.added.at(TILES))
                norm_vector(nc, dve, g)



def routed_ffn(nc, g, name, last, weights, low, experts, rank, chosen, scaling, expert_bias=None, out_bias=None):
    sig, feat, x, bank = g.sig, g.feat, g.x, g.bank
    er = experts * rank
    cols = DIM + experts + er
    per_bank = 512 // er
    with ExitStack() as ctx:
        def sb(what, shape, dt=F32):
            return ctx.enter_context(nc.sbuf_tensor(f"{name}_{what}", shape, dt))
        w = sb("w", [P, CH, cols])
        up = sb("up", [er, DIM])
        before = sb("before", [P, experts, experts])
        logits = sb("logits", [P, TILES, experts])
        larger = sb("larger", [P, TILES, experts, experts])
        equal = sb("equal", [P, TILES, experts, experts])
        place = sb("place", [P, TILES, experts])
        weight = sb("weight", [P, TILES, experts])
        powers = sb("powers", [P, TILES, experts])
        top = sb("top", [P, TILES])
        z = sb("z", [P, 2, er])
        z_t = sb("z_t", [er, 2, P])
        if expert_bias is not None:
            e_bias = sb("e_bias", [P, experts])
        if out_bias is not None:
            o_bias = sb("o_bias", [P, DIM])
        loads = 16 * (3 + (expert_bias is not None) + (out_bias is not None))
        turn_banks = (bank[0], bank[7])

        with nc.Block() as block:
            @block.sync
            def _(sp):
                sp.dma_start(w[:].rearrange("p c n -> p (c n)"), weights).then_inc(sig.small_in.sem, 16)
                sp.dma_start(up[:], low).then_inc(sig.small_in.sem, 16)
                sp.dma_start(before[:].rearrange("p a b -> p (a b)"), g.t["before%d" % experts]).then_inc(
                    sig.small_in.sem, 16)
                if expert_bias is not None:
                    sp.dma_start(e_bias[:], expert_bias).then_inc(sig.small_in.sem, 16)
                if out_bias is not None:
                    sp.dma_start(o_bias[:], out_bias).then_inc(sig.small_in.sem, 16)
                if last:
                    norm_sync(nc, sp, g)

            @block.gpsimd
            def _(pool):
                if out_bias is not None:
                    pool.wait_ge(sig.small_in.sem, loads)
                    nc.gpsimd.tensor_tensor(x[:], x[:], over(o_bias[:], (1, TILES)), ALU.add).then_inc(
                        sig.prepared.sem, 1)
                norm_pool(nc, pool, g)

            @block.tensor
            def _(pe):
                def features(t, c):
                    return feat[:, SELF, c, 2 * t:2 * t + 2, :].rearrange("p b s -> p (b s)")

                def base(t):
                    if t >= 4:
                        pe.wait_ge(sig.added.sem, sig.added.at(t - 3))
                    for c in range(CH):
                        nc.tensor.matmul(bank[3 + t % 4][:, :], features(t, c), w[:, c, 0:DIM],
                                         start=(c == 0), stop=False)

                pe.wait_ge(sig.small_in.sem, loads)
                for t in range(TILES):
                    for c in range(CH):
                        mm = nc.tensor.matmul(bank[0][:, t * experts:(t + 1) * experts], features(t, c),
                                              w[:, c, DIM:DIM + experts], start=(c == 0), stop=(c == CH - 1))
                mm.then_inc(sig.logits_ready.sem, 1)
                for t in range(TILES):
                    at = t % per_bank * er
                    for c in range(CH):
                        mm = nc.tensor.matmul(bank[1 + t // per_bank][:, at:at + er], features(t, c),
                                              w[:, c, DIM + experts:cols], start=(c == 0), stop=(c == CH - 1))
                mm.then_inc(sig.z_ready.sem, 1)
                base(0)
                base(1)
                for t in range(TILES):
                    pe.wait_ge(sig.z_weighted.sem, t + 1)
                    if t >= 2:
                        pe.wait_ge(sig.z_turned.sem, t - 1)
                    nc.tensor.transpose(turn_banks[t % 2][0:er, 0:P], z[:, t % 2, :], g.ident[:]).then_inc(
                        sig.z_turning.sem, 1)
                    if t + 2 < TILES:
                        base(t + 2)
                    pe.wait_ge(sig.z_turned.sem, t + 1)
                    nc.tensor.matmul(bank[3 + t % 4][:, :], z_t[:, t % 2, :], up[:], start=False,
                                     stop=True).then_inc(sig.y_ready.sem, 1)
                if not last:
                    norm_tensor(nc, pe, g)

            @block.scalar
            def _(act):
                if chosen > 1:
                    act.wait_ge(sig.shifted.sem, sig.shifted.at(1))
                    nc.scalar.activation(powers[:], powers[:], ACT.Exp).then_inc(sig.exp_done.sem, 1)
                for t in range(TILES):
                    act.wait_ge(sig.z_turning.sem, t + 1)
                    nc.scalar.copy(z_t[:, t % 2, :], turn_banks[t % 2][0:er, 0:P]).then_inc(sig.z_turned.sem, 1)
                if not last:
                    norm_scalar(nc, act, g)

            @block.vector
            def _(dve):
                steps = Steps(sig.dve_step)
                dve.wait_ge(sig.small_in.sem, loads)
                dve.wait_ge(sig.logits_ready.sem, 1)
                raw = bank[0][:, 0:TILES * experts].rearrange("p (t e) -> p t e", e=experts)
                if expert_bias is not None:
                    nc.vector.tensor_tensor(logits[:], raw, over(e_bias[:], (1, TILES)), ALU.add).then_inc(
                        steps.count(), 1)
                else:
                    nc.vector.tensor_copy(logits[:], raw).then_inc(steps.count(), 1)
                dve.wait_ge(sig.dve_step.sem, steps.so_far())
                if chosen > 1:
                    nc.vector.tensor_reduce(top[:], logits[:], AX.X, ALU.max).then_inc(steps.count(), 1)
                    dve.wait_ge(sig.dve_step.sem, steps.so_far())
                    nc.vector.tensor_tensor(powers[:], logits[:], over(top[:], (2, experts)),
                                            ALU.subtract).then_inc(sig.shifted.sem, 1)
                other, own = over(logits[:], (2, experts)), over(logits[:], (3, experts))
                nc.vector.tensor_tensor(larger[:], other, own, ALU.is_gt).then_inc(steps.count(), 1)
                nc.vector.tensor_tensor(equal[:], other, own, ALU.is_equal).then_inc(steps.count(), 1)
                dve.wait_ge(sig.dve_step.sem, steps.so_far())
                nc.vector.tensor_tensor(equal[:], equal[:], over(before[:], (1, TILES)), ALU.mult).then_inc(
                    steps.count(), 1)
                dve.wait_ge(sig.dve_step.sem, steps.so_far())
                nc.vector.tensor_tensor(larger[:], larger[:], equal[:], ALU.add).then_inc(steps.count(), 1)
                dve.wait_ge(sig.dve_step.sem, steps.so_far())
                nc.vector.tensor_reduce(place[:], larger[:], AX.X, ALU.add).then_inc(steps.count(), 1)
                dve.wait_ge(sig.dve_step.sem, steps.so_far())
                nc.vector.tensor_scalar(weight[:], place[:], float(chosen), None, ALU.is_lt).then_inc(
                    steps.count(), 1)
                dve.wait_ge(sig.dve_step.sem, steps.so_far())
                if chosen > 1:
                    dve.wait_ge(sig.exp_done.sem, 1)
                    nc.vector.tensor_tensor(weight[:], weight[:], powers[:], ALU.mult).then_inc(steps.count(), 1)
                    dve.wait_ge(sig.dve_step.sem, steps.so_far())
                    nc.vector.tensor_reduce(top[:], weight[:], AX.X, ALU.add).then_inc(steps.count(), 1)
                    dve.wait_ge(sig.dve_step.sem, steps.so_far())
                    nc.vector.reciprocal(top[:], top[:]).then_inc(steps.count(), 1)
                    dve.wait_ge(sig.dve_step.sem, steps.so_far())
                    nc.vector.scalar_tensor_tensor(weight[:], weight[:], scaling, over(top[:], (2, experts)),
                                                   ALU.mult, ALU.mult).then_inc(steps.count(), 1)
                    dve.wait_ge(sig.dve_step.sem, steps.so_far())
                dve.wait_ge(sig.z_ready.sem, 1)

                def weigh(t):
                    if t >= 2:
                        dve.wait_ge(sig.z_turning.sem, t - 1)
                    at = t % per_bank * er
                    nc.vector.tensor_tensor(
                        z[:, t % 2, :].rearrange("p (e r) -> p e r", e=experts),
                        bank[1 + t // per_bank][:, at:at + er].rearrange("p (e r) -> p e r", e=experts),
                        over(weight[:, t, :], (2, rank)), ALU.mult).then_inc(sig.z_weighted.sem, 1)

                weigh(0)
                weigh(1)
                if out_bias is not None:
                    dve.wait_ge(sig.prepared.sem, 1)
                for t in range(TILES):
                    if t + 2 < TILES:
                        weigh(t + 2)
                    dve.wait_ge(sig.y_ready.sem, t + 1)
                    nc.vector.tensor_tensor(x[:, t, :], x[:, t, :], bank[3 + t % 4][:, :], ALU.add).then_inc(
                        sig.added.sem, 1)
                dve.wait_ge(sig.added.sem, sig.added.at(TILES))
                norm_vector(nc, dve, g)



def unlike_attention(nc, g, name, last, eta):
    sig, feat, x, bank = g.sig, g.feat, g.x, g.bank
    per_bank = 512 // P
    with ExitStack() as ctx:
        def sb(what, shape, dt=F32):
            return ctx.enter_context(nc.sbuf_tensor(f"{name}_{what}", shape, dt))
        eta_sb = sb("eta", [P, 1])
        twice = sb("twice", [P, TILES, DIM])
        least = sb("least", [P, TILES])
        probs = sb("probs", [P, TILES, P])
        p_t = sb("p_t", [P, 2, P])
        total = sb("total", [P, TILES])
        factor = sb("factor", [P, TILES])
        turn_banks = (bank[2], bank[3])
        out_banks = bank[4:8]

        def block_of(h):
            return slice(h * SEQ, (h + 1) * SEQ)

        with nc.Block() as block:
            @block.sync
            def _(sp):
                sp.dma_start(eta_sb[:], eta).then_inc(sig.small_in.sem, 16)
                if last:
                    norm_sync(nc, sp, g)

            @block.gpsimd
            def _(pool):
                nc.gpsimd.memset(probs[:], 0.0).then_inc(sig.zeroed.sem, 1)
                nc.gpsimd.tensor_tensor(twice[:], x[:], x[:], ALU.add).then_inc(sig.prepared.sem, 1)
                norm_pool(nc, pool, g)

            @block.tensor
            def _(pe):
                for t in range(TILES):
                    for c in range(CH):
                        f = feat[:, SELF, c, 2 * t:2 * t + 2, :].rearrange("p b s -> p (b s)")
                        mm = nc.tensor.matmul(bank[t // per_bank][:, t % per_bank * P:(t % per_bank + 1) * P], f, f,
                                              start=(c == 0), stop=(c == CH - 1))
                    if t % per_bank == per_bank - 1:
                        mm.then_inc(sig.s_ready.sem, 1)
                for t in range(TILES):
                    pe.wait_ge(sig.exp_done.sem, 2 * (t + 1))
                    if t >= 2:
                        pe.wait_ge(sig.pt_done.sem, sig.pt_done.at(t - 1))
                    nc.tensor.transpose(turn_banks[t % 2][:, 0:P], probs[:, t, :], g.ident[:]).then_inc(
                        sig.pt_ready.sem, 1)
                    if t >= 4:
                        pe.wait_ge(sig.added.sem, sig.added.at(t - 3))
                    pe.wait_ge(sig.pt_done.sem, sig.pt_done.at(t + 1))
                    nc.tensor.matmul(out_banks[t % 4][:, :], p_t[:, t % 2, :], x[:, t, :], start=True,
                                     stop=True).then_inc(sig.y_ready.sem, 1)
                if not last:
                    norm_tensor(nc, pe, g)

            @block.scalar
            def _(act):
                act.wait_ge(sig.zeroed.sem, 1)
                for t in range(TILES):
                    if t % per_bank == 0:
                        act.wait_ge(sig.least.sem, t // per_bank + 1)
                    at = t % per_bank * P
                    for h in range(2):
                        rows = block_of(h)
                        nc.scalar.activation(probs[rows, t, rows],
                                             bank[t // per_bank][rows, at + h * SEQ:at + (h + 1) * SEQ], ACT.Exp,
                                             bias=least[rows, t:t + 1], scale=-1.0,
                                             accum_out=total[rows, t:t + 1]).then_inc(sig.exp_done.sem, 1)
                if not last:
                    norm_scalar(nc, act, g)

            @block.vector
            def _(dve):
                steps = Steps(sig.dve_step)
                for n in range(TILES // per_bank):
                    dve.wait_ge(sig.s_ready.sem, n + 1)
                    for h in range(2):
                        rows = block_of(h)
                        src = bank[n][rows, :].rearrange("p (t k) -> p t k", k=P)[:, :, rows]
                        mm = nc.vector.tensor_reduce(least[rows, n * per_bank:(n + 1) * per_bank], src, AX.X,
                                                     ALU.min)
                    mm.then_inc(sig.least.sem, 1)
                for t in range(TILES):
                    at = t % 2
                    dve.wait_ge(sig.pt_ready.sem, t + 1)
                    if t >= 2:
                        dve.wait_ge(sig.y_ready.sem, t - 1)
                    nc.vector.tensor_copy(p_t[:, at, :], turn_banks[at][:, 0:P]).then_inc(sig.pt_done.sem, 1)
                    if t == 0:
                        dve.wait_ge(sig.exp_done.sem, 2 * TILES)
                        nc.vector.reciprocal(factor[:], total[:]).then_inc(steps.count(), 1)
                        dve.wait_ge(sig.small_in.sem, 16)
                        dve.wait_ge(sig.dve_step.sem, steps.so_far())
                        nc.vector.tensor_scalar(factor[:], factor[:], eta_sb[:, 0:1], None, ALU.mult).then_inc(
                            steps.count(), 1)
                        dve.wait_ge(sig.dve_step.sem, steps.so_far())
                        dve.wait_ge(sig.prepared.sem, 1)
                    dve.wait_ge(sig.y_ready.sem, t + 1)
                    nc.vector.scalar_tensor_tensor(x[:, t, :], out_banks[t % 4][:, :], factor[:, t:t + 1],
                                                   twice[:, t, :], ALU.mult, ALU.add).then_inc(sig.added.sem, 1)
                dve.wait_ge(sig.added.sem, sig.added.at(TILES))
                norm_vector(nc, dve, g)



BOTTLE, ROUTE, SLOTS, TOP, VALUE = 64, 48, 128, 8, 32
TAU_LOW, TAU_HIGH, EARLY_EXIT = 0.5, 2.0, 0.05
GELU_CUBE, GELU_SCALE = 0.044715, math.sqrt(2.0 / math.pi)


def memory_ffn(nc, g, name, last):
    sig, feat, x, bank = g.sig, g.feat, g.x, g.bank
    hidden = P
    four = 512 // SLOTS
    groups = TILES // four
    wcols = BOTTLE + hidden + VALUE + SLOTS
    with ExitStack() as ctx:
        def sb(what, shape, dt=F32):
            return ctx.enter_context(nc.sbuf_tensor(f"{name}_{what}", shape, dt))
        w = sb("w", [P, CH, wcols])
        small = sb("small", [BOTTLE, ROUTE + SLOTS])
        w_vu = sb("w_vu", [VALUE, DIM])
        log_rel = sb("log_rel", [P, SLOTS])
        cols = sb("cols", [P, 5])
        q_t = sb("q_t", [BOTTLE, TOKENS])
        rq_t = sb("rq_t", [ROUTE, TOKENS])
        rk_t = sb("rk_t", [ROUTE, SLOTS])
        down = sb("down", [VALUE, SLOTS])
        slot_values = sb("slot_values", [SLOTS, DIM])
        y = sb("y", [P, TOKENS])
        inner = sb("inner", [P, TOKENS])
        th = sb("th", [P, TOKENS])
        route = sb("route", [P, four, SLOTS])
        rest = sb("rest", [P, four, SLOTS])
        top = sb("top", [P, four, TOP])
        scores = sb("scores", [P, four, SLOTS])
        mx = sb("mx", [P, four])
        probs = sb("probs", [P, groups, four, SLOTS])
        p_t = sb("p_t", [P, groups, four * P])
        total = sb("total", [P, TILES])
        stats = sb("stats", [P, TILES, 6])
        mv = sb("mv", [P, TILES, 2])
        log_var = sb("log_var", [P, TILES])
        log_sum = sb("log_sum", [P, 1])
        ones = sb("ones", [P, P])
        mean = sb("mean", [P, 1])
        u = sb("u", [P, TILES])
        gate = sb("gate", [P, TILES])
        loads = 16 * 5
        w_q = (0, BOTTLE)
        w_u1 = (BOTTLE, BOTTLE + hidden)
        w_vd = (BOTTLE + hidden, BOTTLE + hidden + VALUE)
        values = (BOTTLE + hidden + VALUE, wcols)
        out_banks = (bank[7], bank[0], bank[4])

        with nc.Block() as block:
            @block.sync
            def _(sp):
                sp.dma_start(w[:].rearrange("p c n -> p (c n)"), g.t[name + "_w"]).then_inc(sig.small_in.sem, 16)
                sp.dma_start(small[:], g.t[name + "_small"]).then_inc(sig.small_in.sem, 16)
                sp.dma_start(w_vu[:], g.t[name + "_w_vu"]).then_inc(sig.small_in.sem, 16)
                sp.dma_start(log_rel[:], g.t[name + "_log_rel"]).then_inc(sig.small_in.sem, 16)
                sp.dma_start(cols[:], g.t[name + "_cols"]).then_inc(sig.small_in.sem, 16)
                if last:
                    norm_sync(nc, sp, g)

            @block.gpsimd
            def _(pool):
                for n in range(2):
                    part = slice(n * 512, (n + 1) * 512)
                    pool.wait_ge(sig.y_squared.sem, n + 1)
                    nc.gpsimd.tensor_scalar(inner[:, part], inner[:, part], GELU_CUBE, 1.0, ALU.mult,
                                            ALU.add).then_inc(sig.pool_step.sem, 1)
                    pool.wait_ge(sig.pool_step.sem, n + 1)
                    nc.gpsimd.tensor_tensor(inner[:, part], inner[:, part], y[:, part], ALU.mult).then_inc(
                        sig.inner_done.sem, 1)
                pool.wait_ge(sig.x_read.sem, 1)
                nc.gpsimd.tensor_tensor(x[:], x[:], x[:], ALU.add).then_inc(sig.prepared.sem, 1)
                norm_pool(nc, pool, g)

            @block.tensor
            def _(pe):
                def tokens_at(n, c):
                    return feat[:, SELF, c, n * 8:(n + 1) * 8, :].rearrange("p b s -> p (b s)")

                def project(dst, which, n):
                    for c in range(CH):
                        mm = nc.tensor.matmul(dst, w[:, c, which[0]:which[1]], tokens_at(n, c), start=(c == 0),
                                              stop=(c == CH - 1))
                    return mm

                pe.wait_ge(sig.small_in.sem, loads)
                for n in range(2):
                    project(bank[n][0:BOTTLE, :], w_q, n).then_inc(sig.q_ready.sem, 1)
                nc.tensor.matmul(bank[6][0:ROUTE, 0:SLOTS], small[:, 0:ROUTE], small[:, ROUTE:ROUTE + SLOTS],
                                 start=True, stop=True)
                for c in range(CH):
                    mm = nc.tensor.matmul(bank[6][0:VALUE, SLOTS:2 * SLOTS], w[:, c, w_vd[0]:w_vd[1]],
                                          w[:, c, values[0]:values[1]], start=(c == 0), stop=(c == CH - 1))
                mm.then_inc(sig.k_ready.sem, 1)
                for n in range(2):
                    pe.wait_ge(sig.q_done.sem, sig.q_done.at(n + 1))
                    nc.tensor.matmul(bank[4 + n][0:ROUTE, :], small[:, 0:ROUTE], q_t[:, n * 512:(n + 1) * 512],
                                     start=True, stop=True).then_inc(sig.rq_ready.sem, 1)
                pe.wait_ge(sig.k_done.sem, sig.k_done.at(2))
                nc.tensor.matmul(bank[7][:, :], down[:], w_vu[:], start=True, stop=True).then_inc(
                    sig.v_ready.sem, 1)
                for n in range(2):
                    project(bank[2 + n][:, :], w_u1, n).then_inc(sig.hidden_ready.sem, 1)
                pe.wait_ge(sig.rq_done.sem, groups)
                for n in range(groups):
                    for tt in range(four):
                        t = n * four + tt
                        nc.tensor.matmul(bank[n][:, tt * SLOTS:(tt + 1) * SLOTS], rq_t[:, t * P:(t + 1) * P],
                                         rk_t[:], start=True, stop=True)
                        mm = nc.tensor.matmul(bank[4 + n][:, tt * SLOTS:(tt + 1) * SLOTS],
                                              q_t[:, t * P:(t + 1) * P], small[:, ROUTE:ROUTE + SLOTS],
                                              start=True, stop=True)
                    mm.then_inc(sig.s_ready.sem, 1)
                pe.wait_ge(sig.log_summed.sem, 1)
                nc.tensor.matmul(bank[6][:, TILES:TILES + 1], ones[:], log_sum[:], start=True, stop=True)
                pe.wait_ge(sig.gelu_done.sem, 2)
                for t in range(TILES):
                    mm = nc.tensor.matmul(bank[6][:, t:t + 1], y[:, t * P:(t + 1) * P], cols[:, 1:2], start=True,
                                          stop=True)
                mm.then_inc(sig.learned_ready.sem, 1)
                for n in range(groups):
                    pe.wait_ge(sig.exp_done.sem, four * (n + 1))
                    for tt in range(four):
                        mm = nc.tensor.transpose(bank[2 + n][:, tt * P:(tt + 1) * P], probs[:, n, tt, :],
                                                 g.ident[:])
                    mm.then_inc(sig.pt_ready.sem, 1)
                    pe.wait_ge(sig.pt_done.sem, sig.pt_done.at(n + 1))
                    for tt in range(four):
                        t = n * four + tt
                        if t == 0:
                            pe.wait_ge(sig.v_done.sem, sig.v_done.at(1))
                        if t >= 3:
                            pe.wait_ge(sig.added.sem, sig.added.at(t - 2))
                        nc.tensor.matmul(out_banks[t % 3][:, :], p_t[:, n, tt * P:(tt + 1) * P], slot_values[:],
                                         start=True, stop=True).then_inc(sig.y_ready.sem, 1)
                if not last:
                    norm_tensor(nc, pe, g)

            @block.scalar
            def _(act):
                for n in range(2):
                    act.wait_ge(sig.q_ready.sem, n + 1)
                    nc.scalar.copy(q_t[:, n * 512:(n + 1) * 512], bank[n][0:BOTTLE, :]).then_inc(sig.q_done.sem, 1)
                act.wait_ge(sig.k_ready.sem, 1)
                nc.scalar.copy(rk_t[:], bank[6][0:ROUTE, 0:SLOTS]).then_inc(sig.k_done.sem, 1)
                nc.scalar.copy(down[:], bank[6][0:VALUE, SLOTS:2 * SLOTS]).then_inc(sig.k_done.sem, 1)
                for n in range(2):
                    act.wait_ge(sig.rq_ready.sem, n + 1)
                    nc.scalar.copy(rq_t[:, n * 512:(n + 1) * 512], bank[4 + n][0:ROUTE, :]).then_inc(
                        sig.rq_done.sem, 1)
                act.wait_ge(sig.v_ready.sem, 1)
                nc.scalar.copy(slot_values[:], bank[7][:, :]).then_inc(sig.v_done.sem, 1)
                act.wait_ge(sig.small_in.sem, loads)
                for n in range(2):
                    part = slice(n * 512, (n + 1) * 512)
                    act.wait_ge(sig.hidden_ready.sem, n + 1)
                    nc.scalar.activation(y[:, part], bank[2 + n][:, :], ACT.Identity, bias=cols[:, 0:1])
                    nc.scalar.activation(inner[:, part], bank[2 + n][:, :], ACT.Square,
                                         bias=cols[:, 0:1]).then_inc(sig.y_squared.sem, 1)
                for n in range(2):
                    part = slice(n * 512, (n + 1) * 512)
                    act.wait_ge(sig.inner_done.sem, n + 1)
                    nc.scalar.activation(th[:, part], inner[:, part], ACT.Tanh, scale=GELU_SCALE).then_inc(
                        sig.tanh_done.sem, 1)
                act.wait_ge(sig.x_read.sem, 1)
                nc.scalar.activation(log_var[:], log_var[:], ACT.Ln).then_inc(sig.log_done.sem, 1)
                for n in range(groups):
                    act.wait_ge(sig.shifted.sem, sig.shifted.at(n + 1))
                    for tt in range(four):
                        t = n * four + tt
                        nc.scalar.activation(probs[:, n, tt, :], probs[:, n, tt, :], ACT.Exp,
                                             accum_out=total[:, t:t + 1]).then_inc(sig.exp_done.sem, 1)
                    act.wait_ge(sig.logistic_in.sem, n + 1)
                    nc.scalar.activation(gate[:], gate[:], ACT.Tanh, scale=0.5).then_inc(sig.logistic.sem, 1)
                    act.wait_ge(sig.pt_ready.sem, n + 1)
                    nc.scalar.copy(p_t[:, n, :], bank[2 + n][:, :]).then_inc(sig.pt_done.sem, 1)
                if not last:
                    norm_scalar(nc, act, g)

            @block.vector
            def _(dve):
                steps = Steps(sig.dve_step)

                def settle():
                    dve.wait_ge(sig.dve_step.sem, steps.so_far())

                nc.vector.memset(ones[:], 1.0)
                for t in range(TILES):
                    nc.vector.bn_stats(stats[:, t, :], x[:, t, :]).then_inc(steps.count(), 1)
                settle()
                for t in range(TILES):
                    nc.vector.bn_aggr(mv[:, t, :], stats[:, t, :]).then_inc(steps.count(), 1)
                settle()
                nc.vector.tensor_scalar(log_var[:], mv[:, :, 1], 1.0, None, ALU.add).then_inc(sig.x_read.sem, 1)
                for n in range(2):
                    part = slice(n * 512, (n + 1) * 512)
                    dve.wait_ge(sig.tanh_done.sem, n + 1)
                    nc.vector.scalar_tensor_tensor(y[:, part], th[:, part], 1.0, y[:, part], ALU.add,
                                                   ALU.mult).then_inc(sig.gelu_done.sem, 1)
                dve.wait_ge(sig.log_done.sem, 1)
                nc.vector.tensor_reduce(log_sum[:], log_var[:], AX.X, ALU.add).then_inc(sig.log_summed.sem, 1)
                dve.wait_ge(sig.small_in.sem, loads)

                def choose(n):
                    dve.wait_ge(sig.s_ready.sem, n + 1)
                    rel = over(log_rel[:], (1, four))
                    nc.vector.scalar_tensor_tensor(route[:], bank[n][:, :].rearrange("p (t k) -> p t k", t=four),
                                                   ROUTE ** -0.5, rel, ALU.mult, ALU.add).then_inc(steps.count(), 1)
                    nc.vector.scalar_tensor_tensor(scores[:],
                                                   bank[4 + n][:, :].rearrange("p (t k) -> p t k", t=four),
                                                   BOTTLE ** -0.5, rel, ALU.mult, ALU.add).then_inc(steps.count(), 1)
                    settle()
                    for tt in range(four):
                        nc.vector.max(top[:, tt, :], route[:, tt, :]).then_inc(steps.count(), 1)
                    settle()
                    for tt in range(four):
                        nc.vector.match_replace(rest[:, tt, :], top[:, tt, :], route[:, tt, :], NEG).then_inc(
                            steps.count(), 1)
                    settle()
                    nc.vector.tensor_tensor(rest[:], rest[:], route[:], ALU.is_equal).then_inc(steps.count(), 1)
                    settle()
                    nc.vector.scalar_tensor_tensor(scores[:], rest[:], NEG, scores[:], ALU.mult,
                                                   ALU.add).then_inc(steps.count(), 1)
                    settle()
                    nc.vector.tensor_reduce(mx[:], scores[:], AX.X, ALU.max).then_inc(steps.count(), 1)
                    settle()
                    nc.vector.tensor_tensor(probs[:, n, :, :], scores[:], over(mx[:], (2, SLOTS)),
                                            ALU.subtract).then_inc(sig.shifted.sem, 1)

                def logistic(n):
                    dve.wait_ge(sig.logistic.sem, n + 1)
                    nc.vector.tensor_scalar(gate[:], gate[:], 1.0, 0.5, ALU.add, ALU.mult).then_inc(
                        steps.count(), 1)
                    settle()

                choose(0)
                dve.wait_ge(sig.learned_ready.sem, 1)
                nc.vector.tensor_scalar(mean[:], bank[6][:, TILES:TILES + 1], 1.0 / TOKENS, 1e-6, ALU.mult,
                                        ALU.add).then_inc(steps.count(), 1)
                nc.vector.tensor_scalar(gate[:], bank[6][:, 0:TILES], 0.5, cols[:, 2:3], ALU.mult,
                                        ALU.add).then_inc(sig.logistic_in.sem, 1)
                settle()
                nc.vector.reciprocal(mean[:], mean[:]).then_inc(steps.count(), 1)
                settle()
                nc.vector.tensor_scalar(u[:], log_var[:], mean[:, 0:1], 0.5, ALU.mult, ALU.mult).then_inc(
                    steps.count(), 1)
                settle()
                choose(1)
                logistic(0)
                nc.vector.scalar_tensor_tensor(u[:], gate[:], 2.5, u[:], ALU.mult, ALU.add).then_inc(
                    steps.count(), 1)
                settle()
                nc.vector.tensor_scalar(u[:], u[:], 0.0, 5.0, ALU.max, ALU.min).then_inc(steps.count(), 1)
                settle()
                nc.vector.tensor_scalar(u[:], u[:], TAU_LOW, 1.0 / (TAU_HIGH - TAU_LOW), ALU.subtract,
                                        ALU.mult).then_inc(steps.count(), 1)
                settle()
                nc.vector.tensor_scalar(u[:], u[:], 0.0, 1.0, ALU.max, ALU.min).then_inc(steps.count(), 1)
                settle()
                nc.vector.tensor_scalar(gate[:], u[:], cols[:, 3:4], cols[:, 4:5], ALU.mult, ALU.add).then_inc(
                    sig.logistic_in.sem, 1)
                logistic(1)
                nc.vector.scalar_tensor_tensor(gate[:], gate[:], EARLY_EXIT, gate[:], ALU.is_ge,
                                               ALU.mult).then_inc(steps.count(), 1)
                dve.wait_ge(sig.exp_done.sem, TILES)
                nc.vector.reciprocal(total[:], total[:]).then_inc(steps.count(), 1)
                settle()
                nc.vector.tensor_tensor(gate[:], gate[:], total[:], ALU.mult).then_inc(steps.count(), 1)
                settle()
                dve.wait_ge(sig.prepared.sem, 1)
                for t in range(TILES):
                    dve.wait_ge(sig.y_ready.sem, t + 1)
                    nc.vector.scalar_tensor_tensor(x[:, t, :], out_banks[t % 3][:, :], gate[:, t:t + 1], x[:, t, :],
                                                   ALU.mult, ALU.add).then_inc(sig.added.sem, 1)
                dve.wait_ge(sig.added.sem, sig.added.at(TILES))
                norm_vector(nc, dve, g)



MIX, MIX_RANK, MIX_KEY = 8, 64, 128


def mixed_ffn(nc, g, name, last):
    sig, feat, x, bank = g.sig, g.feat, g.x, g.bank
    pairs = MIX * MIX_RANK // P
    half_b = BATCH // 2
    wcols = 2 * DIM + MIX_KEY
    with ExitStack() as ctx:
        def sb(what, shape, dt=F32):
            return ctx.enter_context(nc.sbuf_tensor(f"{name}_{what}", shape, dt))
        w = sb("w", [P, CH, wcols])
        up = sb("up", [P, pairs, DIM])
        keys = sb("keys", [MIX_KEY, MIX])
        sums = sb("sums", [P, CH, BATCH])
        q_t = sb("q_t", [MIX_KEY, BATCH])
        coef = sb("coef", [BATCH, MIX])
        spread = sb("spread", [BATCH, MIX, MIX_RANK])
        stat = sb("stat", [BATCH, 2])
        rows = sb("rows", [P, pairs, BATCH])
        h_t = sb("h_t", [P, pairs, TOKENS])
        loads = 16 * 3
        down_at, q_at = DIM, 2 * DIM
        y_banks = (bank[4], bank[5], bank[6])

        with nc.Block() as block:
            @block.sync
            def _(sp):
                sp.dma_start(w[:].rearrange("p c n -> p (c n)"), g.t[name + "_w"]).then_inc(sig.small_in.sem, 16)
                sp.dma_start(up[:].rearrange("p j n -> p (j n)"), g.t[name + "_up"]).then_inc(sig.small_in.sem, 16)
                sp.dma_start(keys[:], g.t[name + "_keys"]).then_inc(sig.small_in.sem, 16)
                if last:
                    norm_sync(nc, sp, g)

            @block.gpsimd
            def _(pool):
                norm_pool(nc, pool, g)

            @block.tensor
            def _(pe):
                def down(u):
                    half, j = u // pairs, u % pairs
                    if u >= 4:
                        pe.wait_ge(sig.h_done.sem, u - 3)
                    for c in range(CH):
                        mm = nc.tensor.matmul(
                            bank[u % 4][:, :], w[:, c, down_at + j * P:down_at + (j + 1) * P],
                            feat[:, SELF, c, half * half_b:(half + 1) * half_b, :].rearrange("p b s -> p (b s)"),
                            start=(c == 0), stop=(c == CH - 1))
                    mm.then_inc(sig.h_ready.sem, 1)

                def base(t):
                    if t >= 3:
                        pe.wait_ge(sig.added.sem, sig.added.at(t - 2))
                    for c in range(CH):
                        nc.tensor.matmul(y_banks[t % 3][:, :],
                                         feat[:, SELF, c, 2 * t:2 * t + 2, :].rearrange("p b s -> p (b s)"),
                                         w[:, c, 0:DIM], start=(c == 0), stop=False)

                def mix(t):
                    if t % 4 == 0:
                        pe.wait_ge(sig.h_done.sem, pairs * (t // 4 + 1))
                    for j in range(pairs):
                        mm = nc.tensor.matmul(y_banks[t % 3][:, :], h_t[:, j, t * P:(t + 1) * P], up[:, j, :],
                                              start=False, stop=(j == pairs - 1))
                    mm.then_inc(sig.y_ready.sem, 1)

                pe.wait_ge(sig.small_in.sem, loads)
                down(0)
                down(1)
                pe.wait_ge(sig.sums_done.sem, 1)
                for c in range(CH):
                    mm = nc.tensor.matmul(bank[7][:, 0:BATCH], w[:, c, q_at:q_at + MIX_KEY], sums[:, c, :],
                                          start=(c == 0), stop=(c == CH - 1))
                mm.then_inc(sig.q_ready.sem, 1)
                down(2)
                pe.wait_ge(sig.q_done.sem, sig.q_done.at(1))
                nc.tensor.matmul(bank[7][0:BATCH, BATCH:BATCH + MIX], q_t[:], keys[:], start=True,
                                 stop=True).then_inc(sig.s_ready.sem, 1)
                down(3)
                base(0)
                pe.wait_ge(sig.coef_done.sem, 1)
                for j in range(pairs):
                    mm = nc.tensor.matmul(bank[7][:, (2 + j) * BATCH:(3 + j) * BATCH],
                                          spread[:, 2 * j:2 * j + 2, :].rearrange("b e r -> b (e r)"),
                                          g.ident[0:BATCH, 0:BATCH], start=True, stop=True)
                mm.then_inc(sig.rows_ready.sem, 1)
                base(1)
                base(2)
                mix(0)
                for u in range(4, 8):
                    down(u)
                mix(1)
                mix(2)
                for t in range(3, TILES):
                    base(t)
                    mix(t)
                if not last:
                    norm_tensor(nc, pe, g)

            @block.scalar
            def _(act):
                act.wait_ge(sig.q_ready.sem, 1)
                nc.scalar.mul(q_t[:], bank[7][:, 0:BATCH], 1.0 / SEQ).then_inc(sig.q_done.sem, 1)
                act.wait_ge(sig.shifted.sem, sig.shifted.at(1))
                nc.scalar.activation(coef[:], coef[:], ACT.Exp, scale=MIX_KEY ** -0.5,
                                     accum_out=stat[:, 1:2]).then_inc(sig.exp_done.sem, 1)
                if not last:
                    norm_scalar(nc, act, g)

            @block.vector
            def _(dve):
                steps = Steps(sig.dve_step)
                nc.vector.tensor_reduce(sums[:], feat[:, SELF, :, :, :], AX.X, ALU.add).then_inc(
                    sig.sums_done.sem, 1)
                dve.wait_ge(sig.s_ready.sem, 1)
                raw = bank[7][0:BATCH, BATCH:BATCH + MIX]
                nc.vector.tensor_reduce(stat[:, 0:1], raw, AX.X, ALU.max).then_inc(steps.count(), 1)
                dve.wait_ge(sig.dve_step.sem, steps.so_far())
                nc.vector.tensor_scalar(coef[:], raw, stat[:, 0:1], None, ALU.subtract).then_inc(
                    sig.shifted.sem, 1)
                dve.wait_ge(sig.exp_done.sem, 1)
                nc.vector.reciprocal(stat[:, 1:2], stat[:, 1:2]).then_inc(steps.count(), 1)
                dve.wait_ge(sig.dve_step.sem, steps.so_far())
                nc.vector.tensor_scalar(spread[:], over(coef[:], (2, MIX_RANK)), stat[:, 1:2], None,
                                        ALU.mult).then_inc(sig.coef_done.sem, 1)
                dve.wait_ge(sig.rows_ready.sem, 1)
                nc.vector.tensor_copy(rows[:], bank[7][:, 2 * BATCH:(2 + pairs) * BATCH].rearrange(
                    "p (j b) -> p j b", b=BATCH)).then_inc(steps.count(), 1)
                dve.wait_ge(sig.dve_step.sem, steps.so_far())

                def scale(u):
                    half, j = u // pairs, u % pairs
                    dve.wait_ge(sig.h_ready.sem, u + 1)
                    nc.vector.tensor_tensor(
                        h_t[:, j, half * 512:(half + 1) * 512].rearrange("p (b s) -> p b s", s=SEQ),
                        bank[u % 4][:, :].rearrange("p (b s) -> p b s", s=SEQ),
                        over(rows[:, j, half * half_b:(half + 1) * half_b], (2, SEQ)), ALU.mult).then_inc(
                        sig.h_done.sem, 1)

                def add(t):
                    dve.wait_ge(sig.y_ready.sem, t + 1)
                    nc.vector.tensor_tensor(x[:, t, :], x[:, t, :], y_banks[t % 3][:, :], ALU.add).then_inc(
                        sig.added.sem, 1)

                for u in range(4):
                    scale(u)
                add(0)
                for u in range(4, 8):
                    scale(u)
                for t in range(1, TILES):
                    add(t)
                dve.wait_ge(sig.added.sem, sig.added.at(TILES))
                norm_vector(nc, dve, g)



def build(nc, t, out):
    with ExitStack() as ctx:
        g = Record()
        g.out, g.t = out, t
        g.x = ctx.enter_context(nc.sbuf_tensor("x", [P, TILES, DIM], F32))
        g.feat = ctx.enter_context(nc.sbuf_tensor("feat", [P, 2, CH, BATCH, SEQ], F32))
        g.ident = ctx.enter_context(nc.sbuf_tensor("ident", [P, P], F32))
        g.norm = norm_buffers(nc, ctx)
        g.minus_half = ctx.enter_context(nc.sbuf_tensor("minus_half", [P, TILES], F32))
        g.bank = [ctx.enter_context(nc.psum_tensor(f"bank{n}", [P, 512], F32)) for n in range(8)]
        g.out_written = Signal(ctx.enter_context(nc.semaphore("out_written")), 0)
        loaded = ctx.enter_context(nc.semaphore("loaded"))
        g.sig = Signals(nc, ctx)
        numbers = sorted(sem.num for sem in g.sig.all)
        assert numbers == list(range(numbers[0], numbers[-1] + 1))

        with nc.Block() as block:
            @block.sync
            def _(sp):
                for tile in range(TILES):
                    sp.dma_start(g.x[:, tile, :], t["x"][tile]).then_inc(loaded, 16)
                sp.dma_start(g.feat[:, :, :, :, :].rearrange("p k c b s -> p (k c b s)"), t["feat"]).then_inc(loaded, 16)
                sp.dma_start(g.ident[:], t["ident"]).then_inc(loaded, 16)
                sp.wait_ge(loaded, 16 * (TILES + 2))

            @block.vector
            def _(dve):
                nc.vector.memset(g.minus_half[:], -0.5)

        narrow, wide = ND ** -0.5, HD ** -0.5
        stages = [
            lambda last: wide_attention(nc, g, "l0a", last, t["l0a_qo"], t["l0a_kv"], 1, SELF, wide,
                                        bias=t["l0a_bias"]),
            lambda last: narrow_attention(nc, g, "l0x", last, t["l0x_w"], CTX, narrow),
            lambda last: routed_ffn(nc, g, "l0f", last, t["l0f_w"], t["l0f_up"], 4, 8, 1, 1.0,
                                    expert_bias=t["l0f_bias"]),

            lambda last: unlike_attention(nc, g, "l1a", last, t["l1a_eta"]),
            lambda last: wide_attention(nc, g, "l1x", last, t["l1x_qo"], t["l1x_kv"], 1, "both", wide),
            lambda last: routed_ffn(nc, g, "l1f", last, t["l1f_w"], t["l1f_up"], 8, 16, 2, 2.0,
                                    out_bias=t["l1f_bias"]),

            lambda last: narrow_attention(nc, g, "l2a", last, t["l2a_w"], SELF, narrow, rope=t["l2a_consts"],
                                          out_proj=False),
            lambda last: wide_attention(nc, g, "l2x", last, t["l2x_qo"], t["l2x_kv"], 1, CTX, wide,
                                        mask=t["l2x_mask"], q_norm=t["l2x_qn"], k_norm=t["l2x_kn"]),
            lambda last: memory_ffn(nc, g, "l2f", last),

            lambda last: narrow_attention(nc, g, "l3a", last, t["l3a_w"], SELF, narrow, bias=t["l3a_bias"]),
            lambda last: wide_attention(nc, g, "l3x", last, t["l3x_qo"], t["l3x_kv"], GH, CTX, wide,
                                        bias=t["l3x_bias"], key_mask=t["l3x_mask"]),
            lambda last: mixed_ffn(nc, g, "l3f", last),
        ]
        for stage in stages:
            clear_signals(nc, g)
            stage(stage is stages[-1])



def wide_inputs(arrays, name, wq, wk, wv, wo, kv_heads):
    q = wq.reshape(CH, P, GROUPS, GH * HD).transpose(2, 1, 0, 3).reshape(GROUPS, P, -1)
    o = wo.reshape(GROUPS, GH, HD, DIM).transpose(0, 2, 1, 3).reshape(GROUPS, P, -1)
    arrays[name + "_qo"] = np.concatenate([q, o], axis=2)
    n = wk.shape[1] // (kv_heads * HD)
    kv = [w.reshape(CH, P, n, kv_heads * HD).transpose(2, 1, 0, 3).reshape(n, P, -1) for w in (wk, wv)]
    arrays[name + "_kv"] = np.concatenate(kv, axis=2)


def distance_bias():
    slopes = (2.0 ** (-8.0 / HEADS)) ** np.arange(1, HEADS + 1, dtype=np.float32)
    rel = np.arange(SEQ)[:, None] - np.arange(SEQ)[None, :]
    b = -slopes[:, None, None].astype(np.float32) * np.sqrt(np.maximum(rel, 0).astype(np.float32))
    b = np.where(rel[None] >= 0, b, NEG).astype(np.float32)
    b = b.reshape(GROUPS, 2, 2, SEQ, SEQ).transpose(0, 2, 3, 1, 4)
    b = np.repeat(b[:, :, :, :, None, :], 2, axis=4)
    return np.ascontiguousarray(b.reshape(GROUPS, P, 2 * 2 * SEQ), dtype=np.float32)


def narrow_inputs(wq, wk, wv, wo):
    q = wq.reshape(CH, P, KV, NR, ND).transpose(1, 0, 3, 2, 4).reshape(P, -1)
    kv = [m.reshape(CH, P, P).transpose(1, 0, 2).reshape(P, -1) for m in (wk, wv)]
    parts = [q] + kv
    if wo is not None:
        parts.append(wo.reshape(KV, NR, ND, DIM).transpose(0, 2, 1, 3).reshape(P, -1))
    return np.concatenate(parts, axis=1)


def linear_bias():
    slopes = (2.0 ** (-2.0 ** (-(math.log2(HEADS) - 3)))) ** np.arange(1, HEADS + 1, dtype=np.float64)
    rel = (np.arange(SEQ)[None, :] - np.arange(SEQ)[:, None]).astype(np.float32)
    b = slopes.astype(np.float32)[:, None, None] * rel[None]
    b = np.where(rel[None] <= 0, b, np.float32(NEG)).astype(np.float32)
    b = b.reshape(KV, NR, SEQ, SEQ).transpose(2, 1, 0, 3).reshape(SEQ, -1)
    return np.concatenate([b, b], axis=0)


def rope_tables():
    half = ND // 2
    turn = np.zeros((P, P), np.float32)
    for h in range(KV):
        for d in range(half):
            turn[h * ND + half + d, h * ND + d] = -1.0
            turn[h * ND + d, h * ND + half + d] = 1.0
    inv = (1.0 / 10000.0 ** (np.arange(0, ND, 2, dtype=np.float32) / ND)).astype(np.float32)
    ang = np.arange(SEQ, dtype=np.float32)[None, :] * inv[:, None]
    ang = np.tile(np.concatenate([ang, ang], axis=0), (KV, 1))
    return turn, np.cos(ang).astype(np.float32), np.sin(ang).astype(np.float32)


def chunked(*parts):
    m = np.concatenate(parts, axis=1)
    return m.reshape(CH, P, m.shape[1]).transpose(1, 0, 2).reshape(P, -1)


def ffn_inputs(a, i):
    def rows(v, n=P):
        return np.broadcast_to(v.reshape(1, -1), (n, v.size))
    for e in (4, 8):
        a["before%d" % e] = rows(np.tril(np.ones((e, e), np.float32), -1))
    a["l0f_w"] = chunked(i["L0_ffn_W_up"].T, i["L0_ffn_gate_w"].T, i["L0_ffn_lora_A"].reshape(-1, DIM).T)
    a["l0f_up"] = i["L0_ffn_lora_B"].transpose(0, 2, 1).reshape(-1, DIM)
    a["l0f_bias"] = rows(i["L0_ffn_expert_bias"])
    a["l1a_eta"] = rows(i["L1_attn_eta"])
    a["l1f_w"] = chunked(i["L1_ffn_W_base"].T, i["L1_ffn_W_router"].T, i["L1_ffn_A"].reshape(-1, DIM).T)
    a["l1f_up"] = i["L1_ffn_B"].transpose(0, 2, 1).reshape(-1, DIM)
    a["l1f_bias"] = rows(i["L1_ffn_b_base"])
    a["l2f_w"] = chunked(i["L2_ffn_Wq"].T, i["L2_ffn_Wu1"].T, i["L2_ffn_Wvd"].T, i["L2_ffn_aux_values"].T)
    a["l2f_small"] = np.concatenate([i["L2_ffn_Wr"].T, i["L2_ffn_aux_keys"].T], axis=1)
    a["l2f_w_vu"] = i["L2_ffn_Wvu"].T
    a["l2f_log_rel"] = rows(i["L2_ffn_log_rel"])
    a["l2f_cols"] = np.concatenate([i["L2_ffn_bu1"].reshape(P, 1), i["L2_ffn_Wu2"].reshape(P, 1)] +
                                   [rows(i["L2_ffn_" + n]) for n in ("bu2", "gate_w1", "gate_bias")], axis=1)
    down = i["L3_ffn_lora_down"].transpose(1, 0, 2).reshape(DIM, -1)
    a["l3f_w"] = chunked(i["L3_ffn_W_org"].T, down, i["L3_ffn_Wq"].T)
    a["l3f_up"] = chunked(i["L3_ffn_lora_up"].reshape(-1, DIM))
    a["l3f_keys"] = i["L3_ffn_lora_keys"].T


def lay_out(i):
    i = {k: np.asarray(v) for k, v in i.items()}
    a = {}
    x = i["x"].reshape(TOKENS, DIM)
    a["x"] = x.reshape(TILES, P, DIM)
    feats = [f.reshape(BATCH, SEQ, CH, P).transpose(3, 2, 0, 1) for f in (i["ctx_4096"], i["x"])]
    a["feat"] = np.stack(feats, axis=1).reshape(P, -1)
    a["ident"] = np.eye(P, dtype=np.float32)
    w = i["L0_attn_w_qkv"]
    wide_inputs(a, "l0a", w[:, :HEADS * HD], w[:, HEADS * HD:HEADS * HD + GROUPS * HD],
                w[:, HEADS * HD + GROUPS * HD:], i["L0_attn_w_o"], 1)
    a["l0a_bias"] = distance_bias()
    wide_inputs(a, "l1x", i["L1_xattn_Wq"], i["L1_xattn_Wk"], i["L1_xattn_Wv"], i["L1_xattn_Wo"], 1)
    wide_inputs(a, "l2x", i["L2_xattn_q_proj_w"].T, i["L2_xattn_k_proj_w"].T, i["L2_xattn_v_proj_w"].T,
                i["L2_xattn_o_proj_w"].T, 1)
    a["l2x_mask"] = i["mask_1x1xSxS2_ff0"].reshape(SEQ, SEQ)
    a["l2x_qn"] = i["L2_xattn_q_norm_w"].reshape(P, 1)
    a["l2x_kn"] = i["L2_xattn_k_norm_w"].reshape(P, 1)
    wide_inputs(a, "l3x", i["L3_xattn_Wq"], i["L3_xattn_Wk"], i["L3_xattn_Wv"], i["L3_xattn_Wo"], GH)
    b = i["fside_Bx32xSxS2_0"].reshape(UNITS, 2, 2, GROUPS, 2, 2, SEQ, SEQ)
    a["l3x_bias"] = b.transpose(3, 5, 6, 0, 1, 4, 2, 7).reshape(GROUPS, P, -1)
    m = i["mask_BxSxS2_bk0"].transpose(1, 0, 2)
    a["l3x_mask"] = np.concatenate([m, m], axis=0)
    a["head_of"] = np.repeat(np.eye(KV, dtype=np.float32), ND, axis=0)
    a["half_of"] = np.repeat(np.eye(2, dtype=np.float32), SEQ, axis=0)
    a["l0x_w"] = narrow_inputs(i["L0_xattn_Wq"], i["L0_xattn_Wk"], i["L0_xattn_Wv"], i["L0_xattn_Wo"])
    a["l2a_w"] = narrow_inputs(i["L2_attn_wq"], i["L2_attn_wk"], i["L2_attn_wv"], None)
    turn, cos, sin = rope_tables()
    bq = i["L2_attn_bq"].reshape(KV, NR, ND).transpose(0, 2, 1).reshape(P, NR)
    bv = np.broadcast_to(i["L2_attn_bv"].reshape(1, P), (P, P))
    a["l2a_consts"] = np.concatenate([turn, cos, sin, bq, i["L2_attn_bk"].reshape(P, 1), bv], axis=1)
    w = i["L3_attn_Wqkv"]
    wk, wv = (np.tile(w[:, DIM + n * ND:DIM + (n + 1) * ND], (1, KV)) for n in range(2))
    a["l3a_w"] = narrow_inputs(w[:, :DIM], wk, wv, i["L3_attn_Wo"])
    a["l3a_bias"] = linear_bias()
    ffn_inputs(a, i)
    return {k: np.ascontiguousarray(v) for k, v in a.items()}


def kernel(**inputs):
    import concourse.bacc as bacc
    from concourse.bass_utils import run_bass_kernel_spmd

    arrays = lay_out(inputs)
    nc = bacc.Bacc("TRN2", target_bir_lowering=False, num_devices=1)
    t = {k: nc.dram_tensor("in_" + k, v.shape, mybir.dt.from_np(v.dtype), kind="ExternalInput").ap()
         for k, v in arrays.items()}
    out = nc.dram_tensor("out_0_dram", (TOKENS, DIM), F32, kind="ExternalOutput").ap()
    build(nc, t, out)
    r = run_bass_kernel_spmd(nc, [{"in_" + k: v for k, v in arrays.items()}], core_ids=[0])
    return r.results[0]["out_0_dram"].reshape(BATCH, SEQ, DIM)
```

```python
from contextlib import ExitStack
import math

import numpy as np

import concourse.bass as bass
from concourse import mybir

F32 = mybir.dt.float32
F32R = mybir.dt.float32r
U8 = mybir.dt.uint8
ALU = mybir.AluOpType
ACT = mybir.ActivationFunctionType
AX = mybir.AxisListType

P = 128
BATCH, SEQ, DIM = 16, 64, 512
TOKENS = BATCH * SEQ
CH = DIM // P
TILES = TOKENS // P
HEADS = 32
HD = 128
ND = DIM // HEADS
GH = 4
GROUPS = HEADS // GH
UB = 4
UNITS = BATCH // UB
BODY = 2 * UNITS
UT = UB * SEQ
KV = 8
NR = HEADS // KV
NEG = -1.0e30
LN_EPS = 1e-5
HIGH, LOW = 0, 1
CTX, SELF = 0, 1
CREDIT = 8


class Record:
    pass


class Signal:

    def __init__(self, sem, begin):
        self.sem, self.begin = sem, begin

    def at(self, n):
        return self.begin + n


class Signals:

    def __init__(self, nc, ctx):
        self.all, self.credited = [], []

        def plain(name):
            self.all.append(ctx.enter_context(nc.semaphore(name)))
            return Signal(self.all[-1], 0)

        def released(name):
            sig = plain(name)
            self.credited.append(sig.sem)
            return Signal(sig.sem, CREDIT)

        self.q_done = released("q_done")
        self.k_done = released("k_done")
        self.v_done = released("v_done")
        self.s_read = released("s_read")
        self.shifted = released("shifted")
        self.pt_done = released("pt_done")
        self.o_done = released("o_done")
        self.added = released("added")
        self.staged = released("staged")
        self.kd_done = released("kd_done")
        self.keys_taken = released("keys_taken")
        self.squared = released("squared")
        self.attn_taken = released("attn_taken")
        self.wide_a = plain("wide_a")
        self.wide_b = plain("wide_b")
        self.qo_in = plain("qo_in")
        self.wq_high = plain("wq_high")
        self.wo_high = plain("wo_high")
        self.q_split = plain("q_split")
        self.o_split = plain("o_split")
        self.own_high = plain("own_high")
        self.own_low = plain("own_low")
        self.o_high = plain("o_high")
        self.kv_in = plain("kv_in")
        self.small_in = plain("small_in")
        self.q_ready = plain("q_ready")
        self.k_ready = plain("k_ready")
        self.v_ready = plain("v_ready")
        self.s_ready = plain("s_ready")
        self.exp_done = plain("exp_done")
        self.p_ready = plain("p_ready")
        self.pt_ready = plain("pt_ready")
        self.o_ready = plain("o_ready")
        self.y_ready = plain("y_ready")
        self.dve_step = plain("dve_step")
        self.row_max = plain("row_max")
        self.row_sum = plain("row_sum")
        self.rope_step = plain("rope_step")
        self.act_step = plain("act_step")
        self.pool_step = plain("pool_step")
        self.rms_done = plain("rms_done")
        self.rms_sum = plain("rms_sum")
        self.rms_var = plain("rms_var")
        self.rms_power = plain("rms_power")
        self.norm_step = plain("norm_step")
        self.var_ready = plain("var_ready")
        self.rstd_ready = plain("rstd_ready")
        self.normed = plain("normed")
        self.turned = plain("turned")
        self.turn_read = plain("turn_read")
        self.keys_turned = plain("keys_turned")
        self.rotated = plain("rotated")
        self.attn_turned = plain("attn_turned")
        self.prepared = plain("prepared")
        self.logits_ready = plain("logits_ready")
        self.z_ready = plain("z_ready")
        self.z_weighted = plain("z_weighted")
        self.z_turning = plain("z_turning")
        self.z_turned = plain("z_turned")
        self.zeroed = plain("zeroed")
        self.least = plain("least")
        self.y_squared = plain("y_squared")
        self.inner_done = plain("inner_done")
        self.tanh_done = plain("tanh_done")
        self.gelu_done = plain("gelu_done")
        self.x_read = plain("x_read")
        self.log_done = plain("log_done")
        self.log_summed = plain("log_summed")
        self.rq_ready = plain("rq_ready")
        self.rq_done = plain("rq_done")
        self.hidden_ready = plain("hidden_ready")
        self.learned_ready = plain("learned_ready")
        self.logistic_in = plain("logistic_in")
        self.logistic = plain("logistic")
        self.h_ready = plain("h_ready")
        self.h_done = plain("h_done")
        self.sums_done = plain("sums_done")
        self.coef_done = plain("coef_done")
        self.rows_ready = plain("rows_ready")


class Steps:

    def __init__(self, signal, before=0):
        self.of, self.before, self.n = signal, before, 0

    def count(self):
        self.n += 1
        return self.of.sem

    def so_far(self):
        return self.of.at(self.before + self.n)


def over(ap, *dims):
    for axis, size in dims:
        ap = ap.unsqueeze(axis)
        shape = list(ap.shape)
        shape[axis] = size
        ap = ap.to_broadcast(shape)
    return ap


def clear_signals(nc, g):
    with nc.Block() as block:
        @block.sync
        def _(sp):
            numbers = sorted(sem.num for sem in g.sig.all)
            sp.sem_clear(range(numbers[0], numbers[-1] + 1))
            for sem in g.sig.credited:
                sp.sem_inc(sem, CREDIT)



def norm_buffers(nc, ctx):
    norm = Record()
    norm.stats = ctx.enter_context(nc.sbuf_tensor("ln_stats", [P, TILES, 6], F32))
    norm.mv = ctx.enter_context(nc.sbuf_tensor("ln_mean_var", [P, TILES, 2], F32))
    norm.var = ctx.enter_context(nc.sbuf_tensor("ln_var", [P, TILES], F32))
    norm.rstd = ctx.enter_context(nc.sbuf_tensor("ln_rstd", [P, TILES], F32))
    return norm


def norm_vector(nc, dve, g):
    n, steps = g.norm, Steps(g.sig.norm_step)
    for t in range(TILES):
        nc.vector.bn_stats(n.stats[:, t, :], g.x[:, t, :]).then_inc(steps.count(), 1)
    dve.wait_ge(g.sig.norm_step.sem, steps.so_far())
    for t in range(TILES):
        nc.vector.bn_aggr(n.mv[:, t, :], n.stats[:, t, :]).then_inc(steps.count(), 1)
    dve.wait_ge(g.sig.norm_step.sem, steps.so_far())
    nc.vector.tensor_scalar(n.var[:], n.mv[:, :, 1], LN_EPS, None, ALU.add).then_inc(g.sig.var_ready.sem, 1)
    dve.wait_ge(g.sig.rstd_ready.sem, g.sig.rstd_ready.at(1))
    for t in range(TILES):
        nc.vector.tensor_scalar(g.x[:, t, :], g.x[:, t, :], n.mv[:, t, 0:1], n.rstd[:, t:t + 1],
                                ALU.subtract, ALU.mult).then_inc(g.sig.normed.sem, 1)


def norm_pool(nc, pool, g):
    pool.wait_ge(g.sig.var_ready.sem, g.sig.var_ready.at(1))
    nc.gpsimd.tensor_tensor(g.norm.rstd[:], g.norm.var[:], g.minus_half[:, 0:TILES], ALU.pow).then_inc(
        g.sig.rstd_ready.sem, 1)


def norm_tensor(nc, pe, g):
    for t in range(TILES):
        pe.wait_ge(g.sig.normed.sem, g.sig.normed.at(t + 1))
        if t >= 2:
            pe.wait_ge(g.sig.turn_read.sem, g.sig.turn_read.at(t - 1))
        bank = g.bank[t % 2]
        for c in range(CH):
            last = nc.tensor.transpose(bank[:, c * P:(c + 1) * P], g.x[:, t, c * P:(c + 1) * P], g.ident[:])
        last.then_inc(g.sig.turned.sem, 1)


def norm_scalar(nc, act, g):
    for t in range(TILES):
        act.wait_ge(g.sig.turned.sem, g.sig.turned.at(t + 1))
        src = g.bank[t % 2][:, :].rearrange("p (c b s) -> p c b s", c=CH, b=2)
        nc.scalar.copy(g.feat[:, SELF, :, 2 * t:2 * t + 2, :], src).then_inc(g.sig.turn_read.sem, 1)


def norm_sync(nc, sp, g):
    for t in range(TILES):
        sp.wait_ge(g.sig.normed.sem, g.sig.normed.at(t + 1))
        sp.dma_start(g.out[t * P:(t + 1) * P, :], g.x[:, t, :]).then_inc(g.out_written.sem, 16)
    sp.wait_ge(g.out_written.sem, 16 * TILES)



def wide_attention(nc, g, name, last, w_qo, w_kv, kv_heads, keys, scale, bias=None, mask=None,
                   q_norm=None, k_norm=None, key_mask=None):
    sig, feat, x, bank = g.sig, g.feat, g.x, g.bank
    both, rms = keys == "both", q_norm is not None
    klen = 2 * SEQ if both else SEQ
    halves = 2 if both else 1
    kbanks = 2 if kv_heads == GH else 1
    kdim = kv_heads * HD
    rounds = GROUPS // 2
    wq_cols = CH * GH * HD
    with ExitStack() as ctx:
        def sb(what, shape, dt=F32):
            return ctx.enter_context(nc.sbuf_tensor(f"{name}_{what}", shape, dt))
        raw = sb("raw", [P, wq_cols])
        wqo = sb("wqo", [P, 2, wq_cols + GH * DIM], F32R)
        own = sb("own", [P, 2, CH, BATCH, SEQ], F32R)
        wkv = sb("wkv", [P, 1 if both else 2, CH * kdim * 2])
        q_t = sb("q_t", [P, GH, UT])
        if both:
            k_t = sb("k_t", [P, UNITS, UB * klen])
            v = sb("v", [P, UNITS, UB, HD])
        else:
            k_t = sb("k_t", [P, kv_heads, UT])
            v = sb("v", [P, 2, 2, kdim])
        shifted = sb("shifted", [P, halves, 512])
        probs = sb("probs", [P, halves, 512])
        p_t = sb("p_t", [P, halves, 512])
        o_t = sb("o_t", [P, 2, GH, UB, SEQ], F32R)
        ngr = 512 // klen
        mx = sb("mx", [P, halves, ngr])
        total = sb("total", [P, halves, ngr])
        recip = sb("recip", [P, halves, ngr])
        if bias is not None:
            bias_cols = bias.shape[2]
            bias_sb = sb("bias", [P, 2, bias_cols])
        if mask is not None:
            mask_sb = sb("mask", [P, SEQ])
        if key_mask is not None:
            km_u8 = probs[:, 0, 0:BATCH * SEQ // 4].bitcast(U8).rearrange("p (b s) -> p b s", b=BATCH)
            km_one = sb("km_one", [P, BATCH, SEQ])
            km_neg = sb("km_neg", [P, BATCH, SEQ])
        if rms:
            q_sq = sb("q_sq", [P, UB, GH, SEQ])
            q_w = sb("q_w", [P, 1])
            k_w = sb("k_w", [P, 1])
            mean_col = sb("mean_col", [P, 1])
            k_rows = sb("k_rows", [P, 2, HD])
            k_junk = sb("k_junk", [P, HD])
            ssq = sb("ssq", [P, 2])
            k_var = sb("k_var", [P, 2])
            k_rstd = sb("k_rstd", [P, 2])
            q_var = sb("q_var", [P, 8])
            q_rstd = sb("q_rstd", [P, 8])

        def landed(n):
            return sig.wide_a if n % 2 == 0 else sig.wide_b
        small_loads = 16 * (2 * (mask is not None) + (key_mask is not None) + 2 * rms)
        score_bank_free = sig.s_read if (bias is not None or rms) else sig.shifted
        before_exp = 2 if (key_mask is not None or rms) else 1
        after_exp = 3 if key_mask is not None else 2
        score_banks = (bank[4], bank[3])
        value_bank = bank[2] if both else bank[3]
        per_group = 16 * ((not both) + (bias is not None))
        parts = ((HIGH, HIGH), (HIGH, LOW), (LOW, HIGH))

        def pipeline(engine, step):
            step((0, 0), None)
            with engine.Fori(0, rounds - 1) as i:
                for n in range(1, BODY):
                    step((i, n), (i, n - 1))
                step((i + 1, 0), (i, BODY - 1))
            for n in range(1, BODY):
                step((rounds - 1, n), (rounds - 1, n - 1))
            step(None, (rounds - 1, BODY - 1))

        def k_round(i, n):
            return UNITS * i + n if both else BODY * i + n

        def o_part(which, b2):
            return o_t[:, which, :, :, :].rearrange("p h (bp b2) s -> p bp b2 h s", b2=2)[:, :, b2, :, :]

        def o_bank(b2):
            return bank[6 + b2][:, :].rearrange("p (bp h s) -> p bp h s", bp=2, h=GH)

        def q_half(j):
            return slice(j * wq_cols // 2, (j + 1) * wq_cols // 2)

        def units_batches(u):
            return slice(UB * u, UB * u + UB)

        with nc.Block() as block:
            @block.sync
            def _(sp):
                if mask is not None:
                    sp.dma_start(mask_sb[0:SEQ, :], mask).then_inc(sig.small_in.sem, 16)
                    sp.dma_start(mask_sb[SEQ:P, :], mask).then_inc(sig.small_in.sem, 16)
                if key_mask is not None:
                    sp.dma_start(km_u8, key_mask).then_inc(sig.small_in.sem, 16)
                if rms:
                    sp.dma_start(q_w[:], q_norm).then_inc(sig.small_in.sem, 16)
                    sp.dma_start(k_w[:], k_norm).then_inc(sig.small_in.sem, 16)

                def load(n, group):
                    if not both:
                        sp.dma_start(wkv[:, n % 2, :], w_kv[group]).then_inc(landed(n).sem, 16)
                    if bias is not None:
                        sp.dma_start(bias_sb[:, n % 2, :], bias[group]).then_inc(landed(n).sem, 16)

                def load_q(group):
                    sp.dma_start(raw[:], w_qo[group][:, 0:wq_cols]).then_inc(sig.qo_in.sem, 16)

                def load_o(group):
                    sp.wait_ge(sig.q_split.sem, sig.q_split.at(2 * group + 2))
                    sp.dma_start(raw[:], w_qo[group][:, wq_cols:2 * wq_cols]).then_inc(sig.qo_in.sem, 16)

                load_q(0)
                if both:
                    sp.dma_start(wkv[:, 0, :], w_kv[0]).then_inc(sig.kv_in.sem, 16)
                for n in range(2):
                    load(n, n)
                load_o(0)
                with sp.Fori(0, rounds - 1) as i:
                    for n in range(2):
                        sp.wait_ge(sig.o_split.sem, sig.o_split.at(2 * i + n + 1))
                        load_q(2 * i + n + 1)
                        if both and n == 0:
                            sp.wait_ge(sig.k_done.sem, sig.k_done.at(UNITS * i + UNITS))
                            sp.wait_ge(sig.v_done.sem, sig.v_done.at(UNITS * i + UNITS))
                            sp.dma_start(wkv[:, 0, :], w_kv[i + 1]).then_inc(sig.kv_in.sem, 16)
                        load_o(2 * i + n + 1)
                        if per_group:
                            sp.wait_ge(sig.y_ready.sem, sig.y_ready.at(2 * (BODY * i + UNITS * (n + 1))))
                            load(n, 2 * i + 2 + n)
                sp.wait_ge(sig.o_split.sem, sig.o_split.at(GROUPS - 1))
                load_q(GROUPS - 1)
                load_o(GROUPS - 1)
                if last:
                    norm_sync(nc, sp, g)

            @block.gpsimd
            def _(pool):
                def split_q_low(i, slot):
                    group = 2 * i + slot
                    for j in range(2):
                        pool.wait_ge(sig.wq_high.sem, sig.wq_high.at(2 * group + j + 1))
                        part = q_half(j)
                        nc.gpsimd.tensor_tensor(wqo[:, LOW, part], raw[:, part], wqo[:, HIGH, part],
                                                ALU.subtract).then_inc(sig.q_split.sem, 1)

                def split_o_low(i, slot):
                    group = 2 * i + slot
                    pool.wait_ge(sig.wo_high.sem, sig.wo_high.at(group + 1))
                    nc.gpsimd.tensor_tensor(wqo[:, LOW, wq_cols:], raw[:], wqo[:, HIGH, wq_cols:],
                                            ALU.subtract).then_inc(sig.o_split.sem, 1)

                def rms_powers(i, n):
                    uu = BODY * i + n
                    pool.wait_ge(sig.rms_var.sem, sig.rms_var.at(2 * uu + 1))
                    nc.gpsimd.tensor_tensor(k_rstd[:], k_var[:], g.minus_half[:, 0:2], ALU.pow).then_inc(
                        sig.rms_power.sem, 1)
                    pool.wait_ge(sig.rms_var.sem, sig.rms_var.at(2 * uu + 2))
                    nc.gpsimd.tensor_tensor(q_rstd[:], q_var[:], g.minus_half[:, 0:8], ALU.pow).then_inc(
                        sig.rms_power.sem, 1)

                with pool.Fori(0, rounds) as i:
                    for n in range(BODY):
                        if n % UNITS == 0:
                            split_q_low(i, n // UNITS)
                        if rms:
                            rms_powers(i, n)
                        if n % UNITS == 0:
                            split_o_low(i, n // UNITS)
                norm_pool(nc, pool, g)

            @block.tensor
            def _(pe):
                def group_in(i, slot):
                    pe.wait_ge(landed(slot).sem, landed(slot).at(per_group * (i + 1)))

                def project_q(i, n):
                    uu, slot, u = BODY * i + n, n // UNITS, n % UNITS
                    if u == 0 and per_group and not rms:
                        group_in(i, slot)
                    for j in range(2):
                        if u == 0:
                            pe.wait_ge(sig.q_split.sem, sig.q_split.at(4 * i + 2 * slot + j + 1))
                        pe.wait_ge(sig.q_done.sem, sig.q_done.at(2 * uu - 1 + j))
                        for hh in range(2):
                            h = 2 * j + hh
                            for c in range(CH):
                                at = (h * CH + c) * HD
                                for n_part, (wp, fp) in enumerate(parts):
                                    mm = nc.tensor.matmul(
                                        bank[j][:, hh * UT:(hh + 1) * UT].rearrange("p (b s) -> p b s", b=UB),
                                        wqo[:, wp, at:at + HD], own[:, fp, c, UB * u:UB * u + UB, :],
                                        start=(c == 0 and n_part == 0), stop=(c == CH - 1 and n_part == 2))
                        mm.then_inc(sig.q_ready.sem, 1)

                def project_k(i, n):
                    slot, u = (0 if both else n // UNITS), n % UNITS
                    kr = k_round(i, n)
                    if both and n == 0:
                        pe.wait_ge(sig.kv_in.sem, sig.kv_in.at(16 * (i + 1)))
                    if rms:
                        pe.wait_ge(sig.keys_taken.sem, sig.keys_taken.at(kr))
                    else:
                        pe.wait_ge(sig.k_done.sem, sig.k_done.at(kbanks * kr))
                    if both or kbanks == 2:
                        pe.wait_ge(sig.v_done.sem, sig.v_done.at(kbanks * kr))
                    if rms:
                        if u == 0:
                            group_in(i, slot)
                        for tt in range(2):
                            for c in range(CH):
                                mm = nc.tensor.matmul(
                                    bank[2][:, tt * HD:(tt + 1) * HD],
                                    feat[:, keys, c, UB * u + 2 * tt:UB * u + 2 * tt + 2, :],
                                    wkv[:, slot, c * HD:(c + 1) * HD], start=(c == 0), stop=(c == CH - 1))
                        mm.then_inc(sig.k_ready.sem, 1)
                        return
                    for h in range(kv_heads):
                        for c in range(CH):
                            w = wkv[:, slot, c * kdim + h * HD:c * kdim + (h + 1) * HD]
                            if both:
                                mm = nc.tensor.matmul(bank[2][:, :].rearrange("p (b k s) -> p b k s", k=2, s=SEQ), w,
                                                      feat[:, :, c, UB * u:UB * u + UB, :].rearrange(
                                                          "p k b s -> p b k s"),
                                                      start=(c == 0), stop=(c == CH - 1))
                            else:
                                out = bank[2 + h // 2][:, (h % 2) * UT:(h % 2 + 1) * UT]
                                mm = nc.tensor.matmul(out.rearrange("p (b s) -> p b s", b=UB), w,
                                                      feat[:, keys, c, UB * u:UB * u + UB, :],
                                                      start=(c == 0), stop=(c == CH - 1))
                        if h % 2 == 1 or kv_heads == 1:
                            mm.then_inc(sig.k_ready.sem, 1)

                def project_v(i, n):
                    slot, u = (0 if both else n // UNITS), n % UNITS
                    kr = k_round(i, n)
                    off = CH * kdim
                    if both or kbanks == 2:
                        pe.wait_ge(sig.k_done.sem, sig.k_done.at(kbanks * (kr + 1)))
                    else:
                        pe.wait_ge(sig.v_done.sem, sig.v_done.at(kr))
                    if both:
                        for b in range(UB):
                            for c in range(CH):
                                for k in (CTX, SELF):
                                    mm = nc.tensor.matmul(
                                        value_bank[k * SEQ:(k + 1) * SEQ, b * HD:(b + 1) * HD],
                                        feat[:, k, c, UB * u + b, :], wkv[:, slot, off + c * HD:off + (c + 1) * HD],
                                        start=(c == 0), stop=(c == CH - 1))
                        mm.then_inc(sig.v_ready.sem, 1)
                        return
                    for tt in range(2):
                        for c in range(CH):
                            out = bank[2 + tt][:, :] if kbanks == 2 else bank[3][:, tt * HD:(tt + 1) * HD]
                            mm = nc.tensor.matmul(
                                out, feat[:, keys, c, UB * u + 2 * tt:UB * u + 2 * tt + 2, :],
                                wkv[:, slot, off + c * kdim:off + (c + 1) * kdim],
                                start=(c == 0), stop=(c == CH - 1))
                        if kbanks == 2 or tt == 1:
                            mm.then_inc(sig.v_ready.sem, 1)

                def turn_keys(i, n):
                    uu = BODY * i + n
                    pe.wait_ge(sig.rms_done.sem, sig.rms_done.at(uu + 1))
                    for tt in range(2):
                        mm = nc.tensor.transpose(bank[2][:, tt * P:(tt + 1) * P], k_rows[:, tt, :], g.ident[:])
                    mm.then_inc(sig.keys_turned.sem, 1)

                def query_squares(i, n):
                    uu = BODY * i + n
                    pe.wait_ge(sig.squared.sem, sig.squared.at(2 * uu + 2))
                    for b in range(UB):
                        for j in range(2):
                            col = (b // 2) * 4 + j * 2 + b % 2
                            mm = nc.tensor.matmul(bank[5][:, col:col + 1],
                                                  q_sq[:, b, 2 * j:2 * j + 2, :].rearrange("p h s -> p (h s)"),
                                                  mean_col[:], start=True, stop=True)
                    mm.then_inc(sig.rms_sum.sem, 1)

                def scores(i, n):
                    uu, u = BODY * i + n, n % UNITS
                    pe.wait_ge(sig.q_done.sem, sig.q_done.at(2 * uu + 2))
                    if rms:
                        pe.wait_ge(sig.keys_taken.sem, sig.keys_taken.at(uu + 1))
                    elif n < UNITS or not both:
                        pe.wait_ge(sig.k_done.sem, sig.k_done.at(kbanks * (k_round(i, n) + 1)))
                    pe.wait_ge(score_bank_free.sem, score_bank_free.at(halves * uu))
                    for b in range(UB):
                        for h in range(GH):
                            j, h2 = h // 2, h % 2
                            if both:
                                dst = score_banks[b // 2][h2 * SEQ:(h2 + 1) * SEQ,
                                                            ((b % 2) * 2 + j) * klen:((b % 2) * 2 + j + 1) * klen]
                                key = k_t[:, u, b * klen:(b + 1) * klen]
                            else:
                                col = ((b // 2) * 4 + j * 2 + b % 2) * SEQ
                                dst = score_banks[0][h2 * SEQ:(h2 + 1) * SEQ, col:col + SEQ]
                                key = k_t[:, h if kv_heads == GH else 0, b * SEQ:(b + 1) * SEQ]
                            mm = nc.tensor.matmul(dst, q_t[:, h, b * SEQ:(b + 1) * SEQ], key,
                                                  start=True, stop=True)
                        if both and b % 2 == 1 or b == UB - 1 and not both:
                            mm.then_inc(sig.s_ready.sem, 1)

                def turn_probs(i, n):
                    uu = BODY * i + n
                    for half in range(halves):
                        pe.wait_ge(sig.p_ready.sem, sig.p_ready.at(halves * uu + half + 1))
                        pe.wait_ge(sig.pt_done.sem, sig.pt_done.at(halves * uu + half))
                        for blk in range(4):
                            mm = nc.tensor.transpose(bank[5][:, blk * P:(blk + 1) * P],
                                                     probs[:, half, blk * P:(blk + 1) * P], g.ident[:])
                        mm.then_inc(sig.pt_ready.sem, 1)

                def weighted_values(i, n):
                    uu, u, par = BODY * i + n, n % UNITS, n % 2
                    pe.wait_ge(sig.pt_done.sem, sig.pt_done.at(halves * (uu + 1)))
                    if n < UNITS or not both:
                        pe.wait_ge(sig.v_done.sem, sig.v_done.at(kbanks * (k_round(i, n) + 1)))
                    pe.wait_ge(sig.added.sem, sig.added.at(2 * uu))
                    for b2 in range(2):
                        for bp in range(2):
                            out = bank[6 + b2]
                            if both:
                                mm = nc.tensor.matmul(out[:, bp * UT:(bp + 1) * UT], v[:, u, 2 * bp + b2, :],
                                                      p_t[:, bp, b2 * UT:(b2 + 1) * UT], start=True, stop=True)
                                continue
                            rows = slice(b2 * SEQ, (b2 + 1) * SEQ)
                            if kv_heads == 1:
                                mm = nc.tensor.matmul(out[:, bp * UT:(bp + 1) * UT], v[rows, par, bp, :],
                                                      p_t[rows, 0, bp * UT:(bp + 1) * UT], start=True, stop=True)
                                continue
                            for h in range(GH):
                                mm = nc.tensor.matmul(
                                    out[:, bp * UT + h * SEQ:bp * UT + (h + 1) * SEQ],
                                    v[rows, par, bp, h * HD:(h + 1) * HD],
                                    p_t[rows, 0, bp * UT + h * SEQ:bp * UT + (h + 1) * SEQ], start=True, stop=True)
                        mm.then_inc(sig.o_ready.sem, 1)

                def project_out(i, n):
                    uu, slot, u = BODY * i + n, n // UNITS, n % UNITS
                    pe.wait_ge(sig.o_done.sem, sig.o_done.at(2 * (uu + 1)))
                    if u == 0:
                        pe.wait_ge(sig.o_split.sem, sig.o_split.at(2 * i + slot + 1))
                    for tt in range(2):
                        for h in range(GH):
                            for n_part, (op, wp) in enumerate(parts):
                                mm = nc.tensor.matmul(bank[6 + tt][:, :], o_t[:, op, h, 2 * tt:2 * tt + 2, :],
                                                      wqo[:, wp, wq_cols + h * DIM:wq_cols + (h + 1) * DIM],
                                                      start=(h == 0 and n_part == 0),
                                                      stop=(h == GH - 1 and n_part == 2))
                        mm.then_inc(sig.y_ready.sem, 1)

                pe.wait_ge(sig.own_low.sem, sig.own_low.at(UNITS))

                def step(front, back):
                    new_keys = front and (front[1] < UNITS or not both)
                    if front and rms:
                        project_k(*front)
                    if front:
                        project_q(*front)
                    if new_keys and not rms:
                        project_k(*front)
                    if back:
                        turn_probs(*back)
                    if new_keys:
                        project_v(*front)
                    if back:
                        weighted_values(*back)
                    if front and rms:
                        turn_keys(*front)
                        query_squares(*front)
                    if front:
                        scores(*front)
                    if back:
                        project_out(*back)

                pipeline(pe, step)
                if not last:
                    norm_tensor(nc, pe, g)

            @block.scalar
            def _(act):
                def queries(i, n):
                    uu = BODY * i + n
                    for j in range(2):
                        act.wait_ge(sig.q_ready.sem, sig.q_ready.at(2 * uu + j + 1))
                        if rms:
                            nc.scalar.activation(q_sq[:, :, 2 * j:2 * j + 2, :].rearrange("p b h s -> p h b s"),
                                                 bank[j][:, :].rearrange("p (h b s) -> p h b s", h=2, b=UB),
                                                 ACT.Square).then_inc(sig.squared.sem, 1)
                            nc.scalar.mul(q_t[:, 2 * j:2 * j + 2, :].rearrange("p h s -> p (h s)"),
                                          bank[j][:, :], q_w[:, 0:1]).then_inc(sig.q_done.sem, 1)
                        else:
                            nc.scalar.copy(q_t[:, 2 * j:2 * j + 2, :].rearrange("p h s -> p (h s)"),
                                           bank[j][:, :]).then_inc(sig.q_done.sem, 1)

                def keys_out(i, n):
                    kr = k_round(i, n)
                    if rms:
                        act.wait_ge(sig.k_ready.sem, sig.k_ready.at(kr + 1))
                        for tt in range(2):
                            if tt == 1:
                                act.wait_ge(sig.act_step.sem, sig.act_step.at(2 * kr + 1))
                            nc.scalar.activation(k_junk[:], bank[2][:, tt * HD:(tt + 1) * HD], ACT.Square,
                                                 accum_out=ssq[:, tt:tt + 1]).then_inc(sig.act_step.sem, 1)
                        return
                    for j in range(kbanks):
                        act.wait_ge(sig.k_ready.sem, sig.k_ready.at(kbanks * kr + j + 1))
                        if both:
                            dst, src = k_t[:, n % UNITS, :], bank[2][:, :]
                        elif kv_heads == 1:
                            dst, src = k_t[:, 0, :], bank[2][:, 0:UT]
                        else:
                            dst = k_t[:, 2 * j:2 * j + 2, :].rearrange("p h s -> p (h s)")
                            src = bank[2 + j][:, :]
                        nc.scalar.copy(dst, src).then_inc(sig.k_done.sem, 1)

                def turned_keys(i, n):
                    uu = BODY * i + n
                    act.wait_ge(sig.keys_turned.sem, sig.keys_turned.at(uu + 1))
                    nc.scalar.mul(k_t[:, 0, :], bank[2][:, 0:UT], k_w[:, 0:1]).then_inc(sig.keys_taken.sem, 1)

                def outputs(i, n):
                    uu = BODY * i + n
                    for b2 in range(2):
                        act.wait_ge(sig.o_ready.sem, sig.o_ready.at(2 * uu + b2 + 1))
                        nc.scalar.copy(o_part(HIGH, b2), o_bank(b2)).then_inc(sig.o_high.sem, 1)

                def exponentials(i, n):
                    uu = BODY * i + n
                    for half in range(halves):
                        act.wait_ge(sig.shifted.sem, sig.shifted.at(halves * uu + half + 1))
                        nc.scalar.activation(probs[:, half, :], shifted[:, half, :], ACT.Exp,
                                             scale=1.0 if (bias is not None or rms) else scale).then_inc(
                            sig.exp_done.sem, 1)

                for u in range(UNITS):
                    nc.scalar.copy(own[:, HIGH, :, units_batches(u), :], feat[:, SELF, :, units_batches(u), :]).then_inc(
                        sig.own_high.sem, 1)
                if rms or key_mask is not None or mask is not None:
                    act.wait_ge(sig.small_in.sem, sig.small_in.at(small_loads))

                def split_q_high(group):
                    act.wait_ge(sig.qo_in.sem, sig.qo_in.at(32 * group + 16))
                    for j in range(2):
                        nc.scalar.copy(wqo[:, HIGH, q_half(j)], raw[:, q_half(j)]).then_inc(sig.wq_high.sem, 1)

                def split_o_high(group):
                    act.wait_ge(sig.qo_in.sem, sig.qo_in.at(32 * group + 32))
                    act.wait_ge(sig.added.sem, sig.added.at(2 * UNITS * group))
                    nc.scalar.copy(wqo[:, HIGH, wq_cols:], raw[:]).then_inc(sig.wo_high.sem, 1)

                def step(front, back):
                    if front:
                        i, n = front
                        if rms:
                            keys_out(i, n)
                        queries(i, n)
                        next_group = 2 * i + n // UNITS + 1
                        very_last = n == BODY - 1 and isinstance(i, int)
                        if n % UNITS == UNITS - 1 and not very_last:
                            split_q_high(next_group)
                        if not rms and (n < UNITS or not both):
                            keys_out(i, n)
                    if back:
                        outputs(*back)
                    if front:
                        if rms:
                            turned_keys(i, n)
                        exponentials(i, n)
                        if n % UNITS == 0:
                            split_o_high(2 * i + n // UNITS)

                split_q_high(0)
                pipeline(act, step)
                if not last:
                    norm_scalar(nc, act, g)

            @block.vector
            def _(dve):
                head_steps = Steps(sig.dve_step)
                for u in range(UNITS):
                    dve.wait_ge(sig.own_high.sem, u + 1)
                    nc.vector.tensor_tensor(own[:, LOW, :, units_batches(u), :], feat[:, SELF, :, units_batches(u), :],
                                            own[:, HIGH, :, units_batches(u), :], ALU.subtract).then_inc(
                        sig.own_low.sem, 1)
                if key_mask is not None:
                    dve.wait_ge(sig.small_in.sem, sig.small_in.at(small_loads))
                    nc.vector.tensor_copy(km_one[:], km_u8).then_inc(head_steps.count(), 1)
                    dve.wait_ge(sig.dve_step.sem, head_steps.so_far())
                    nc.vector.tensor_scalar(km_neg[:], km_one[:], 1.0, -NEG, ALU.subtract, ALU.mult).then_inc(
                        head_steps.count(), 1)
                    dve.wait_ge(sig.dve_step.sem, head_steps.so_far())
                if mask is not None:
                    dve.wait_ge(sig.small_in.sem, sig.small_in.at(small_loads))
                if rms:
                    nc.vector.memset(mean_col[:], 1.0 / HD).then_inc(head_steps.count(), 1)
                    dve.wait_ge(sig.dve_step.sem, head_steps.so_far())
                head = head_steps.n
                per_unit = halves * (before_exp + after_exp)

                def turned(i, n):
                    uu = BODY * i + n
                    for half in range(halves):
                        dve.wait_ge(sig.pt_ready.sem, sig.pt_ready.at(halves * uu + half + 1))
                        nc.vector.tensor_copy(p_t[:, half, :], bank[5][:, :]).then_inc(sig.pt_done.sem, 1)

                def values(i, n):
                    kr = k_round(i, n)
                    for j in range(kbanks):
                        dve.wait_ge(sig.v_ready.sem, sig.v_ready.at(kbanks * kr + j + 1))
                        if both:
                            dst, src = v[:, n % UNITS, :, :].rearrange("p b d -> p (b d)"), value_bank[:, :]
                        elif kbanks == 2:
                            dst, src = v[:, n % 2, j, :], bank[2 + j][:, :]
                        else:
                            dst, src = v[:, n % 2, :, :].rearrange("p t d -> p (t d)"), bank[3][:, 0:2 * HD]
                        nc.vector.tensor_copy(dst, src).then_inc(sig.v_done.sem, 1)

                def rms_keys(i, n):
                    uu = BODY * i + n
                    dve.wait_ge(sig.act_step.sem, sig.act_step.at(2 * uu + 2))
                    nc.vector.tensor_scalar(k_var[:], ssq[:], 1.0 / HD, LN_EPS, ALU.mult, ALU.add).then_inc(
                        sig.rms_var.sem, 1)
                    dve.wait_ge(sig.rms_power.sem, sig.rms_power.at(2 * uu + 1))
                    for tt in range(2):
                        mm = nc.vector.tensor_scalar(k_rows[:, tt, :], bank[2][:, tt * HD:(tt + 1) * HD],
                                                     k_rstd[:, tt:tt + 1], None, ALU.mult)
                    mm.then_inc(sig.rms_done.sem, 1)

                def rms_queries(i, n):
                    uu = BODY * i + n
                    dve.wait_ge(sig.rms_sum.sem, sig.rms_sum.at(uu + 1))
                    nc.vector.tensor_scalar(q_var[:], bank[5][:, 0:8], LN_EPS, 1.0 / scale ** 2, ALU.add,
                                            ALU.mult).then_inc(sig.rms_var.sem, 1)

                def softmax(i, n):
                    uu = BODY * i + n
                    for half in range(halves):
                        steps = Steps(sig.dve_step, head + per_unit * uu + before_exp * half)
                        dve.wait_ge(sig.s_ready.sem, sig.s_ready.at(halves * uu + half + 1))
                        raw = score_banks[half][:, :]
                        sh = shifted[:, half, :]
                        rows = raw.rearrange("p (g k) -> p g k", k=klen)
                        sh_rows = sh.rearrange("p (g k) -> p g k", k=klen)
                        m = mx[:, half, :]
                        if bias is not None:
                            if bias_cols == BATCH * GH // 2 * SEQ:
                                u = n % UNITS
                                b_ap = bias_sb[:, n // UNITS, u * 512:(u + 1) * 512]
                                nc.vector.scalar_tensor_tensor(sh, raw, scale, b_ap, ALU.mult,
                                                               ALU.add).then_inc(sig.s_read.sem, 1)
                            else:
                                b_ap = over(bias_sb[:, n // UNITS, :], (1, 2))
                                nc.vector.scalar_tensor_tensor(
                                    sh.rearrange("p (a c) -> p a c", a=2), raw.rearrange("p (a c) -> p a c", a=2),
                                    scale, b_ap, ALU.mult, ALU.add).then_inc(sig.s_read.sem, 1)
                            dve.wait_ge(sig.s_read.sem, sig.s_read.at(uu + 1))
                            if key_mask is not None:
                                u = n % UNITS
                                km = km_neg[:, UB * u:UB * u + UB, :].rearrange("p (a b) s -> p a (b s)", a=2)
                                four = sh.rearrange("p (a j c) -> p a j c", a=2, j=2)
                                nc.vector.tensor_tensor(four, four, over(km, (2, 2)), ALU.add).then_inc(
                                    steps.count(), 1)
                                dve.wait_ge(sig.dve_step.sem, steps.so_far())
                            nc.vector.tensor_reduce(m, sh_rows, AX.X, ALU.max).then_inc(steps.count(), 1)
                            dve.wait_ge(sig.dve_step.sem, steps.so_far())
                            nc.vector.tensor_tensor(sh_rows, sh_rows, over(m, (2, klen)), ALU.subtract).then_inc(
                                sig.shifted.sem, 1)
                        elif rms:
                            dve.wait_ge(sig.rms_power.sem, sig.rms_power.at(2 * uu + 2))
                            nc.vector.tensor_tensor(sh_rows, rows, over(q_rstd[:], (2, klen)), ALU.mult).then_inc(
                                sig.s_read.sem, 1)
                            dve.wait_ge(sig.s_read.sem, sig.s_read.at(uu + 1))
                            nc.vector.tensor_tensor(sh_rows, sh_rows, over(mask_sb[:], (1, ngr)),
                                                    ALU.add).then_inc(steps.count(), 1)
                            dve.wait_ge(sig.dve_step.sem, steps.so_far())
                            nc.vector.tensor_reduce(m, sh_rows, AX.X, ALU.max).then_inc(steps.count(), 1)
                            dve.wait_ge(sig.dve_step.sem, steps.so_far())
                            nc.vector.tensor_tensor(sh_rows, sh_rows, over(m, (2, klen)), ALU.subtract).then_inc(
                                sig.shifted.sem, 1)
                        else:
                            nc.vector.tensor_reduce(m, rows, AX.X, ALU.max).then_inc(steps.count(), 1)
                            dve.wait_ge(sig.dve_step.sem, steps.so_far())
                            nc.vector.tensor_tensor(sh_rows, rows, over(m, (2, klen)), ALU.subtract).then_inc(
                                sig.shifted.sem, 1)
                    for half in range(halves):
                        steps = Steps(sig.dve_step, head + per_unit * uu + before_exp * halves + after_exp * half)
                        pr_rows = probs[:, half, :].rearrange("p (g k) -> p g k", k=klen)
                        t, r = total[:, half, :], recip[:, half, :]
                        dve.wait_ge(sig.exp_done.sem, sig.exp_done.at(halves * uu + half + 1))
                        nc.vector.tensor_reduce(t, pr_rows, AX.X, ALU.add).then_inc(steps.count(), 1)
                        dve.wait_ge(sig.dve_step.sem, steps.so_far())
                        nc.vector.reciprocal(r, t).then_inc(steps.count(), 1)
                        dve.wait_ge(sig.dve_step.sem, steps.so_far())
                        if key_mask is not None:
                            u = n % UNITS
                            nc.vector.tensor_tensor(pr_rows, pr_rows, over(r, (2, klen)), ALU.mult).then_inc(
                                steps.count(), 1)
                            dve.wait_ge(sig.dve_step.sem, steps.so_far())
                            km = km_one[:, UB * u:UB * u + UB, :].rearrange("p (a b) s -> p a (b s)", a=2)
                            four = probs[:, half, :].rearrange("p (a j c) -> p a j c", a=2, j=2)
                            nc.vector.tensor_tensor(four, four, over(km, (2, 2)), ALU.mult).then_inc(
                                sig.p_ready.sem, 1)
                        else:
                            nc.vector.tensor_tensor(pr_rows, pr_rows, over(r, (2, klen)), ALU.mult).then_inc(
                                sig.p_ready.sem, 1)

                def outputs_low(i, n):
                    uu = BODY * i + n
                    for b2 in range(2):
                        dve.wait_ge(sig.o_high.sem, sig.o_high.at(2 * uu + b2 + 1))
                        nc.vector.tensor_tensor(o_part(LOW, b2), o_bank(b2), o_part(HIGH, b2),
                                                ALU.subtract).then_inc(sig.o_done.sem, 1)

                def add(i, n):
                    uu, u = BODY * i + n, n % UNITS
                    for tt in range(2):
                        dve.wait_ge(sig.y_ready.sem, sig.y_ready.at(2 * uu + tt + 1))
                        t = 2 * u + tt
                        nc.vector.tensor_tensor(x[:, t, :], x[:, t, :], bank[6 + tt][:, :], ALU.add).then_inc(
                            sig.added.sem, 1)

                def step(front, back):
                    if front and rms:
                        rms_keys(*front)
                    if back:
                        turned(*back)
                    if front and (front[1] < UNITS or not both):
                        values(*front)
                    if back:
                        outputs_low(*back)
                    if front:
                        if rms:
                            rms_queries(*front)
                        softmax(*front)
                    if back:
                        add(*back)

                pipeline(dve, step)
                dve.wait_ge(sig.added.sem, sig.added.at(2 * rounds * BODY))
                norm_vector(nc, dve, g)



def narrow_attention(nc, g, name, last, weights, keys, scale, bias=None, rope=None, out_proj=True):
    sig, feat, x, bank = g.sig, g.feat, g.x, g.bank
    nbody = 2
    rounds = TILES // nbody
    blocks = KV // 2
    wk_at, wv_at, wo_at = CH * DIM, CH * (DIM + P), CH * (DIM + 2 * P)
    vcols = 2 * (ND + 1)
    with ExitStack() as ctx:
        def sb(what, shape, dt=F32):
            return ctx.enter_context(nc.sbuf_tensor(f"{name}_{what}", shape, dt))
        w = sb("w", [P, weights.shape[1]])
        ks = sb("ks", [P, 2, CH, P])
        q_t = sb("q_t", [P, 2, NR, P])
        k_t = sb("k_t", [P, P])
        k_diag = sb("k_diag", [P, 2, 2, KV, SEQ])
        v_diag = sb("v_diag", [P, 2, 2, blocks, 2, ND + 1])
        v_sum = sb("v_sum", [P, 2 * P])
        head_of = sb("head_of", [P, KV])
        half_of = sb("half_of", [P, 2])
        shifted = sb("shifted", [P, 2, 512])
        probs = sb("probs", [P, 2, 512])
        p_t = sb("p_t", [P, 512])
        mx = sb("mx", [P, 2, KV])
        recip = sb("recip", [P, HEADS])
        attn = sb("attn", [P, HEADS, ND])
        attn_t = sb("attn_t", [P, NR, P])
        if bias is not None:
            bias_sb = sb("bias", [P, NR, 512])
        if rope is not None:
            consts = sb("consts", [P, rope.shape[1]])
            rot = consts[:, 0:P]
            cos, sin = consts[:, P:P + SEQ], consts[:, P + SEQ:P + 2 * SEQ]
            at = P + 2 * SEQ
            q_bias, k_bias, v_bias = consts[:, at:at + NR], consts[:, at + NR:at + NR + 1], \
                consts[:, at + NR + 1:at + NR + 1 + P]
            turned_q = sb("turned_q", [P, NR * P])
            turned_k = sb("turned_k", [P, P])
        loads = 16 * (3 + (bias is not None) + (rope is not None))
        score_bank_free = sig.s_read if bias is not None else sig.shifted
        o_banks = (bank[3], bank[7])

        def o_block(r, jj):
            n = r * blocks + jj
            return (o_banks[0], n) if r < NR - 1 else (o_banks[1], n - (NR - 1) * blocks)

        def pipeline(engine, step):
            step(None, (0, 0), None)
            step((0, 0), (0, 1), None)
            with engine.Fori(0, rounds - 1) as i:
                step((i, 1), (i + 1, 0), (i, 0))
                step((i + 1, 0), (i + 1, 1), (i, 1))
            step((rounds - 1, 1), None, (rounds - 1, 0))
            step(None, None, (rounds - 1, 1))

        def own_batches(i, n):
            return bass.ds(2 * (nbody * i + n), 2)

        with nc.Block() as block:
            @block.sync
            def _(sp):
                sp.dma_start(head_of[:], g.t["head_of"]).then_inc(sig.small_in.sem, 16)
                sp.dma_start(half_of[:], g.t["half_of"]).then_inc(sig.small_in.sem, 16)
                if rope is not None:
                    sp.dma_start(consts[:], rope).then_inc(sig.small_in.sem, 16)
                sp.dma_start(w[:], weights).then_inc(sig.small_in.sem, 16)
                if bias is not None:
                    sp.dma_start(bias_sb[:].rearrange("p r c -> p (r c)"), bias).then_inc(sig.small_in.sem, 16)
                if last:
                    norm_sync(nc, sp, g)

            @block.gpsimd
            def _(pool):
                norm_pool(nc, pool, g)

            @block.tensor
            def _(pe):
                def project_v(i, n, b):
                    uu = nbody * i + n
                    if b == 0:
                        pe.wait_ge(sig.staged.sem, sig.staged.at(uu + 1))
                        pe.wait_ge(sig.kd_done.sem, sig.kd_done.at(uu))
                        pe.wait_ge(sig.v_done.sem, sig.v_done.at(uu))
                        if rope is not None:
                            pe.wait_ge(sig.q_done.sem, sig.q_done.at(uu + 1))
                    for c in range(CH):
                        for dup in range(2):
                            mm = nc.tensor.matmul(
                                bank[2][dup * SEQ:(dup + 1) * SEQ, (2 + b) * P:(3 + b) * P],
                                ks[:, n % 2, c, b * SEQ:(b + 1) * SEQ],
                                w[:, wv_at + c * P:wv_at + (c + 1) * P], start=(c == 0), stop=(c == CH - 1))
                    if b == 1:
                        mm.then_inc(sig.v_ready.sem, 1)

                def project_k(i, n):
                    uu = nbody * i + n
                    pe.wait_ge(sig.kd_done.sem, sig.kd_done.at(uu))
                    pe.wait_ge(sig.v_done.sem, sig.v_done.at(uu))
                    for c in range(CH):
                        mm = nc.tensor.matmul(bank[2][:, 0:P].rearrange("p (b s) -> p b s", b=2),
                                              w[:, wk_at + c * P:wk_at + (c + 1) * P],
                                              feat[:, keys, c, own_batches(i, n), :],
                                              start=(c == 0), stop=(c == CH - 1))
                    mm.then_inc(sig.k_ready.sem, 1)

                def project_q(i, n, chunks):
                    uu = nbody * i + n
                    if chunks[0] == 0:
                        if out_proj:
                            pe.wait_ge(sig.added.sem, sig.added.at(uu - 1))
                        if rope is not None:
                            pe.wait_ge(sig.kd_done.sem, sig.kd_done.at(uu))
                        pe.wait_ge(sig.q_done.sem, sig.q_done.at(uu))
                    for r in chunks:
                        for c in range(CH):
                            mm = nc.tensor.matmul(bank[0][:, r * P:(r + 1) * P].rearrange("p (b s) -> p b s", b=2),
                                                  w[:, c * DIM + r * P:c * DIM + (r + 1) * P],
                                                  feat[:, SELF, c, own_batches(i, n), :],
                                                  start=(c == 0), stop=(c == CH - 1))
                    if chunks[-1] == NR - 1:
                        mm.then_inc(sig.q_ready.sem, 1)

                def rotate(i, n):
                    uu = nbody * i + n
                    pe.wait_ge(sig.q_done.sem, sig.q_done.at(uu + 1))
                    nc.tensor.matmul(bank[1][:, :], rot, q_t[:, n % 2, :, :].rearrange("p r s -> p (r s)"),
                                     start=True, stop=True)
                    nc.tensor.matmul(bank[0][:, 0:P], rot, k_t[:], start=True, stop=True).then_inc(
                        sig.rotated.sem, 1)

                def scores(i, n, r):
                    uu = nbody * i + n
                    if r == 0:
                        pe.wait_ge(sig.kd_done.sem, sig.kd_done.at(uu + 1))
                        if rope is None:
                            pe.wait_ge(sig.q_done.sem, sig.q_done.at(uu + 1))
                    ss = NR * uu + r
                    pe.wait_ge(score_bank_free.sem, score_bank_free.at(ss - 1))
                    for b in range(2):
                        mm = nc.tensor.matmul(bank[4 + r % 2][b * SEQ:(b + 1) * SEQ, :],
                                              q_t[:, n % 2, r, b * SEQ:(b + 1) * SEQ],
                                              k_diag[:, n % 2, b, :, :].rearrange("p h k -> p (h k)"),
                                              start=True, stop=True)
                    mm.then_inc(sig.s_ready.sem, 1)

                def turn_probs(i, n, r):
                    ss = NR * (nbody * i + n) + r
                    pe.wait_ge(sig.exp_done.sem, sig.exp_done.at(ss + 1))
                    pe.wait_ge(sig.pt_done.sem, sig.pt_done.at(ss))
                    for jj in range(blocks):
                        mm = nc.tensor.transpose(bank[6][:, jj * P:(jj + 1) * P],
                                                 probs[:, r % 2, jj * P:(jj + 1) * P], g.ident[:])
                    mm.then_inc(sig.pt_ready.sem, 1)

                def weighted_values(i, n, r):
                    uu = nbody * i + n
                    ss = NR * uu + r
                    if r == 0:
                        pe.wait_ge(sig.v_done.sem, sig.v_done.at(uu + 1))
                        pe.wait_ge(sig.o_done.sem, sig.o_done.at(uu))
                    pe.wait_ge(sig.pt_done.sem, sig.pt_done.at(ss + 1))
                    for jj in range(blocks):
                        ob, at_block = o_block(r, jj)
                        for b in range(2):
                            mm = nc.tensor.matmul(
                                ob[b * SEQ:(b + 1) * SEQ, at_block * vcols:(at_block + 1) * vcols],
                                p_t[:, jj * P + b * SEQ:jj * P + (b + 1) * SEQ],
                                v_diag[:, n % 2, b, jj, :, :].rearrange("p h d -> p (h d)"),
                                start=True, stop=True)
                    if r == NR - 1:
                        mm.then_inc(sig.o_ready.sem, 1)

                def turn_output(i, n):
                    uu = nbody * i + n
                    pe.wait_ge(sig.o_done.sem, sig.o_done.at(uu + 1))
                    pe.wait_ge(sig.attn_taken.sem, sig.attn_taken.at(uu))
                    for r in range(NR):
                        mm = nc.tensor.transpose(bank[1][:, r * P:(r + 1) * P],
                                                 attn[:, r * KV:(r + 1) * KV, :].rearrange("p h d -> p (h d)"),
                                                 g.ident[:])
                    mm.then_inc(sig.attn_turned.sem, 1)

                def project_out(i, n, queries_too):
                    uu = nbody * i + n
                    pe.wait_ge(sig.attn_taken.sem, sig.attn_taken.at(uu + 1))
                    if queries_too:
                        pe.wait_ge(sig.q_done.sem, sig.q_done.at(uu + 2))
                    for r in range(NR):
                        mm = nc.tensor.matmul(bank[0][:, :], attn_t[:, r, :],
                                              w[:, wo_at + r * DIM:wo_at + (r + 1) * DIM],
                                              start=(r == 0), stop=(r == NR - 1))
                    mm.then_inc(sig.y_ready.sem, 1)

                pe.wait_ge(sig.small_in.sem, sig.small_in.at(loads))

                def step(unit, ahead, back):
                    late = rope is None
                    if unit:
                        scores(*unit, 0)
                        scores(*unit, 1)
                    if back and out_proj:
                        turn_output(*back)
                    if ahead:
                        if late:
                            project_v(*ahead, 0)
                            project_v(*ahead, 1)
                        project_k(*ahead)
                    if unit:
                        turn_probs(*unit, 0)
                        scores(*unit, 2)
                        weighted_values(*unit, 0)
                    if back and out_proj:
                        project_out(*back, unit is not None)
                    if ahead and not late:
                        project_q(*ahead, range(NR))
                    if unit:
                        turn_probs(*unit, 1)
                        scores(*unit, 3)
                        weighted_values(*unit, 1)
                    if ahead and not late:
                        rotate(*ahead)
                    for r in (2, 3):
                        if unit:
                            turn_probs(*unit, r)
                        if ahead and late:
                            project_q(*ahead, range((r - 2) * NR // 2, (r - 1) * NR // 2))
                        if ahead and not late:
                            project_v(*ahead, r - 2)
                        if unit:
                            weighted_values(*unit, r)

                pipeline(pe, step)
                if not last:
                    norm_tensor(nc, pe, g)

            @block.scalar
            def _(act):
                def stage(i, n):
                    nc.scalar.copy(ks[:, n % 2, :, :].rearrange("p c (b s) -> p c b s", s=SEQ),
                                   feat[:, keys, :, own_batches(i, n), :]).then_inc(sig.staged.sem, 1)

                def queries(i, n):
                    uu = nbody * i + n
                    act.wait_ge(sig.q_ready.sem, sig.q_ready.at(uu + 1))
                    if rope is None:
                        nc.scalar.copy(q_t[:, n % 2, :, :].rearrange("p r s -> p (r s)"), bank[0][:, :]).then_inc(
                            sig.q_done.sem, 1)
                        return
                    for r in range(NR):
                        nc.scalar.activation(q_t[:, n % 2, r, :], bank[0][:, r * P:(r + 1) * P], ACT.Identity,
                                             bias=q_bias[:, r:r + 1])
                    nc.scalar.activation(k_t[:], bank[2][:, 0:P], ACT.Identity, bias=k_bias).then_inc(
                        sig.q_done.sem, 1)

                def exponentials(i, n, r):
                    ss = NR * (nbody * i + n) + r
                    act.wait_ge(sig.shifted.sem, sig.shifted.at(ss + 1))
                    nc.scalar.activation(probs[:, r % 2, :], shifted[:, r % 2, :], ACT.Exp,
                                         scale=1.0 if bias is not None else scale).then_inc(sig.exp_done.sem, 1)

                def turned(i, n, r):
                    ss = NR * (nbody * i + n) + r
                    act.wait_ge(sig.pt_ready.sem, sig.pt_ready.at(ss + 1))
                    nc.scalar.copy(p_t[:], bank[6][:, :]).then_inc(sig.pt_done.sem, 1)

                def output(i, n):
                    uu = nbody * i + n
                    act.wait_ge(sig.attn_turned.sem, sig.attn_turned.at(uu + 1))
                    nc.scalar.copy(attn_t[:].rearrange("p r s -> p (r s)"), bank[1][:, :]).then_inc(
                        sig.attn_taken.sem, 1)

                act.wait_ge(sig.small_in.sem, sig.small_in.at(loads))

                def step(unit, ahead, back):
                    if ahead:
                        stage(*ahead)
                    if unit:
                        exponentials(*unit, 0)
                    if back and out_proj:
                        output(*back)
                    if unit:
                        exponentials(*unit, 1)
                        turned(*unit, 0)
                        exponentials(*unit, 2)
                    if ahead and rope is not None:
                        queries(*ahead)
                    if unit:
                        turned(*unit, 1)
                        exponentials(*unit, 3)
                        turned(*unit, 2)
                        turned(*unit, 3)
                    if ahead and rope is None:
                        queries(*ahead)

                pipeline(act, step)
                if not last:
                    norm_scalar(nc, act, g)

            @block.vector
            def _(dve):
                def spread_values(i, n):
                    uu = nbody * i + n
                    dve.wait_ge(sig.v_ready.sem, sig.v_ready.at(uu + 1))
                    if rope is None:
                        dve.wait_ge(sig.k_ready.sem, sig.k_ready.at(uu + 1))
                    vals = bank[2][:, 2 * P:4 * P]
                    if rope is not None:
                        steps = Steps(sig.rope_step, 7 * uu + 6)
                        nc.vector.tensor_tensor(v_sum[:].rearrange("p (b c) -> p b c", b=2),
                                                vals.rearrange("p (b c) -> p b c", b=2), over(v_bias, (1, 2)),
                                                ALU.add).then_inc(steps.count(), 1)
                        dve.wait_ge(sig.rope_step.sem, steps.so_far())
                        vals = v_sum[:]
                    nc.vector.tensor_tensor(
                        v_diag[:, n % 2, :, :, :, 0:ND].rearrange("p b j h d -> p (b j) h d"),
                        vals.rearrange("p (bj h d) -> p bj h d", h=2, d=ND),
                        over(half_of[:], (1, 2 * blocks), (3, ND)), ALU.mult).then_inc(sig.v_done.sem, 1)

                def spread_keys(i, n):
                    uu = nbody * i + n
                    key = bank[2][:, 0:P]
                    dve.wait_ge(sig.k_ready.sem, sig.k_ready.at(uu + 1))
                    if rope is not None:
                        steps = Steps(sig.rope_step, 7 * uu)
                        own_q = q_t[:, n % 2, :, :]
                        dve.wait_ge(sig.rotated.sem, sig.rotated.at(uu + 1))
                        nc.vector.tensor_tensor(turned_q[:].rearrange("p (a s) -> p a s", s=SEQ),
                                                bank[1][:, :].rearrange("p (a s) -> p a s", s=SEQ),
                                                over(sin, (1, 2 * NR)), ALU.mult).then_inc(steps.count(), 1)
                        nc.vector.tensor_tensor(turned_k[:].rearrange("p (a s) -> p a s", s=SEQ),
                                                bank[0][:, 0:P].rearrange("p (a s) -> p a s", s=SEQ),
                                                over(sin, (1, 2)), ALU.mult).then_inc(steps.count(), 1)
                        q_rows = own_q.rearrange("p r (b s) -> p (r b) s", s=SEQ)
                        k_rows = k_t[:].rearrange("p (b s) -> p b s", s=SEQ)
                        nc.vector.tensor_tensor(q_rows, q_rows, over(cos, (1, 2 * NR)), ALU.mult).then_inc(
                            steps.count(), 1)
                        nc.vector.tensor_tensor(k_rows, k_rows, over(cos, (1, 2)), ALU.mult).then_inc(
                            steps.count(), 1)
                        dve.wait_ge(sig.rope_step.sem, steps.so_far())
                        q_flat = own_q.rearrange("p r s -> p (r s)")
                        nc.vector.tensor_tensor(q_flat, q_flat, turned_q[:], ALU.add).then_inc(steps.count(), 1)
                        nc.vector.tensor_tensor(k_t[:], k_t[:], turned_k[:], ALU.add).then_inc(steps.count(), 1)
                        dve.wait_ge(sig.rope_step.sem, steps.so_far())
                        key = k_t[:]
                    for b in range(2):
                        ins = nc.vector.tensor_tensor(k_diag[:, n % 2, b, :, :],
                                                      over(key[:, b * SEQ:(b + 1) * SEQ], (1, KV)),
                                                      over(head_of[:], (2, SEQ)), ALU.mult)
                    ins.then_inc(sig.kd_done.sem, 1)

                def softmax(i, n, r):
                    ss = NR * (nbody * i + n) + r
                    dve.wait_ge(sig.s_ready.sem, sig.s_ready.at(ss + 1))
                    raw = bank[4 + r % 2][:, :]
                    sh = shifted[:, r % 2, :]
                    m = mx[:, r % 2, :]
                    src = raw
                    if bias is not None:
                        nc.vector.scalar_tensor_tensor(sh, raw, scale, bias_sb[:, r, :], ALU.mult, ALU.add).then_inc(
                            sig.s_read.sem, 1)
                        dve.wait_ge(sig.s_read.sem, sig.s_read.at(ss + 1))
                        src = sh
                    rows = src.rearrange("p (h k) -> p h k", k=SEQ)
                    nc.vector.tensor_reduce(m, rows, AX.X, ALU.max).then_inc(sig.row_max.sem, 1)
                    dve.wait_ge(sig.row_max.sem, sig.row_max.at(ss + 1))
                    nc.vector.tensor_tensor(sh.rearrange("p (h k) -> p h k", k=SEQ), rows, over(m, (2, SEQ)),
                                            ALU.subtract).then_inc(sig.shifted.sem, 1)

                def normalise(i, n):
                    uu = nbody * i + n
                    steps = Steps(sig.row_sum, 2 * uu)
                    dve.wait_ge(sig.o_ready.sem, sig.o_ready.at(uu + 1))
                    first = (NR - 1) * KV
                    parts = [(o_banks[0][:, 0:first * (ND + 1)], 0, first),
                             (o_banks[1][:, 0:KV * (ND + 1)], first, HEADS)]
                    for ob, lo, hi in parts:
                        rows = ob.rearrange("p (h d) -> p h d", d=ND + 1)
                        nc.vector.reciprocal(recip[:, lo:hi], rows[:, :, ND]).then_inc(steps.count(), 1)
                    dve.wait_ge(sig.row_sum.sem, steps.so_far())
                    for ob, lo, hi in parts:
                        rows = ob.rearrange("p (h d) -> p h d", d=ND + 1)
                        ins = nc.vector.tensor_tensor(attn[:, lo:hi, :], rows[:, :, 0:ND],
                                                      over(recip[:, lo:hi], (2, ND)), ALU.mult)
                    ins.then_inc(sig.o_done.sem, 1)
                    if not out_proj:
                        dve.wait_ge(sig.o_done.sem, sig.o_done.at(uu + 1))
                        tile = x[:, bass.ds(uu, 1), :].rearrange("p t (k r d) -> p (t r) k d", k=KV, r=NR)
                        nc.vector.tensor_tensor(tile, tile, attn[:].rearrange("p (r k) d -> p r k d", r=NR),
                                                ALU.add).then_inc(sig.added.sem, 1)

                def add(i, n):
                    uu = nbody * i + n
                    dve.wait_ge(sig.y_ready.sem, sig.y_ready.at(uu + 1))
                    tile = x[:, bass.ds(uu, 1), :].rearrange("p t c -> p (t c)")
                    nc.vector.tensor_tensor(tile, tile, bank[0][:, :], ALU.add).then_inc(sig.added.sem, 1)

                head = Steps(sig.dve_step)
                dve.wait_ge(sig.small_in.sem, sig.small_in.at(loads))
                nc.vector.memset(v_diag[:], 0.0).then_inc(head.count(), 1)
                dve.wait_ge(sig.dve_step.sem, head.so_far())
                for par in range(2):
                    for h in range(2):
                        nc.vector.tensor_copy(v_diag[:, par, :, :, h, ND:ND + 1].rearrange("p b j d -> p (b j) d"),
                                              over(half_of[:, h:h + 1], (1, 2 * blocks))).then_inc(head.count(), 1)
                dve.wait_ge(sig.dve_step.sem, head.so_far())

                def step(unit, ahead, back):
                    if back:
                        normalise(*back)
                    if unit:
                        softmax(*unit, 0)
                        softmax(*unit, 1)
                    if ahead and rope is None:
                        spread_values(*ahead)
                        spread_keys(*ahead)
                    if unit:
                        softmax(*unit, 2)
                    if back and out_proj:
                        add(*back)
                    if unit:
                        softmax(*unit, 3)
                    if ahead and rope is not None:
                        spread_keys(*ahead)
                        spread_values(*ahead)

                pipeline(dve, step)
                dve.wait_ge(sig.added.sem, sig.added.at(TILES))
                norm_vector(nc, dve, g)



def routed_ffn(nc, g, name, last, weights, low, experts, rank, chosen, scaling, expert_bias=None, out_bias=None):
    sig, feat, x, bank = g.sig, g.feat, g.x, g.bank
    er = experts * rank
    cols = DIM + experts + er
    per_bank = 512 // er
    with ExitStack() as ctx:
        def sb(what, shape, dt=F32):
            return ctx.enter_context(nc.sbuf_tensor(f"{name}_{what}", shape, dt))
        w = sb("w", [P, CH, cols])
        up = sb("up", [er, DIM])
        before = sb("before", [P, experts, experts])
        logits = sb("logits", [P, TILES, experts])
        larger = sb("larger", [P, TILES, experts, experts])
        equal = sb("equal", [P, TILES, experts, experts])
        place = sb("place", [P, TILES, experts])
        weight = sb("weight", [P, TILES, experts])
        powers = sb("powers", [P, TILES, experts])
        top = sb("top", [P, TILES])
        z = sb("z", [P, 2, er])
        z_t = sb("z_t", [er, 2, P])
        if expert_bias is not None:
            e_bias = sb("e_bias", [P, experts])
        if out_bias is not None:
            o_bias = sb("o_bias", [P, DIM])
        loads = 16 * (3 + (expert_bias is not None) + (out_bias is not None))
        turn_banks = (bank[0], bank[7])

        with nc.Block() as block:
            @block.sync
            def _(sp):
                sp.dma_start(w[:].rearrange("p c n -> p (c n)"), weights).then_inc(sig.small_in.sem, 16)
                sp.dma_start(up[:], low).then_inc(sig.small_in.sem, 16)
                sp.dma_start(before[:].rearrange("p a b -> p (a b)"), g.t["before%d" % experts]).then_inc(
                    sig.small_in.sem, 16)
                if expert_bias is not None:
                    sp.dma_start(e_bias[:], expert_bias).then_inc(sig.small_in.sem, 16)
                if out_bias is not None:
                    sp.dma_start(o_bias[:], out_bias).then_inc(sig.small_in.sem, 16)
                if last:
                    norm_sync(nc, sp, g)

            @block.gpsimd
            def _(pool):
                if out_bias is not None:
                    pool.wait_ge(sig.small_in.sem, loads)
                    nc.gpsimd.tensor_tensor(x[:], x[:], over(o_bias[:], (1, TILES)), ALU.add).then_inc(
                        sig.prepared.sem, 1)
                norm_pool(nc, pool, g)

            @block.tensor
            def _(pe):
                def features(t, c):
                    return feat[:, SELF, c, 2 * t:2 * t + 2, :].rearrange("p b s -> p (b s)")

                def base(t):
                    if t >= 4:
                        pe.wait_ge(sig.added.sem, sig.added.at(t - 3))
                    for c in range(CH):
                        nc.tensor.matmul(bank[3 + t % 4][:, :], features(t, c), w[:, c, 0:DIM],
                                         start=(c == 0), stop=False)

                pe.wait_ge(sig.small_in.sem, loads)
                for t in range(TILES):
                    for c in range(CH):
                        mm = nc.tensor.matmul(bank[0][:, t * experts:(t + 1) * experts], features(t, c),
                                              w[:, c, DIM:DIM + experts], start=(c == 0), stop=(c == CH - 1))
                mm.then_inc(sig.logits_ready.sem, 1)
                for t in range(TILES):
                    at = t % per_bank * er
                    for c in range(CH):
                        mm = nc.tensor.matmul(bank[1 + t // per_bank][:, at:at + er], features(t, c),
                                              w[:, c, DIM + experts:cols], start=(c == 0), stop=(c == CH - 1))
                mm.then_inc(sig.z_ready.sem, 1)
                base(0)
                base(1)
                for t in range(TILES):
                    pe.wait_ge(sig.z_weighted.sem, t + 1)
                    if t >= 2:
                        pe.wait_ge(sig.z_turned.sem, t - 1)
                    nc.tensor.transpose(turn_banks[t % 2][0:er, 0:P], z[:, t % 2, :], g.ident[:]).then_inc(
                        sig.z_turning.sem, 1)
                    if t + 2 < TILES:
                        base(t + 2)
                    pe.wait_ge(sig.z_turned.sem, t + 1)
                    nc.tensor.matmul(bank[3 + t % 4][:, :], z_t[:, t % 2, :], up[:], start=False,
                                     stop=True).then_inc(sig.y_ready.sem, 1)
                if not last:
                    norm_tensor(nc, pe, g)

            @block.scalar
            def _(act):
                if chosen > 1:
                    act.wait_ge(sig.shifted.sem, sig.shifted.at(1))
                    nc.scalar.activation(powers[:], powers[:], ACT.Exp).then_inc(sig.exp_done.sem, 1)
                for t in range(TILES):
                    act.wait_ge(sig.z_turning.sem, t + 1)
                    nc.scalar.copy(z_t[:, t % 2, :], turn_banks[t % 2][0:er, 0:P]).then_inc(sig.z_turned.sem, 1)
                if not last:
                    norm_scalar(nc, act, g)

            @block.vector
            def _(dve):
                steps = Steps(sig.dve_step)
                dve.wait_ge(sig.small_in.sem, loads)
                dve.wait_ge(sig.logits_ready.sem, 1)
                raw = bank[0][:, 0:TILES * experts].rearrange("p (t e) -> p t e", e=experts)
                if expert_bias is not None:
                    nc.vector.tensor_tensor(logits[:], raw, over(e_bias[:], (1, TILES)), ALU.add).then_inc(
                        steps.count(), 1)
                else:
                    nc.vector.tensor_copy(logits[:], raw).then_inc(steps.count(), 1)
                dve.wait_ge(sig.dve_step.sem, steps.so_far())
                if chosen > 1:
                    nc.vector.tensor_reduce(top[:], logits[:], AX.X, ALU.max).then_inc(steps.count(), 1)
                    dve.wait_ge(sig.dve_step.sem, steps.so_far())
                    nc.vector.tensor_tensor(powers[:], logits[:], over(top[:], (2, experts)),
                                            ALU.subtract).then_inc(sig.shifted.sem, 1)
                other, own = over(logits[:], (2, experts)), over(logits[:], (3, experts))
                nc.vector.tensor_tensor(larger[:], other, own, ALU.is_gt).then_inc(steps.count(), 1)
                nc.vector.tensor_tensor(equal[:], other, own, ALU.is_equal).then_inc(steps.count(), 1)
                dve.wait_ge(sig.dve_step.sem, steps.so_far())
                nc.vector.tensor_tensor(equal[:], equal[:], over(before[:], (1, TILES)), ALU.mult).then_inc(
                    steps.count(), 1)
                dve.wait_ge(sig.dve_step.sem, steps.so_far())
                nc.vector.tensor_tensor(larger[:], larger[:], equal[:], ALU.add).then_inc(steps.count(), 1)
                dve.wait_ge(sig.dve_step.sem, steps.so_far())
                nc.vector.tensor_reduce(place[:], larger[:], AX.X, ALU.add).then_inc(steps.count(), 1)
                dve.wait_ge(sig.dve_step.sem, steps.so_far())
                nc.vector.tensor_scalar(weight[:], place[:], float(chosen), None, ALU.is_lt).then_inc(
                    steps.count(), 1)
                dve.wait_ge(sig.dve_step.sem, steps.so_far())
                if chosen > 1:
                    dve.wait_ge(sig.exp_done.sem, 1)
                    nc.vector.tensor_tensor(weight[:], weight[:], powers[:], ALU.mult).then_inc(steps.count(), 1)
                    dve.wait_ge(sig.dve_step.sem, steps.so_far())
                    nc.vector.tensor_reduce(top[:], weight[:], AX.X, ALU.add).then_inc(steps.count(), 1)
                    dve.wait_ge(sig.dve_step.sem, steps.so_far())
                    nc.vector.reciprocal(top[:], top[:]).then_inc(steps.count(), 1)
                    dve.wait_ge(sig.dve_step.sem, steps.so_far())
                    nc.vector.scalar_tensor_tensor(weight[:], weight[:], scaling, over(top[:], (2, experts)),
                                                   ALU.mult, ALU.mult).then_inc(steps.count(), 1)
                    dve.wait_ge(sig.dve_step.sem, steps.so_far())
                dve.wait_ge(sig.z_ready.sem, 1)

                def weigh(t):
                    if t >= 2:
                        dve.wait_ge(sig.z_turning.sem, t - 1)
                    at = t % per_bank * er
                    nc.vector.tensor_tensor(
                        z[:, t % 2, :].rearrange("p (e r) -> p e r", e=experts),
                        bank[1 + t // per_bank][:, at:at + er].rearrange("p (e r) -> p e r", e=experts),
                        over(weight[:, t, :], (2, rank)), ALU.mult).then_inc(sig.z_weighted.sem, 1)

                weigh(0)
                weigh(1)
                if out_bias is not None:
                    dve.wait_ge(sig.prepared.sem, 1)
                for t in range(TILES):
                    if t + 2 < TILES:
                        weigh(t + 2)
                    dve.wait_ge(sig.y_ready.sem, t + 1)
                    nc.vector.tensor_tensor(x[:, t, :], x[:, t, :], bank[3 + t % 4][:, :], ALU.add).then_inc(
                        sig.added.sem, 1)
                dve.wait_ge(sig.added.sem, sig.added.at(TILES))
                norm_vector(nc, dve, g)



def unlike_attention(nc, g, name, last, eta):
    sig, feat, x, bank = g.sig, g.feat, g.x, g.bank
    per_bank = 512 // P
    with ExitStack() as ctx:
        def sb(what, shape, dt=F32):
            return ctx.enter_context(nc.sbuf_tensor(f"{name}_{what}", shape, dt))
        eta_sb = sb("eta", [P, 1])
        twice = sb("twice", [P, TILES, DIM])
        least = sb("least", [P, TILES])
        probs = sb("probs", [P, TILES, P])
        p_t = sb("p_t", [P, 2, P])
        total = sb("total", [P, TILES])
        factor = sb("factor", [P, TILES])
        turn_banks = (bank[2], bank[3])
        out_banks = bank[4:8]

        def block_of(h):
            return slice(h * SEQ, (h + 1) * SEQ)

        with nc.Block() as block:
            @block.sync
            def _(sp):
                sp.dma_start(eta_sb[:], eta).then_inc(sig.small_in.sem, 16)
                if last:
                    norm_sync(nc, sp, g)

            @block.gpsimd
            def _(pool):
                nc.gpsimd.memset(probs[:], 0.0).then_inc(sig.zeroed.sem, 1)
                nc.gpsimd.tensor_tensor(twice[:], x[:], x[:], ALU.add).then_inc(sig.prepared.sem, 1)
                norm_pool(nc, pool, g)

            @block.tensor
            def _(pe):
                for t in range(TILES):
                    for c in range(CH):
                        f = feat[:, SELF, c, 2 * t:2 * t + 2, :].rearrange("p b s -> p (b s)")
                        mm = nc.tensor.matmul(bank[t // per_bank][:, t % per_bank * P:(t % per_bank + 1) * P], f, f,
                                              start=(c == 0), stop=(c == CH - 1))
                    if t % per_bank == per_bank - 1:
                        mm.then_inc(sig.s_ready.sem, 1)
                for t in range(TILES):
                    pe.wait_ge(sig.exp_done.sem, 2 * (t + 1))
                    if t >= 2:
                        pe.wait_ge(sig.pt_done.sem, sig.pt_done.at(t - 1))
                    nc.tensor.transpose(turn_banks[t % 2][:, 0:P], probs[:, t, :], g.ident[:]).then_inc(
                        sig.pt_ready.sem, 1)
                    if t >= 4:
                        pe.wait_ge(sig.added.sem, sig.added.at(t - 3))
                    pe.wait_ge(sig.pt_done.sem, sig.pt_done.at(t + 1))
                    nc.tensor.matmul(out_banks[t % 4][:, :], p_t[:, t % 2, :], x[:, t, :], start=True,
                                     stop=True).then_inc(sig.y_ready.sem, 1)
                if not last:
                    norm_tensor(nc, pe, g)

            @block.scalar
            def _(act):
                act.wait_ge(sig.zeroed.sem, 1)
                for t in range(TILES):
                    if t % per_bank == 0:
                        act.wait_ge(sig.least.sem, t // per_bank + 1)
                    at = t % per_bank * P
                    for h in range(2):
                        rows = block_of(h)
                        nc.scalar.activation(probs[rows, t, rows],
                                             bank[t // per_bank][rows, at + h * SEQ:at + (h + 1) * SEQ], ACT.Exp,
                                             bias=least[rows, t:t + 1], scale=-1.0,
                                             accum_out=total[rows, t:t + 1]).then_inc(sig.exp_done.sem, 1)
                if not last:
                    norm_scalar(nc, act, g)

            @block.vector
            def _(dve):
                steps = Steps(sig.dve_step)
                for n in range(TILES // per_bank):
                    dve.wait_ge(sig.s_ready.sem, n + 1)
                    for h in range(2):
                        rows = block_of(h)
                        src = bank[n][rows, :].rearrange("p (t k) -> p t k", k=P)[:, :, rows]
                        mm = nc.vector.tensor_reduce(least[rows, n * per_bank:(n + 1) * per_bank], src, AX.X,
                                                     ALU.min)
                    mm.then_inc(sig.least.sem, 1)
                for t in range(TILES):
                    at = t % 2
                    dve.wait_ge(sig.pt_ready.sem, t + 1)
                    if t >= 2:
                        dve.wait_ge(sig.y_ready.sem, t - 1)
                    nc.vector.tensor_copy(p_t[:, at, :], turn_banks[at][:, 0:P]).then_inc(sig.pt_done.sem, 1)
                    if t == 0:
                        dve.wait_ge(sig.exp_done.sem, 2 * TILES)
                        nc.vector.reciprocal(factor[:], total[:]).then_inc(steps.count(), 1)
                        dve.wait_ge(sig.small_in.sem, 16)
                        dve.wait_ge(sig.dve_step.sem, steps.so_far())
                        nc.vector.tensor_scalar(factor[:], factor[:], eta_sb[:, 0:1], None, ALU.mult).then_inc(
                            steps.count(), 1)
                        dve.wait_ge(sig.dve_step.sem, steps.so_far())
                        dve.wait_ge(sig.prepared.sem, 1)
                    dve.wait_ge(sig.y_ready.sem, t + 1)
                    nc.vector.scalar_tensor_tensor(x[:, t, :], out_banks[t % 4][:, :], factor[:, t:t + 1],
                                                   twice[:, t, :], ALU.mult, ALU.add).then_inc(sig.added.sem, 1)
                dve.wait_ge(sig.added.sem, sig.added.at(TILES))
                norm_vector(nc, dve, g)



BOTTLE, ROUTE, SLOTS, TOP, VALUE = 64, 48, 128, 8, 32
TAU_LOW, TAU_HIGH, EARLY_EXIT = 0.5, 2.0, 0.05
GELU_CUBE, GELU_SCALE = 0.044715, math.sqrt(2.0 / math.pi)


def memory_ffn(nc, g, name, last):
    sig, feat, x, bank = g.sig, g.feat, g.x, g.bank
    hidden = P
    four = 512 // SLOTS
    groups = TILES // four
    wcols = BOTTLE + hidden + VALUE + SLOTS
    with ExitStack() as ctx:
        def sb(what, shape, dt=F32):
            return ctx.enter_context(nc.sbuf_tensor(f"{name}_{what}", shape, dt))
        w = sb("w", [P, CH, wcols])
        small = sb("small", [BOTTLE, ROUTE + SLOTS])
        w_vu = sb("w_vu", [VALUE, DIM])
        log_rel = sb("log_rel", [P, SLOTS])
        cols = sb("cols", [P, 5])
        q_t = sb("q_t", [BOTTLE, TOKENS])
        rq_t = sb("rq_t", [ROUTE, TOKENS])
        rk_t = sb("rk_t", [ROUTE, SLOTS])
        down = sb("down", [VALUE, SLOTS])
        slot_values = sb("slot_values", [SLOTS, DIM])
        y = sb("y", [P, TOKENS])
        inner = sb("inner", [P, TOKENS])
        th = sb("th", [P, TOKENS])
        route = sb("route", [P, four, SLOTS])
        rest = sb("rest", [P, four, SLOTS])
        top = sb("top", [P, four, TOP])
        scores = sb("scores", [P, four, SLOTS])
        mx = sb("mx", [P, four])
        probs = sb("probs", [P, groups, four, SLOTS])
        p_t = sb("p_t", [P, groups, four * P])
        total = sb("total", [P, TILES])
        stats = sb("stats", [P, TILES, 6])
        mv = sb("mv", [P, TILES, 2])
        log_var = sb("log_var", [P, TILES])
        log_sum = sb("log_sum", [P, 1])
        ones = sb("ones", [P, P])
        mean = sb("mean", [P, 1])
        u = sb("u", [P, TILES])
        gate = sb("gate", [P, TILES])
        loads = 16 * 5
        w_q = (0, BOTTLE)
        w_u1 = (BOTTLE, BOTTLE + hidden)
        w_vd = (BOTTLE + hidden, BOTTLE + hidden + VALUE)
        values = (BOTTLE + hidden + VALUE, wcols)
        out_banks = (bank[7], bank[0], bank[4])

        with nc.Block() as block:
            @block.sync
            def _(sp):
                sp.dma_start(w[:].rearrange("p c n -> p (c n)"), g.t[name + "_w"]).then_inc(sig.small_in.sem, 16)
                sp.dma_start(small[:], g.t[name + "_small"]).then_inc(sig.small_in.sem, 16)
                sp.dma_start(w_vu[:], g.t[name + "_w_vu"]).then_inc(sig.small_in.sem, 16)
                sp.dma_start(log_rel[:], g.t[name + "_log_rel"]).then_inc(sig.small_in.sem, 16)
                sp.dma_start(cols[:], g.t[name + "_cols"]).then_inc(sig.small_in.sem, 16)
                if last:
                    norm_sync(nc, sp, g)

            @block.gpsimd
            def _(pool):
                for n in range(2):
                    part = slice(n * 512, (n + 1) * 512)
                    pool.wait_ge(sig.y_squared.sem, n + 1)
                    nc.gpsimd.tensor_scalar(inner[:, part], inner[:, part], GELU_CUBE, 1.0, ALU.mult,
                                            ALU.add).then_inc(sig.pool_step.sem, 1)
                    pool.wait_ge(sig.pool_step.sem, n + 1)
                    nc.gpsimd.tensor_tensor(inner[:, part], inner[:, part], y[:, part], ALU.mult).then_inc(
                        sig.inner_done.sem, 1)
                pool.wait_ge(sig.x_read.sem, 1)
                nc.gpsimd.tensor_tensor(x[:], x[:], x[:], ALU.add).then_inc(sig.prepared.sem, 1)
                norm_pool(nc, pool, g)

            @block.tensor
            def _(pe):
                def tokens_at(n, c):
                    return feat[:, SELF, c, n * 8:(n + 1) * 8, :].rearrange("p b s -> p (b s)")

                def project(dst, which, n):
                    for c in range(CH):
                        mm = nc.tensor.matmul(dst, w[:, c, which[0]:which[1]], tokens_at(n, c), start=(c == 0),
                                              stop=(c == CH - 1))
                    return mm

                pe.wait_ge(sig.small_in.sem, loads)
                for n in range(2):
                    project(bank[n][0:BOTTLE, :], w_q, n).then_inc(sig.q_ready.sem, 1)
                nc.tensor.matmul(bank[6][0:ROUTE, 0:SLOTS], small[:, 0:ROUTE], small[:, ROUTE:ROUTE + SLOTS],
                                 start=True, stop=True)
                for c in range(CH):
                    mm = nc.tensor.matmul(bank[6][0:VALUE, SLOTS:2 * SLOTS], w[:, c, w_vd[0]:w_vd[1]],
                                          w[:, c, values[0]:values[1]], start=(c == 0), stop=(c == CH - 1))
                mm.then_inc(sig.k_ready.sem, 1)
                for n in range(2):
                    pe.wait_ge(sig.q_done.sem, sig.q_done.at(n + 1))
                    nc.tensor.matmul(bank[4 + n][0:ROUTE, :], small[:, 0:ROUTE], q_t[:, n * 512:(n + 1) * 512],
                                     start=True, stop=True).then_inc(sig.rq_ready.sem, 1)
                pe.wait_ge(sig.k_done.sem, sig.k_done.at(2))
                nc.tensor.matmul(bank[7][:, :], down[:], w_vu[:], start=True, stop=True).then_inc(
                    sig.v_ready.sem, 1)
                for n in range(2):
                    project(bank[2 + n][:, :], w_u1, n).then_inc(sig.hidden_ready.sem, 1)
                pe.wait_ge(sig.rq_done.sem, groups)
                for n in range(groups):
                    for tt in range(four):
                        t = n * four + tt
                        nc.tensor.matmul(bank[n][:, tt * SLOTS:(tt + 1) * SLOTS], rq_t[:, t * P:(t + 1) * P],
                                         rk_t[:], start=True, stop=True)
                        mm = nc.tensor.matmul(bank[4 + n][:, tt * SLOTS:(tt + 1) * SLOTS],
                                              q_t[:, t * P:(t + 1) * P], small[:, ROUTE:ROUTE + SLOTS],
                                              start=True, stop=True)
                    mm.then_inc(sig.s_ready.sem, 1)
                pe.wait_ge(sig.log_summed.sem, 1)
                nc.tensor.matmul(bank[6][:, TILES:TILES + 1], ones[:], log_sum[:], start=True, stop=True)
                pe.wait_ge(sig.gelu_done.sem, 2)
                for t in range(TILES):
                    mm = nc.tensor.matmul(bank[6][:, t:t + 1], y[:, t * P:(t + 1) * P], cols[:, 1:2], start=True,
                                          stop=True)
                mm.then_inc(sig.learned_ready.sem, 1)
                for n in range(groups):
                    pe.wait_ge(sig.exp_done.sem, four * (n + 1))
                    for tt in range(four):
                        mm = nc.tensor.transpose(bank[2 + n][:, tt * P:(tt + 1) * P], probs[:, n, tt, :],
                                                 g.ident[:])
                    mm.then_inc(sig.pt_ready.sem, 1)
                    pe.wait_ge(sig.pt_done.sem, sig.pt_done.at(n + 1))
                    for tt in range(four):
                        t = n * four + tt
                        if t == 0:
                            pe.wait_ge(sig.v_done.sem, sig.v_done.at(1))
                        if t >= 3:
                            pe.wait_ge(sig.added.sem, sig.added.at(t - 2))
                        nc.tensor.matmul(out_banks[t % 3][:, :], p_t[:, n, tt * P:(tt + 1) * P], slot_values[:],
                                         start=True, stop=True).then_inc(sig.y_ready.sem, 1)
                if not last:
                    norm_tensor(nc, pe, g)

            @block.scalar
            def _(act):
                for n in range(2):
                    act.wait_ge(sig.q_ready.sem, n + 1)
                    nc.scalar.copy(q_t[:, n * 512:(n + 1) * 512], bank[n][0:BOTTLE, :]).then_inc(sig.q_done.sem, 1)
                act.wait_ge(sig.k_ready.sem, 1)
                nc.scalar.copy(rk_t[:], bank[6][0:ROUTE, 0:SLOTS]).then_inc(sig.k_done.sem, 1)
                nc.scalar.copy(down[:], bank[6][0:VALUE, SLOTS:2 * SLOTS]).then_inc(sig.k_done.sem, 1)
                for n in range(2):
                    act.wait_ge(sig.rq_ready.sem, n + 1)
                    nc.scalar.copy(rq_t[:, n * 512:(n + 1) * 512], bank[4 + n][0:ROUTE, :]).then_inc(
                        sig.rq_done.sem, 1)
                act.wait_ge(sig.v_ready.sem, 1)
                nc.scalar.copy(slot_values[:], bank[7][:, :]).then_inc(sig.v_done.sem, 1)
                act.wait_ge(sig.small_in.sem, loads)
                for n in range(2):
                    part = slice(n * 512, (n + 1) * 512)
                    act.wait_ge(sig.hidden_ready.sem, n + 1)
                    nc.scalar.activation(y[:, part], bank[2 + n][:, :], ACT.Identity, bias=cols[:, 0:1])
                    nc.scalar.activation(inner[:, part], bank[2 + n][:, :], ACT.Square,
                                         bias=cols[:, 0:1]).then_inc(sig.y_squared.sem, 1)
                for n in range(2):
                    part = slice(n * 512, (n + 1) * 512)
                    act.wait_ge(sig.inner_done.sem, n + 1)
                    nc.scalar.activation(th[:, part], inner[:, part], ACT.Tanh, scale=GELU_SCALE).then_inc(
                        sig.tanh_done.sem, 1)
                act.wait_ge(sig.x_read.sem, 1)
                nc.scalar.activation(log_var[:], log_var[:], ACT.Ln).then_inc(sig.log_done.sem, 1)
                for n in range(groups):
                    act.wait_ge(sig.shifted.sem, sig.shifted.at(n + 1))
                    for tt in range(four):
                        t = n * four + tt
                        nc.scalar.activation(probs[:, n, tt, :], probs[:, n, tt, :], ACT.Exp,
                                             accum_out=total[:, t:t + 1]).then_inc(sig.exp_done.sem, 1)
                    act.wait_ge(sig.logistic_in.sem, n + 1)
                    nc.scalar.activation(gate[:], gate[:], ACT.Tanh, scale=0.5).then_inc(sig.logistic.sem, 1)
                    act.wait_ge(sig.pt_ready.sem, n + 1)
                    nc.scalar.copy(p_t[:, n, :], bank[2 + n][:, :]).then_inc(sig.pt_done.sem, 1)
                if not last:
                    norm_scalar(nc, act, g)

            @block.vector
            def _(dve):
                steps = Steps(sig.dve_step)

                def settle():
                    dve.wait_ge(sig.dve_step.sem, steps.so_far())

                nc.vector.memset(ones[:], 1.0)
                for t in range(TILES):
                    nc.vector.bn_stats(stats[:, t, :], x[:, t, :]).then_inc(steps.count(), 1)
                settle()
                for t in range(TILES):
                    nc.vector.bn_aggr(mv[:, t, :], stats[:, t, :]).then_inc(steps.count(), 1)
                settle()
                nc.vector.tensor_scalar(log_var[:], mv[:, :, 1], 1.0, None, ALU.add).then_inc(sig.x_read.sem, 1)
                for n in range(2):
                    part = slice(n * 512, (n + 1) * 512)
                    dve.wait_ge(sig.tanh_done.sem, n + 1)
                    nc.vector.scalar_tensor_tensor(y[:, part], th[:, part], 1.0, y[:, part], ALU.add,
                                                   ALU.mult).then_inc(sig.gelu_done.sem, 1)
                dve.wait_ge(sig.log_done.sem, 1)
                nc.vector.tensor_reduce(log_sum[:], log_var[:], AX.X, ALU.add).then_inc(sig.log_summed.sem, 1)
                dve.wait_ge(sig.small_in.sem, loads)

                def choose(n):
                    dve.wait_ge(sig.s_ready.sem, n + 1)
                    rel = over(log_rel[:], (1, four))
                    nc.vector.scalar_tensor_tensor(route[:], bank[n][:, :].rearrange("p (t k) -> p t k", t=four),
                                                   ROUTE ** -0.5, rel, ALU.mult, ALU.add).then_inc(steps.count(), 1)
                    nc.vector.scalar_tensor_tensor(scores[:],
                                                   bank[4 + n][:, :].rearrange("p (t k) -> p t k", t=four),
                                                   BOTTLE ** -0.5, rel, ALU.mult, ALU.add).then_inc(steps.count(), 1)
                    settle()
                    for tt in range(four):
                        nc.vector.max(top[:, tt, :], route[:, tt, :]).then_inc(steps.count(), 1)
                    settle()
                    for tt in range(four):
                        nc.vector.match_replace(rest[:, tt, :], top[:, tt, :], route[:, tt, :], NEG).then_inc(
                            steps.count(), 1)
                    settle()
                    nc.vector.tensor_tensor(rest[:], rest[:], route[:], ALU.is_equal).then_inc(steps.count(), 1)
                    settle()
                    nc.vector.scalar_tensor_tensor(scores[:], rest[:], NEG, scores[:], ALU.mult,
                                                   ALU.add).then_inc(steps.count(), 1)
                    settle()
                    nc.vector.tensor_reduce(mx[:], scores[:], AX.X, ALU.max).then_inc(steps.count(), 1)
                    settle()
                    nc.vector.tensor_tensor(probs[:, n, :, :], scores[:], over(mx[:], (2, SLOTS)),
                                            ALU.subtract).then_inc(sig.shifted.sem, 1)

                def logistic(n):
                    dve.wait_ge(sig.logistic.sem, n + 1)
                    nc.vector.tensor_scalar(gate[:], gate[:], 1.0, 0.5, ALU.add, ALU.mult).then_inc(
                        steps.count(), 1)
                    settle()

                choose(0)
                dve.wait_ge(sig.learned_ready.sem, 1)
                nc.vector.tensor_scalar(mean[:], bank[6][:, TILES:TILES + 1], 1.0 / TOKENS, 1e-6, ALU.mult,
                                        ALU.add).then_inc(steps.count(), 1)
                nc.vector.tensor_scalar(gate[:], bank[6][:, 0:TILES], 0.5, cols[:, 2:3], ALU.mult,
                                        ALU.add).then_inc(sig.logistic_in.sem, 1)
                settle()
                nc.vector.reciprocal(mean[:], mean[:]).then_inc(steps.count(), 1)
                settle()
                nc.vector.tensor_scalar(u[:], log_var[:], mean[:, 0:1], 0.5, ALU.mult, ALU.mult).then_inc(
                    steps.count(), 1)
                settle()
                choose(1)
                logistic(0)
                nc.vector.scalar_tensor_tensor(u[:], gate[:], 2.5, u[:], ALU.mult, ALU.add).then_inc(
                    steps.count(), 1)
                settle()
                nc.vector.tensor_scalar(u[:], u[:], 0.0, 5.0, ALU.max, ALU.min).then_inc(steps.count(), 1)
                settle()
                nc.vector.tensor_scalar(u[:], u[:], TAU_LOW, 1.0 / (TAU_HIGH - TAU_LOW), ALU.subtract,
                                        ALU.mult).then_inc(steps.count(), 1)
                settle()
                nc.vector.tensor_scalar(u[:], u[:], 0.0, 1.0, ALU.max, ALU.min).then_inc(steps.count(), 1)
                settle()
                nc.vector.tensor_scalar(gate[:], u[:], cols[:, 3:4], cols[:, 4:5], ALU.mult, ALU.add).then_inc(
                    sig.logistic_in.sem, 1)
                logistic(1)
                nc.vector.scalar_tensor_tensor(gate[:], gate[:], EARLY_EXIT, gate[:], ALU.is_ge,
                                               ALU.mult).then_inc(steps.count(), 1)
                dve.wait_ge(sig.exp_done.sem, TILES)
                nc.vector.reciprocal(total[:], total[:]).then_inc(steps.count(), 1)
                settle()
                nc.vector.tensor_tensor(gate[:], gate[:], total[:], ALU.mult).then_inc(steps.count(), 1)
                settle()
                dve.wait_ge(sig.prepared.sem, 1)
                for t in range(TILES):
                    dve.wait_ge(sig.y_ready.sem, t + 1)
                    nc.vector.scalar_tensor_tensor(x[:, t, :], out_banks[t % 3][:, :], gate[:, t:t + 1], x[:, t, :],
                                                   ALU.mult, ALU.add).then_inc(sig.added.sem, 1)
                dve.wait_ge(sig.added.sem, sig.added.at(TILES))
                norm_vector(nc, dve, g)



MIX, MIX_RANK, MIX_KEY = 8, 64, 128


def mixed_ffn(nc, g, name, last):
    sig, feat, x, bank = g.sig, g.feat, g.x, g.bank
    pairs = MIX * MIX_RANK // P
    half_b = BATCH // 2
    wcols = 2 * DIM + MIX_KEY
    with ExitStack() as ctx:
        def sb(what, shape, dt=F32):
            return ctx.enter_context(nc.sbuf_tensor(f"{name}_{what}", shape, dt))
        w = sb("w", [P, CH, wcols])
        up = sb("up", [P, pairs, DIM])
        keys = sb("keys", [MIX_KEY, MIX])
        sums = sb("sums", [P, CH, BATCH])
        q_t = sb("q_t", [MIX_KEY, BATCH])
        coef = sb("coef", [BATCH, MIX])
        spread = sb("spread", [BATCH, MIX, MIX_RANK])
        stat = sb("stat", [BATCH, 2])
        rows = sb("rows", [P, pairs, BATCH])
        h_t = sb("h_t", [P, pairs, TOKENS])
        loads = 16 * 3
        down_at, q_at = DIM, 2 * DIM
        y_banks = (bank[4], bank[5], bank[6])

        with nc.Block() as block:
            @block.sync
            def _(sp):
                sp.dma_start(w[:].rearrange("p c n -> p (c n)"), g.t[name + "_w"]).then_inc(sig.small_in.sem, 16)
                sp.dma_start(up[:].rearrange("p j n -> p (j n)"), g.t[name + "_up"]).then_inc(sig.small_in.sem, 16)
                sp.dma_start(keys[:], g.t[name + "_keys"]).then_inc(sig.small_in.sem, 16)
                if last:
                    norm_sync(nc, sp, g)

            @block.gpsimd
            def _(pool):
                norm_pool(nc, pool, g)

            @block.tensor
            def _(pe):
                def down(u):
                    half, j = u // pairs, u % pairs
                    if u >= 4:
                        pe.wait_ge(sig.h_done.sem, u - 3)
                    for c in range(CH):
                        mm = nc.tensor.matmul(
                            bank[u % 4][:, :], w[:, c, down_at + j * P:down_at + (j + 1) * P],
                            feat[:, SELF, c, half * half_b:(half + 1) * half_b, :].rearrange("p b s -> p (b s)"),
                            start=(c == 0), stop=(c == CH - 1))
                    mm.then_inc(sig.h_ready.sem, 1)

                def base(t):
                    if t >= 3:
                        pe.wait_ge(sig.added.sem, sig.added.at(t - 2))
                    for c in range(CH):
                        nc.tensor.matmul(y_banks[t % 3][:, :],
                                         feat[:, SELF, c, 2 * t:2 * t + 2, :].rearrange("p b s -> p (b s)"),
                                         w[:, c, 0:DIM], start=(c == 0), stop=False)

                def mix(t):
                    if t % 4 == 0:
                        pe.wait_ge(sig.h_done.sem, pairs * (t // 4 + 1))
                    for j in range(pairs):
                        mm = nc.tensor.matmul(y_banks[t % 3][:, :], h_t[:, j, t * P:(t + 1) * P], up[:, j, :],
                                              start=False, stop=(j == pairs - 1))
                    mm.then_inc(sig.y_ready.sem, 1)

                pe.wait_ge(sig.small_in.sem, loads)
                down(0)
                down(1)
                pe.wait_ge(sig.sums_done.sem, 1)
                for c in range(CH):
                    mm = nc.tensor.matmul(bank[7][:, 0:BATCH], w[:, c, q_at:q_at + MIX_KEY], sums[:, c, :],
                                          start=(c == 0), stop=(c == CH - 1))
                mm.then_inc(sig.q_ready.sem, 1)
                down(2)
                pe.wait_ge(sig.q_done.sem, sig.q_done.at(1))
                nc.tensor.matmul(bank[7][0:BATCH, BATCH:BATCH + MIX], q_t[:], keys[:], start=True,
                                 stop=True).then_inc(sig.s_ready.sem, 1)
                down(3)
                base(0)
                pe.wait_ge(sig.coef_done.sem, 1)
                for j in range(pairs):
                    mm = nc.tensor.matmul(bank[7][:, (2 + j) * BATCH:(3 + j) * BATCH],
                                          spread[:, 2 * j:2 * j + 2, :].rearrange("b e r -> b (e r)"),
                                          g.ident[0:BATCH, 0:BATCH], start=True, stop=True)
                mm.then_inc(sig.rows_ready.sem, 1)
                base(1)
                base(2)
                mix(0)
                for u in range(4, 8):
                    down(u)
                mix(1)
                mix(2)
                for t in range(3, TILES):
                    base(t)
                    mix(t)
                if not last:
                    norm_tensor(nc, pe, g)

            @block.scalar
            def _(act):
                act.wait_ge(sig.q_ready.sem, 1)
                nc.scalar.mul(q_t[:], bank[7][:, 0:BATCH], 1.0 / SEQ).then_inc(sig.q_done.sem, 1)
                act.wait_ge(sig.shifted.sem, sig.shifted.at(1))
                nc.scalar.activation(coef[:], coef[:], ACT.Exp, scale=MIX_KEY ** -0.5,
                                     accum_out=stat[:, 1:2]).then_inc(sig.exp_done.sem, 1)
                if not last:
                    norm_scalar(nc, act, g)

            @block.vector
            def _(dve):
                steps = Steps(sig.dve_step)
                nc.vector.tensor_reduce(sums[:], feat[:, SELF, :, :, :], AX.X, ALU.add).then_inc(
                    sig.sums_done.sem, 1)
                dve.wait_ge(sig.s_ready.sem, 1)
                raw = bank[7][0:BATCH, BATCH:BATCH + MIX]
                nc.vector.tensor_reduce(stat[:, 0:1], raw, AX.X, ALU.max).then_inc(steps.count(), 1)
                dve.wait_ge(sig.dve_step.sem, steps.so_far())
                nc.vector.tensor_scalar(coef[:], raw, stat[:, 0:1], None, ALU.subtract).then_inc(
                    sig.shifted.sem, 1)
                dve.wait_ge(sig.exp_done.sem, 1)
                nc.vector.reciprocal(stat[:, 1:2], stat[:, 1:2]).then_inc(steps.count(), 1)
                dve.wait_ge(sig.dve_step.sem, steps.so_far())
                nc.vector.tensor_scalar(spread[:], over(coef[:], (2, MIX_RANK)), stat[:, 1:2], None,
                                        ALU.mult).then_inc(sig.coef_done.sem, 1)
                dve.wait_ge(sig.rows_ready.sem, 1)
                nc.vector.tensor_copy(rows[:], bank[7][:, 2 * BATCH:(2 + pairs) * BATCH].rearrange(
                    "p (j b) -> p j b", b=BATCH)).then_inc(steps.count(), 1)
                dve.wait_ge(sig.dve_step.sem, steps.so_far())

                def scale(u):
                    half, j = u // pairs, u % pairs
                    dve.wait_ge(sig.h_ready.sem, u + 1)
                    nc.vector.tensor_tensor(
                        h_t[:, j, half * 512:(half + 1) * 512].rearrange("p (b s) -> p b s", s=SEQ),
                        bank[u % 4][:, :].rearrange("p (b s) -> p b s", s=SEQ),
                        over(rows[:, j, half * half_b:(half + 1) * half_b], (2, SEQ)), ALU.mult).then_inc(
                        sig.h_done.sem, 1)

                def add(t):
                    dve.wait_ge(sig.y_ready.sem, t + 1)
                    nc.vector.tensor_tensor(x[:, t, :], x[:, t, :], y_banks[t % 3][:, :], ALU.add).then_inc(
                        sig.added.sem, 1)

                for u in range(4):
                    scale(u)
                add(0)
                for u in range(4, 8):
                    scale(u)
                for t in range(1, TILES):
                    add(t)
                dve.wait_ge(sig.added.sem, sig.added.at(TILES))
                norm_vector(nc, dve, g)



def build(nc, t, out):
    with ExitStack() as ctx:
        g = Record()
        g.out, g.t = out, t
        g.x = ctx.enter_context(nc.sbuf_tensor("x", [P, TILES, DIM], F32))
        g.feat = ctx.enter_context(nc.sbuf_tensor("feat", [P, 2, CH, BATCH, SEQ], F32))
        g.ident = ctx.enter_context(nc.sbuf_tensor("ident", [P, P], F32))
        g.norm = norm_buffers(nc, ctx)
        g.minus_half = ctx.enter_context(nc.sbuf_tensor("minus_half", [P, TILES], F32))
        g.bank = [ctx.enter_context(nc.psum_tensor(f"bank{n}", [P, 512], F32)) for n in range(8)]
        g.out_written = Signal(ctx.enter_context(nc.semaphore("out_written")), 0)
        loaded = ctx.enter_context(nc.semaphore("loaded"))
        g.sig = Signals(nc, ctx)
        numbers = sorted(sem.num for sem in g.sig.all)
        assert numbers == list(range(numbers[0], numbers[-1] + 1))

        with nc.Block() as block:
            @block.sync
            def _(sp):
                for tile in range(TILES):
                    sp.dma_start(g.x[:, tile, :], t["x"][tile]).then_inc(loaded, 16)
                sp.dma_start(g.feat[:, :, :, :, :].rearrange("p k c b s -> p (k c b s)"), t["feat"]).then_inc(loaded, 16)
                sp.dma_start(g.ident[:], t["ident"]).then_inc(loaded, 16)
                sp.wait_ge(loaded, 16 * (TILES + 2))

            @block.vector
            def _(dve):
                nc.vector.memset(g.minus_half[:], -0.5)

        narrow, wide = ND ** -0.5, HD ** -0.5
        stages = [
            lambda last: wide_attention(nc, g, "l0a", last, t["l0a_qo"], t["l0a_kv"], 1, SELF, wide,
                                        bias=t["l0a_bias"]),
            lambda last: narrow_attention(nc, g, "l0x", last, t["l0x_w"], CTX, narrow),
            lambda last: routed_ffn(nc, g, "l0f", last, t["l0f_w"], t["l0f_up"], 4, 8, 1, 1.0,
                                    expert_bias=t["l0f_bias"]),

            lambda last: unlike_attention(nc, g, "l1a", last, t["l1a_eta"]),
            lambda last: wide_attention(nc, g, "l1x", last, t["l1x_qo"], t["l1x_kv"], 1, "both", wide),
            lambda last: routed_ffn(nc, g, "l1f", last, t["l1f_w"], t["l1f_up"], 8, 16, 2, 2.0,
                                    out_bias=t["l1f_bias"]),

            lambda last: narrow_attention(nc, g, "l2a", last, t["l2a_w"], SELF, narrow, rope=t["l2a_consts"],
                                          out_proj=False),
            lambda last: wide_attention(nc, g, "l2x", last, t["l2x_qo"], t["l2x_kv"], 1, CTX, wide,
                                        mask=t["l2x_mask"], q_norm=t["l2x_qn"], k_norm=t["l2x_kn"]),
            lambda last: memory_ffn(nc, g, "l2f", last),

            lambda last: narrow_attention(nc, g, "l3a", last, t["l3a_w"], SELF, narrow, bias=t["l3a_bias"]),
            lambda last: wide_attention(nc, g, "l3x", last, t["l3x_qo"], t["l3x_kv"], GH, CTX, wide,
                                        bias=t["l3x_bias"], key_mask=t["l3x_mask"]),
            lambda last: mixed_ffn(nc, g, "l3f", last),
        ]
        for stage in stages:
            clear_signals(nc, g)
            stage(stage is stages[-1])



def wide_inputs(arrays, name, wq, wk, wv, wo, kv_heads):
    q = wq.reshape(CH, P, GROUPS, GH, HD).transpose(2, 1, 3, 0, 4).reshape(GROUPS, P, -1)
    o = wo.reshape(GROUPS, GH, HD, DIM).transpose(0, 2, 1, 3).reshape(GROUPS, P, -1)
    arrays[name + "_qo"] = np.concatenate([q, o], axis=2)
    n = wk.shape[1] // (kv_heads * HD)
    kv = [w.reshape(CH, P, n, kv_heads * HD).transpose(2, 1, 0, 3).reshape(n, P, -1) for w in (wk, wv)]
    arrays[name + "_kv"] = np.concatenate(kv, axis=2)


def distance_bias():
    slopes = (2.0 ** (-8.0 / HEADS)) ** np.arange(1, HEADS + 1, dtype=np.float32)
    rel = np.arange(SEQ)[:, None] - np.arange(SEQ)[None, :]
    b = -slopes[:, None, None].astype(np.float32) * np.sqrt(np.maximum(rel, 0).astype(np.float32))
    b = np.where(rel[None] >= 0, b, NEG).astype(np.float32)
    b = b.reshape(GROUPS, 2, 2, SEQ, SEQ).transpose(0, 2, 3, 1, 4)
    b = np.repeat(b[:, :, :, :, None, :], 2, axis=4)
    return np.ascontiguousarray(b.reshape(GROUPS, P, 2 * 2 * SEQ), dtype=np.float32)


def narrow_inputs(wq, wk, wv, wo):
    q = wq.reshape(CH, P, KV, NR, ND).transpose(1, 0, 3, 2, 4).reshape(P, -1)
    kv = [m.reshape(CH, P, P).transpose(1, 0, 2).reshape(P, -1) for m in (wk, wv)]
    parts = [q] + kv
    if wo is not None:
        parts.append(wo.reshape(KV, NR, ND, DIM).transpose(0, 2, 1, 3).reshape(P, -1))
    return np.concatenate(parts, axis=1)


def linear_bias():
    slopes = (2.0 ** (-2.0 ** (-(math.log2(HEADS) - 3)))) ** np.arange(1, HEADS + 1, dtype=np.float64)
    rel = (np.arange(SEQ)[None, :] - np.arange(SEQ)[:, None]).astype(np.float32)
    b = slopes.astype(np.float32)[:, None, None] * rel[None]
    b = np.where(rel[None] <= 0, b, np.float32(NEG)).astype(np.float32)
    b = b.reshape(KV, NR, SEQ, SEQ).transpose(2, 1, 0, 3).reshape(SEQ, -1)
    return np.concatenate([b, b], axis=0)


def rope_tables():
    half = ND // 2
    turn = np.zeros((P, P), np.float32)
    for h in range(KV):
        for d in range(half):
            turn[h * ND + half + d, h * ND + d] = -1.0
            turn[h * ND + d, h * ND + half + d] = 1.0
    inv = (1.0 / 10000.0 ** (np.arange(0, ND, 2, dtype=np.float32) / ND)).astype(np.float32)
    ang = np.arange(SEQ, dtype=np.float32)[None, :] * inv[:, None]
    ang = np.tile(np.concatenate([ang, ang], axis=0), (KV, 1))
    return turn, np.cos(ang).astype(np.float32), np.sin(ang).astype(np.float32)


def chunked(*parts):
    m = np.concatenate(parts, axis=1)
    return m.reshape(CH, P, m.shape[1]).transpose(1, 0, 2).reshape(P, -1)


def ffn_inputs(a, i):
    def rows(v, n=P):
        return np.broadcast_to(v.reshape(1, -1), (n, v.size))
    for e in (4, 8):
        a["before%d" % e] = rows(np.tril(np.ones((e, e), np.float32), -1))
    a["l0f_w"] = chunked(i["L0_ffn_W_up"].T, i["L0_ffn_gate_w"].T, i["L0_ffn_lora_A"].reshape(-1, DIM).T)
    a["l0f_up"] = i["L0_ffn_lora_B"].transpose(0, 2, 1).reshape(-1, DIM)
    a["l0f_bias"] = rows(i["L0_ffn_expert_bias"])
    a["l1a_eta"] = rows(i["L1_attn_eta"])
    a["l1f_w"] = chunked(i["L1_ffn_W_base"].T, i["L1_ffn_W_router"].T, i["L1_ffn_A"].reshape(-1, DIM).T)
    a["l1f_up"] = i["L1_ffn_B"].transpose(0, 2, 1).reshape(-1, DIM)
    a["l1f_bias"] = rows(i["L1_ffn_b_base"])
    a["l2f_w"] = chunked(i["L2_ffn_Wq"].T, i["L2_ffn_Wu1"].T, i["L2_ffn_Wvd"].T, i["L2_ffn_aux_values"].T)
    a["l2f_small"] = np.concatenate([i["L2_ffn_Wr"].T, i["L2_ffn_aux_keys"].T], axis=1)
    a["l2f_w_vu"] = i["L2_ffn_Wvu"].T
    a["l2f_log_rel"] = rows(i["L2_ffn_log_rel"])
    a["l2f_cols"] = np.concatenate([i["L2_ffn_bu1"].reshape(P, 1), i["L2_ffn_Wu2"].reshape(P, 1)] +
                                   [rows(i["L2_ffn_" + n]) for n in ("bu2", "gate_w1", "gate_bias")], axis=1)
    down = i["L3_ffn_lora_down"].transpose(1, 0, 2).reshape(DIM, -1)
    a["l3f_w"] = chunked(i["L3_ffn_W_org"].T, down, i["L3_ffn_Wq"].T)
    a["l3f_up"] = chunked(i["L3_ffn_lora_up"].reshape(-1, DIM))
    a["l3f_keys"] = i["L3_ffn_lora_keys"].T


def lay_out(i):
    i = {k: np.asarray(v) for k, v in i.items()}
    a = {}
    x = i["x"].reshape(TOKENS, DIM)
    a["x"] = x.reshape(TILES, P, DIM)
    feats = [f.reshape(BATCH, SEQ, CH, P).transpose(3, 2, 0, 1) for f in (i["ctx_4096"], i["x"])]
    a["feat"] = np.stack(feats, axis=1).reshape(P, -1)
    a["ident"] = np.eye(P, dtype=np.float32)
    w = i["L0_attn_w_qkv"]
    wide_inputs(a, "l0a", w[:, :HEADS * HD], w[:, HEADS * HD:HEADS * HD + GROUPS * HD],
                w[:, HEADS * HD + GROUPS * HD:], i["L0_attn_w_o"], 1)
    a["l0a_bias"] = distance_bias()
    wide_inputs(a, "l1x", i["L1_xattn_Wq"], i["L1_xattn_Wk"], i["L1_xattn_Wv"], i["L1_xattn_Wo"], 1)
    wide_inputs(a, "l2x", i["L2_xattn_q_proj_w"].T, i["L2_xattn_k_proj_w"].T, i["L2_xattn_v_proj_w"].T,
                i["L2_xattn_o_proj_w"].T, 1)
    a["l2x_mask"] = i["mask_1x1xSxS2_ff0"].reshape(SEQ, SEQ)
    a["l2x_qn"] = i["L2_xattn_q_norm_w"].reshape(P, 1)
    a["l2x_kn"] = i["L2_xattn_k_norm_w"].reshape(P, 1)
    wide_inputs(a, "l3x", i["L3_xattn_Wq"], i["L3_xattn_Wk"], i["L3_xattn_Wv"], i["L3_xattn_Wo"], GH)
    b = i["fside_Bx32xSxS2_0"].reshape(UNITS, 2, 2, GROUPS, 2, 2, SEQ, SEQ)
    a["l3x_bias"] = b.transpose(3, 5, 6, 0, 1, 4, 2, 7).reshape(GROUPS, P, -1)
    m = i["mask_BxSxS2_bk0"].transpose(1, 0, 2)
    a["l3x_mask"] = np.concatenate([m, m], axis=0)
    a["head_of"] = np.repeat(np.eye(KV, dtype=np.float32), ND, axis=0)
    a["half_of"] = np.repeat(np.eye(2, dtype=np.float32), SEQ, axis=0)
    a["l0x_w"] = narrow_inputs(i["L0_xattn_Wq"], i["L0_xattn_Wk"], i["L0_xattn_Wv"], i["L0_xattn_Wo"])
    a["l2a_w"] = narrow_inputs(i["L2_attn_wq"], i["L2_attn_wk"], i["L2_attn_wv"], None)
    turn, cos, sin = rope_tables()
    bq = i["L2_attn_bq"].reshape(KV, NR, ND).transpose(0, 2, 1).reshape(P, NR)
    bv = np.broadcast_to(i["L2_attn_bv"].reshape(1, P), (P, P))
    a["l2a_consts"] = np.concatenate([turn, cos, sin, bq, i["L2_attn_bk"].reshape(P, 1), bv], axis=1)
    w = i["L3_attn_Wqkv"]
    wk, wv = (np.tile(w[:, DIM + n * ND:DIM + (n + 1) * ND], (1, KV)) for n in range(2))
    a["l3a_w"] = narrow_inputs(w[:, :DIM], wk, wv, i["L3_attn_Wo"])
    a["l3a_bias"] = linear_bias()
    ffn_inputs(a, i)
    return {k: np.ascontiguousarray(v) for k, v in a.items()}


def kernel(**inputs):
    import concourse.bacc as bacc
    from concourse.bass_utils import run_bass_kernel_spmd

    arrays = lay_out(inputs)
    nc = bacc.Bacc("TRN2", target_bir_lowering=False, num_devices=1)
    t = {k: nc.dram_tensor("in_" + k, v.shape, mybir.dt.from_np(v.dtype), kind="ExternalInput").ap()
         for k, v in arrays.items()}
    out = nc.dram_tensor("out_0_dram", (TOKENS, DIM), F32, kind="ExternalOutput").ap()
    build(nc, t, out)
    r = run_bass_kernel_spmd(nc, [{"in_" + k: v for k, v in arrays.items()}], core_ids=[0])
    return r.results[0]["out_0_dram"].reshape(BATCH, SEQ, DIM)
```

```python
from contextlib import ExitStack
import math

import numpy as np

import concourse.bass as bass
from concourse import mybir

F32 = mybir.dt.float32
F32R = mybir.dt.float32r
U8 = mybir.dt.uint8
ALU = mybir.AluOpType
ACT = mybir.ActivationFunctionType
AX = mybir.AxisListType

P = 128
BATCH, SEQ, DIM = 16, 64, 512
TOKENS = BATCH * SEQ
CH = DIM // P
TILES = TOKENS // P
HEADS = 32
HD = 128
ND = DIM // HEADS
GH = 4
GROUPS = HEADS // GH
UB = 4
UNITS = BATCH // UB
HOME = 5136
BODY = 2 * UNITS
UT = UB * SEQ
KV = 8
NR = HEADS // KV
NEG = -1.0e30
LN_EPS = 1e-5
HIGH, LOW = 0, 1
CTX, SELF = 0, 1
CREDIT = 8


class Record:
    pass


class Signal:

    def __init__(self, sem, begin):
        self.sem, self.begin = sem, begin

    def at(self, n):
        return self.begin + n


class Signals:

    def __init__(self, nc, ctx):
        self.all, self.credited = [], []

        def plain(name):
            self.all.append(ctx.enter_context(nc.semaphore(name)))
            return Signal(self.all[-1], 0)

        def released(name):
            sig = plain(name)
            self.credited.append(sig.sem)
            return Signal(sig.sem, CREDIT)

        self.q_done = released("q_done")
        self.k_done = released("k_done")
        self.v_done = released("v_done")
        self.s_read = released("s_read")
        self.shifted = released("shifted")
        self.pt_done = released("pt_done")
        self.o_done = released("o_done")
        self.added = released("added")
        self.staged = released("staged")
        self.kd_done = released("kd_done")
        self.keys_taken = released("keys_taken")
        self.squared = released("squared")
        self.attn_taken = released("attn_taken")
        self.wide_a = plain("wide_a")
        self.wide_b = plain("wide_b")
        self.qo_in = plain("qo_in")
        self.wq_high = plain("wq_high")
        self.wo_high = plain("wo_high")
        self.q_split = plain("q_split")
        self.o_split = plain("o_split")
        self.own_high = plain("own_high")
        self.own_low = plain("own_low")
        self.o_high = plain("o_high")
        self.kv_raw_in = plain("kv_raw_in")
        self.kv_high = plain("kv_high")
        self.kv_low = plain("kv_low")
        self.context_high = plain("context_high")
        self.context_low = plain("context_low")
        self.kv_in = plain("kv_in")
        self.small_in = plain("small_in")
        self.q_ready = plain("q_ready")
        self.k_ready = plain("k_ready")
        self.v_ready = plain("v_ready")
        self.s_ready = plain("s_ready")
        self.exp_done = plain("exp_done")
        self.p_ready = plain("p_ready")
        self.pt_ready = plain("pt_ready")
        self.o_ready = plain("o_ready")
        self.y_ready = plain("y_ready")
        self.dve_step = plain("dve_step")
        self.row_max = plain("row_max")
        self.row_sum = plain("row_sum")
        self.rope_step = plain("rope_step")
        self.act_step = plain("act_step")
        self.pool_step = plain("pool_step")
        self.rms_done = plain("rms_done")
        self.rms_sum = plain("rms_sum")
        self.rms_var = plain("rms_var")
        self.rms_power = plain("rms_power")
        self.norm_step = plain("norm_step")
        self.var_ready = plain("var_ready")
        self.rstd_ready = plain("rstd_ready")
        self.normed = plain("normed")
        self.turned = plain("turned")
        self.turn_read = plain("turn_read")
        self.keys_turned = plain("keys_turned")
        self.rotated = plain("rotated")
        self.attn_turned = plain("attn_turned")
        self.prepared = plain("prepared")
        self.logits_ready = plain("logits_ready")
        self.z_ready = plain("z_ready")
        self.z_weighted = plain("z_weighted")
        self.z_turning = plain("z_turning")
        self.z_turned = plain("z_turned")
        self.zeroed = plain("zeroed")
        self.least = plain("least")
        self.y_squared = plain("y_squared")
        self.inner_done = plain("inner_done")
        self.tanh_done = plain("tanh_done")
        self.gelu_done = plain("gelu_done")
        self.x_read = plain("x_read")
        self.log_done = plain("log_done")
        self.log_summed = plain("log_summed")
        self.rq_ready = plain("rq_ready")
        self.rq_done = plain("rq_done")
        self.hidden_ready = plain("hidden_ready")
        self.learned_ready = plain("learned_ready")
        self.logistic_in = plain("logistic_in")
        self.logistic = plain("logistic")
        self.h_ready = plain("h_ready")
        self.h_done = plain("h_done")
        self.sums_done = plain("sums_done")
        self.coef_done = plain("coef_done")
        self.rows_ready = plain("rows_ready")


class Stage:

    def __init__(self, home, loads, run):
        self.home, self.loads, self.run = home, loads, run
        self.arrived = None


def load_ahead(sp, g):
    for there, here in g.ahead.loads:
        sp.dma_start(there, here).then_inc(g.home_in[g.ahead.home], 16)


class Steps:

    def __init__(self, signal, before=0):
        self.of, self.before, self.n = signal, before, 0

    def count(self):
        self.n += 1
        return self.of.sem

    def so_far(self):
        return self.of.at(self.before + self.n)


def over(ap, *dims):
    for axis, size in dims:
        ap = ap.unsqueeze(axis)
        shape = list(ap.shape)
        shape[axis] = size
        ap = ap.to_broadcast(shape)
    return ap


def clear_signals(nc, g):
    with nc.Block() as block:
        @block.sync
        def _(sp):
            numbers = sorted(sem.num for sem in g.sig.all)
            sp.sem_clear(range(numbers[0], numbers[-1] + 1))
            for sem in g.sig.credited:
                sp.sem_inc(sem, CREDIT)



def norm_buffers(nc, ctx):
    norm = Record()
    norm.stats = ctx.enter_context(nc.sbuf_tensor("ln_stats", [P, TILES, 6], F32))
    norm.mv = ctx.enter_context(nc.sbuf_tensor("ln_mean_var", [P, TILES, 2], F32))
    norm.var = ctx.enter_context(nc.sbuf_tensor("ln_var", [P, TILES], F32))
    norm.rstd = ctx.enter_context(nc.sbuf_tensor("ln_rstd", [P, TILES], F32))
    return norm


def norm_tile(nc, dve, g, t, added, scale=True):
    n, step = g.norm, g.sig.norm_step
    dve.wait_ge(g.sig.added.sem, g.sig.added.at(added))
    nc.vector.bn_stats(n.stats[:, t, :], g.x[:, t, :]).then_inc(step.sem, 1)
    dve.wait_ge(step.sem, step.at(2 * t + 1))
    nc.vector.bn_aggr(n.mv[:, t, :], n.stats[:, t, :]).then_inc(step.sem, 1)
    dve.wait_ge(step.sem, step.at(2 * t + 2))
    nc.vector.tensor_scalar(n.var[:, t:t + 1], n.mv[:, t, 1:2], LN_EPS, None, ALU.add).then_inc(
        g.sig.var_ready.sem, 1)
    if t and scale:
        norm_scale(nc, dve, g, t - 1)


def norm_scale(nc, dve, g, t):
    n = g.norm
    dve.wait_ge(g.sig.rstd_ready.sem, g.sig.rstd_ready.at(t + 1))
    nc.vector.tensor_scalar(g.x[:, t, :], g.x[:, t, :], n.mv[:, t, 0:1], n.rstd[:, t:t + 1],
                            ALU.subtract, ALU.mult).then_inc(g.sig.normed.sem, 1)


def norm_pool(nc, pool, g):
    for t in range(TILES):
        pool.wait_ge(g.sig.var_ready.sem, g.sig.var_ready.at(t + 1))
        nc.gpsimd.tensor_tensor(g.norm.rstd[:, t:t + 1], g.norm.var[:, t:t + 1], g.minus_half[:, 0:1],
                                ALU.pow).then_inc(g.sig.rstd_ready.sem, 1)


def norm_tensor(nc, pe, g, banks):
    for t in range(TILES):
        pe.wait_ge(g.sig.normed.sem, g.sig.normed.at(t + 1))
        if t >= 2:
            pe.wait_ge(g.sig.turn_read.sem, g.sig.turn_read.at(t - 1))
        bank = g.bank[banks[t % 2]]
        for c in range(CH):
            last = nc.tensor.transpose(bank[:, c * P:(c + 1) * P], g.x[:, t, c * P:(c + 1) * P], g.ident[:])
        last.then_inc(g.sig.turned.sem, 1)


def norm_scalar(nc, act, g, banks):
    for t in range(TILES):
        act.wait_ge(g.sig.turned.sem, g.sig.turned.at(t + 1))
        src = g.bank[banks[t % 2]][:, :].rearrange("p (c b s) -> p c b s", c=CH, b=2)
        nc.scalar.copy(g.feat[:, SELF, :, 2 * t:2 * t + 2, :], src).then_inc(g.sig.turn_read.sem, 1)


def norm_sync(nc, sp, g):
    for t in range(TILES):
        sp.wait_ge(g.sig.normed.sem, g.sig.normed.at(t + 1))
        sp.dma_start(g.out[t * P:(t + 1) * P, :], g.x[:, t, :]).then_inc(g.out_written.sem, 16)
    sp.wait_ge(g.out_written.sem, 16 * TILES)



def wide_attention(nc, g, name, last, w_qo, w_kv, kv_heads, keys, scale, bias=None, mask=None,
                   q_norm=None, k_norm=None, key_mask=None):
    sig, feat, x, bank = g.sig, g.feat, g.x, g.bank
    both, rms = keys == "both", q_norm is not None
    klen = 2 * SEQ if both else SEQ
    halves = 2 if both else 1
    kbanks = 2 if kv_heads == GH else 1
    kdim = kv_heads * HD
    kv_split = kv_heads == GH
    rounds = GROUPS // 2
    wq_cols = CH * GH * HD
    with ExitStack() as ctx:
        def sb(what, shape, dt=F32):
            return ctx.enter_context(nc.sbuf_tensor(f"{name}_{what}", shape, dt))
        raw = g.raw
        wqo = sb("wqo", [P, 2, wq_cols + GH * DIM], F32R)
        if kv_split:
            own = sb("own", [P, 2, CH, UB, SEQ], F32R)
            context = sb("context", [P, 2, CH, UB, SEQ], F32R)
            kv_parts = sb("kv_parts", [P, 2, CH * kdim * 2], F32R)
        else:
            own = sb("own", [P, 2, CH, BATCH, SEQ], F32R)
        kv_cols = CH * kdim * 2
        homes_full = 2 * kv_cols > HOME
        spare = kv_cols if homes_full else 2 * kv_cols
        if homes_full:
            wkv = (g.home[:, 0:kv_cols], None)
        else:
            wkv = (g.home[:, 0:kv_cols], g.home[:, kv_cols:2 * kv_cols])
        q_t = sb("q_t", [P, GH, UT])
        if both:
            k_t = sb("k_t", [P, UNITS, UB * klen])
            v = sb("v", [P, UNITS, UB, HD])
        else:
            k_t = sb("k_t", [P, kv_heads, UT])
            v = sb("v", [P, 2, 2, kdim])
        shifted = sb("shifted", [P, halves, 512])
        probs = sb("probs", [P, halves, 512])
        p_t = sb("p_t", [P, halves, 512])
        o_t = sb("o_t", [P, 2, GH, UB, SEQ], F32R)
        ngr = 512 // klen
        mx = sb("mx", [P, halves, ngr])
        total = sb("total", [P, halves, ngr])
        recip = sb("recip", [P, halves, ngr])
        if bias is not None:
            bias_cols = bias.shape[2]
            if homes_full:
                bias_sb = g.other[:, 0:2 * bias_cols].rearrange("p (n c) -> p n c", n=2)
            else:
                bias_sb = sb("bias", [P, 2, bias_cols])
        if mask is not None:
            mask_sb = sb("mask", [P, SEQ])
        if key_mask is not None:
            km_u8 = probs[:, 0, 0:BATCH * SEQ // 4].bitcast(U8).rearrange("p (b s) -> p b s", b=BATCH)
            km_one, km_neg = (h[:, spare:spare + BATCH * SEQ].rearrange("p (b s) -> p b s", b=BATCH)
                              for h in (g.home, g.other))
        if rms:
            q_sq = sb("q_sq", [P, UB, GH, SEQ])
            q_w = sb("q_w", [P, 1])
            k_w = sb("k_w", [P, 1])
            mean_col = sb("mean_col", [P, 1])
            k_rows = sb("k_rows", [P, 2, HD])
            k_junk = sb("k_junk", [P, HD])
            ssq = sb("ssq", [P, 2])
            k_var = sb("k_var", [P, 2])
            k_rstd = sb("k_rstd", [P, 2])
            q_var = sb("q_var", [P, 8])
            q_rstd = sb("q_rstd", [P, 8])

        def landed(n):
            return sig.wide_a if n % 2 == 0 else sig.wide_b
        small_loads = 16 * (2 * (mask is not None) + (key_mask is not None) + 2 * rms)
        score_bank_free = sig.s_read if (bias is not None or rms) else sig.shifted
        before_exp = 2 if (key_mask is not None or rms) else 1
        after_exp = 3 if key_mask is not None else 2
        score_banks = (bank[4], bank[3])
        value_bank = bank[2] if both else bank[3]
        own_slot = not both and not kv_split
        per_group = 16 * (own_slot + (bias is not None))
        parts = ((HIGH, HIGH), (HIGH, LOW), (LOW, HIGH))

        def pipeline(engine, step):
            step((0, 0), None)
            with engine.Fori(0, rounds - 1) as i:
                for n in range(1, BODY):
                    step((i, n), (i, n - 1))
                step((i + 1, 0), (i, BODY - 1))
            for n in range(1, BODY):
                step((rounds - 1, n), (rounds - 1, n - 1))
            step(None, (rounds - 1, BODY - 1))

        def k_round(i, n):
            return UNITS * i + n if both else BODY * i + n

        def o_part(which, b2):
            return o_t[:, which, :, :, :].rearrange("p h (bp b2) s -> p bp b2 h s", b2=2)[:, :, b2, :, :]

        def o_bank(b2):
            return bank[6 + b2][:, :].rearrange("p (bp h s) -> p bp h s", bp=2, h=GH)

        def q_half(j):
            return slice(j * wq_cols // 2, (j + 1) * wq_cols // 2)

        def units_batches(u):
            return slice(UB * u, UB * u + UB)

        def own_part(which, n):
            if kv_split:
                return own[:, which, :, :, :]
            return own[:, which, :, units_batches(n % UNITS), :]

        def kv_part(which, value, c):
            at = (value * CH + c) * kdim
            return kv_parts[:, which, at:at + kdim]

        with nc.Block() as block:
            @block.sync
            def _(sp):
                if mask is not None:
                    sp.dma_start(mask_sb[0:SEQ, :], mask).then_inc(sig.small_in.sem, 16)
                    sp.dma_start(mask_sb[SEQ:P, :], mask).then_inc(sig.small_in.sem, 16)
                if key_mask is not None:
                    sp.dma_start(km_u8, key_mask).then_inc(sig.small_in.sem, 16)
                if rms:
                    sp.dma_start(q_w[:], q_norm).then_inc(sig.small_in.sem, 16)
                    sp.dma_start(k_w[:], k_norm).then_inc(sig.small_in.sem, 16)

                def load(n, group, keys_too=True):
                    if own_slot and keys_too:
                        sp.dma_start(wkv[n % 2], w_kv[group]).then_inc(landed(n).sem, 16)
                    if bias is not None:
                        sp.dma_start(bias_sb[:, n % 2, :], bias[group]).then_inc(landed(n).sem, 16)

                def load_q(group):
                    sp.dma_start(raw[:], w_qo[group][:, 0:wq_cols]).then_inc(sig.qo_in.sem, 16)

                def load_o(group):
                    sp.wait_ge(sig.q_split.sem, sig.q_split.at(2 * group + 2))
                    sp.dma_start(raw[:], w_qo[group][:, wq_cols:2 * wq_cols]).then_inc(sig.qo_in.sem, 16)

                def load_kv(group):
                    sp.wait_ge(sig.kv_low.sem, sig.kv_low.at(2 * group))
                    sp.dma_start(wkv[0], w_kv[group]).then_inc(sig.kv_raw_in.sem, 16)

                for n in range(2):
                    load(n, n, keys_too=n > 0)
                load_o(0)
                if g.x_pending:
                    for tile in range(TILES):
                        sp.dma_start(g.x[:, tile, :], g.t["x"][tile]).then_inc(g.x_in, 16)
                    sp.dma_start(feat[:, CTX, :, :, :].rearrange("p c b s -> p (c b s)"), g.t["feat"][0]).then_inc(
                        g.context_in, 16)
                if not homes_full:
                    load_ahead(sp, g)
                with sp.Fori(0, rounds - 1) as i:
                    for n in range(2):
                        if kv_split:
                            load_kv(2 * i + n + 1)
                        sp.wait_ge(sig.o_split.sem, sig.o_split.at(2 * i + n + 1))
                        load_q(2 * i + n + 1)
                        if both and n == 0:
                            sp.wait_ge(sig.k_done.sem, sig.k_done.at(UNITS * i + UNITS))
                            sp.wait_ge(sig.v_done.sem, sig.v_done.at(UNITS * i + UNITS))
                            sp.dma_start(wkv[0], w_kv[i + 1]).then_inc(sig.kv_in.sem, 16)
                        load_o(2 * i + n + 1)
                        if per_group:
                            sp.wait_ge(sig.y_ready.sem, sig.y_ready.at(2 * (BODY * i + UNITS * (n + 1))))
                            load(n, 2 * i + 2 + n)
                if kv_split:
                    load_kv(GROUPS - 1)
                sp.wait_ge(sig.o_split.sem, sig.o_split.at(GROUPS - 1))
                load_q(GROUPS - 1)
                load_o(GROUPS - 1)
                if homes_full:
                    sp.wait_ge(sig.v_done.sem, sig.v_done.at(kbanks * rounds * BODY))
                    load_ahead(sp, g)
                if g.x_pending:
                    sp.wait_ge(g.context_in, 16)
                if last:
                    norm_sync(nc, sp, g)

            @block.gpsimd
            def _(pool):
                def split_q_low(i, slot):
                    group = 2 * i + slot
                    for j in range(2):
                        pool.wait_ge(sig.wq_high.sem, sig.wq_high.at(2 * group + j + 1))
                        part = q_half(j)
                        nc.gpsimd.tensor_tensor(wqo[:, LOW, part], raw[:, part], wqo[:, HIGH, part],
                                                ALU.subtract).then_inc(sig.q_split.sem, 1)

                def split_o_low(i, slot):
                    group = 2 * i + slot
                    pool.wait_ge(sig.wo_high.sem, sig.wo_high.at(group + 1))
                    nc.gpsimd.tensor_tensor(wqo[:, LOW, wq_cols:], raw[:], wqo[:, HIGH, wq_cols:],
                                            ALU.subtract).then_inc(sig.o_split.sem, 1)

                def rms_powers(i, n):
                    uu = BODY * i + n
                    pool.wait_ge(sig.rms_var.sem, sig.rms_var.at(2 * uu + 1))
                    nc.gpsimd.tensor_tensor(k_rstd[:], k_var[:], g.minus_half[:, 0:2], ALU.pow).then_inc(
                        sig.rms_power.sem, 1)
                    pool.wait_ge(sig.rms_var.sem, sig.rms_var.at(2 * uu + 2))
                    nc.gpsimd.tensor_tensor(q_rstd[:], q_var[:], g.minus_half[:, 0:8], ALU.pow).then_inc(
                        sig.rms_power.sem, 1)

                with pool.Fori(0, rounds) as i:
                    for n in range(BODY):
                        if n % UNITS == 0 and not rms:
                            split_q_low(i, n // UNITS)
                        if rms:
                            rms_powers(i, n)
                        if n % UNITS == 0:
                            split_o_low(i, n // UNITS)
                norm_pool(nc, pool, g)

            @block.tensor
            def _(pe):
                def group_in(i, slot):
                    ahead = 16 if slot == 0 and own_slot else 0
                    if per_group > ahead or not isinstance(i, int) or i > 0 or slot:
                        pe.wait_ge(landed(slot).sem, landed(slot).at(per_group * (i + 1) - ahead))

                def project_q(i, n, heads=range(GH)):
                    uu, slot, u = BODY * i + n, n // UNITS, n % UNITS
                    if heads[0] == 0:
                        if u == 0 and per_group and not rms:
                            group_in(i, slot)
                        split_units = uu if kv_split else u
                        pe.wait_ge(sig.own_low.sem, sig.own_low.at(split_units + 1))
                    for h in heads:
                        j, hh = h // 2, h % 2
                        if hh == 0:
                            if u == 0:
                                pe.wait_ge(sig.q_split.sem, sig.q_split.at(4 * i + 2 * slot + j + 1))
                            pe.wait_ge(sig.q_done.sem, sig.q_done.at(2 * uu - 1 + j))
                        for c in range(CH):
                            at = (h * CH + c) * HD
                            for n_part, (wp, fp) in enumerate(parts):
                                mm = nc.tensor.matmul(
                                    bank[j][:, hh * UT:(hh + 1) * UT].rearrange("p (b s) -> p b s", b=UB),
                                    wqo[:, wp, at:at + HD], own_part(fp, n)[:, c, :, :],
                                    start=(c == 0 and n_part == 0), stop=(c == CH - 1 and n_part == 2))
                        if hh == 1:
                            mm.then_inc(sig.q_ready.sem, 1)

                def project_k(i, n):
                    slot, u = (0 if both else n // UNITS), n % UNITS
                    kr = k_round(i, n)
                    if both and n == 0 and not isinstance(i, int):
                        pe.wait_ge(sig.kv_in.sem, sig.kv_in.at(16 * i))
                    if rms:
                        pe.wait_ge(sig.keys_taken.sem, sig.keys_taken.at(kr))
                    else:
                        pe.wait_ge(sig.k_done.sem, sig.k_done.at(kbanks * kr))
                    if both or kbanks == 2:
                        pe.wait_ge(sig.v_done.sem, sig.v_done.at(kbanks * kr))
                    if rms:
                        if u == 0:
                            group_in(i, slot)
                        for tt in range(2):
                            for c in range(CH):
                                mm = nc.tensor.matmul(
                                    bank[2][:, tt * HD:(tt + 1) * HD],
                                    feat[:, keys, c, UB * u + 2 * tt:UB * u + 2 * tt + 2, :],
                                    wkv[slot][:, c * HD:(c + 1) * HD], start=(c == 0), stop=(c == CH - 1))
                        mm.then_inc(sig.k_ready.sem, 1)
                        return
                    if kv_split:
                        if u == 0:
                            group = 2 * i + slot
                            pe.wait_ge(sig.kv_low.sem, sig.kv_low.at(2 * group + 1))
                        pe.wait_ge(sig.context_low.sem, sig.context_low.at(BODY * i + n + 1))
                    for h in range(kv_heads):
                        for c in range(CH):
                            if kv_split:
                                for n_part, (wp, fp) in enumerate(parts):
                                    mm = nc.tensor.matmul(
                                        bank[2 + h // 2][:, (h % 2) * UT:(h % 2 + 1) * UT].rearrange(
                                            "p (b s) -> p b s", b=UB),
                                        kv_part(wp, 0, c)[:, h * HD:(h + 1) * HD],
                                        context[:, fp, c, :, :],
                                        start=(c == 0 and n_part == 0), stop=(c == CH - 1 and n_part == 2))
                                continue
                            w = wkv[slot][:, c * kdim + h * HD:c * kdim + (h + 1) * HD]
                            if both:
                                mm = nc.tensor.matmul(bank[2][:, :].rearrange("p (b k s) -> p b k s", k=2, s=SEQ), w,
                                                      feat[:, :, c, UB * u:UB * u + UB, :].rearrange(
                                                          "p k b s -> p b k s"),
                                                      start=(c == 0), stop=(c == CH - 1))
                            else:
                                out = bank[2 + h // 2][:, (h % 2) * UT:(h % 2 + 1) * UT]
                                mm = nc.tensor.matmul(out.rearrange("p (b s) -> p b s", b=UB), w,
                                                      feat[:, keys, c, UB * u:UB * u + UB, :],
                                                      start=(c == 0), stop=(c == CH - 1))
                        if h % 2 == 1 or kv_heads == 1:
                            mm.then_inc(sig.k_ready.sem, 1)

                def project_v(i, n):
                    slot, u = (0 if both else n // UNITS), n % UNITS
                    kr = k_round(i, n)
                    off = CH * kdim
                    if both or kbanks == 2:
                        pe.wait_ge(sig.k_done.sem, sig.k_done.at(kbanks * (kr + 1)))
                    else:
                        pe.wait_ge(sig.v_done.sem, sig.v_done.at(kr))
                    if both:
                        for b in range(UB):
                            for c in range(CH):
                                for k in (CTX, SELF):
                                    mm = nc.tensor.matmul(
                                        value_bank[k * SEQ:(k + 1) * SEQ, b * HD:(b + 1) * HD],
                                        feat[:, k, c, UB * u + b, :], wkv[slot][:, off + c * HD:off + (c + 1) * HD],
                                        start=(c == 0), stop=(c == CH - 1))
                        mm.then_inc(sig.v_ready.sem, 1)
                        return
                    if kv_split and u == 0:
                        group = 2 * i + slot
                        pe.wait_ge(sig.kv_low.sem, sig.kv_low.at(2 * group + 2))
                    for tt in range(2):
                        for c in range(CH):
                            if kv_split:
                                for n_part, (fp, wp) in enumerate(parts):
                                    mm = nc.tensor.matmul(
                                        bank[2 + tt][:, :], context[:, fp, c, 2 * tt:2 * tt + 2, :],
                                        kv_part(wp, 1, c),
                                        start=(c == 0 and n_part == 0), stop=(c == CH - 1 and n_part == 2))
                                continue
                            out = bank[2 + tt][:, :] if kbanks == 2 else bank[3][:, tt * HD:(tt + 1) * HD]
                            mm = nc.tensor.matmul(
                                out, feat[:, keys, c, UB * u + 2 * tt:UB * u + 2 * tt + 2, :],
                                wkv[slot][:, off + c * kdim:off + (c + 1) * kdim],
                                start=(c == 0), stop=(c == CH - 1))
                        if kbanks == 2 or tt == 1:
                            mm.then_inc(sig.v_ready.sem, 1)

                def turn_keys(i, n):
                    uu = BODY * i + n
                    pe.wait_ge(sig.rms_done.sem, sig.rms_done.at(uu + 1))
                    for tt in range(2):
                        mm = nc.tensor.transpose(bank[2][:, tt * P:(tt + 1) * P], k_rows[:, tt, :], g.ident[:])
                    mm.then_inc(sig.keys_turned.sem, 1)

                def query_squares(i, n):
                    uu = BODY * i + n
                    pe.wait_ge(sig.squared.sem, sig.squared.at(2 * uu + 2))
                    for b in range(UB):
                        for j in range(2):
                            col = (b // 2) * 4 + j * 2 + b % 2
                            mm = nc.tensor.matmul(bank[5][:, col:col + 1],
                                                  q_sq[:, b, 2 * j:2 * j + 2, :].rearrange("p h s -> p (h s)"),
                                                  mean_col[:], start=True, stop=True)
                    mm.then_inc(sig.rms_sum.sem, 1)

                def scores(i, n):
                    uu, u = BODY * i + n, n % UNITS
                    pe.wait_ge(sig.q_done.sem, sig.q_done.at(2 * uu + 2))
                    if rms:
                        pe.wait_ge(sig.keys_taken.sem, sig.keys_taken.at(uu + 1))
                    elif n < UNITS or not both:
                        pe.wait_ge(sig.k_done.sem, sig.k_done.at(kbanks * (k_round(i, n) + 1)))
                    pe.wait_ge(score_bank_free.sem, score_bank_free.at(halves * uu))
                    for b in range(UB):
                        for h in range(GH):
                            j, h2 = h // 2, h % 2
                            if both:
                                dst = score_banks[b // 2][h2 * SEQ:(h2 + 1) * SEQ,
                                                            ((b % 2) * 2 + j) * klen:((b % 2) * 2 + j + 1) * klen]
                                key = k_t[:, u, b * klen:(b + 1) * klen]
                            else:
                                col = ((b // 2) * 4 + j * 2 + b % 2) * SEQ
                                dst = score_banks[0][h2 * SEQ:(h2 + 1) * SEQ, col:col + SEQ]
                                key = k_t[:, h if kv_heads == GH else 0, b * SEQ:(b + 1) * SEQ]
                            mm = nc.tensor.matmul(dst, q_t[:, h, b * SEQ:(b + 1) * SEQ], key,
                                                  start=True, stop=True)
                        if both and b % 2 == 1 or b == UB - 1 and not both:
                            mm.then_inc(sig.s_ready.sem, 1)

                def turn_probs(i, n, which=range(halves)):
                    uu = BODY * i + n
                    for half in which:
                        pe.wait_ge(sig.p_ready.sem, sig.p_ready.at(halves * uu + half + 1))
                        pe.wait_ge(sig.pt_done.sem, sig.pt_done.at(halves * uu + half))
                        for blk in range(4):
                            mm = nc.tensor.transpose(bank[5][:, blk * P:(blk + 1) * P],
                                                     probs[:, half, blk * P:(blk + 1) * P], g.ident[:])
                        mm.then_inc(sig.pt_ready.sem, 1)

                def weighted_values(i, n):
                    uu, u, par = BODY * i + n, n % UNITS, n % 2
                    pe.wait_ge(sig.pt_done.sem, sig.pt_done.at(halves * (uu + 1)))
                    if n < UNITS or not both:
                        pe.wait_ge(sig.v_done.sem, sig.v_done.at(kbanks * (k_round(i, n) + 1)))
                    pe.wait_ge(sig.added.sem, sig.added.at(2 * uu))
                    for b2 in range(2):
                        for bp in range(2):
                            out = bank[6 + b2]
                            if both:
                                mm = nc.tensor.matmul(out[:, bp * UT:(bp + 1) * UT], v[:, u, 2 * bp + b2, :],
                                                      p_t[:, bp, b2 * UT:(b2 + 1) * UT], start=True, stop=True)
                                continue
                            rows = slice(b2 * SEQ, (b2 + 1) * SEQ)
                            if kv_heads == 1:
                                mm = nc.tensor.matmul(out[:, bp * UT:(bp + 1) * UT], v[rows, par, bp, :],
                                                      p_t[rows, 0, bp * UT:(bp + 1) * UT], start=True, stop=True)
                                continue
                            for h in range(GH):
                                mm = nc.tensor.matmul(
                                    out[:, bp * UT + h * SEQ:bp * UT + (h + 1) * SEQ],
                                    v[rows, par, bp, h * HD:(h + 1) * HD],
                                    p_t[rows, 0, bp * UT + h * SEQ:bp * UT + (h + 1) * SEQ], start=True, stop=True)
                        mm.then_inc(sig.o_ready.sem, 1)

                def project_out(i, n):
                    uu, slot, u = BODY * i + n, n // UNITS, n % UNITS
                    pe.wait_ge(sig.o_done.sem, sig.o_done.at(2 * (uu + 1)))
                    if u == 0:
                        pe.wait_ge(sig.o_split.sem, sig.o_split.at(2 * i + slot + 1))
                    for tt in range(2):
                        for h in range(GH):
                            for n_part, (op, wp) in enumerate(parts):
                                mm = nc.tensor.matmul(bank[6 + tt][:, :], o_t[:, op, h, 2 * tt:2 * tt + 2, :],
                                                      wqo[:, wp, wq_cols + h * DIM:wq_cols + (h + 1) * DIM],
                                                      start=(h == 0 and n_part == 0),
                                                      stop=(h == GH - 1 and n_part == 2))
                        mm.then_inc(sig.y_ready.sem, 1)

                def step(front, back):
                    new_keys = front and (front[1] < UNITS or not both)
                    if front and rms:
                        project_k(*front)
                    if front and back and both:
                        project_q(*front, range(2))
                        turn_probs(*back, range(1))
                        project_q(*front, range(2, 3))
                        turn_probs(*back, range(1, 2))
                        project_q(*front, range(3, 4))
                    elif front:
                        project_q(*front)
                    if new_keys and not rms:
                        project_k(*front)
                    if back and not (front and both):
                        turn_probs(*back)
                    if new_keys:
                        project_v(*front)
                    if back:
                        weighted_values(*back)
                    if front and rms:
                        turn_keys(*front)
                        query_squares(*front)
                    if front:
                        scores(*front)
                    if back:
                        project_out(*back)

                pe.wait_ge(g.home_in[g.stage.home], g.stage.arrived)
                pipeline(pe, step)
                if not last:
                    norm_tensor(nc, pe, g, (0, 1))

            @block.scalar
            def _(act):
                def queries(i, n):
                    uu = BODY * i + n
                    for j in range(2):
                        act.wait_ge(sig.q_ready.sem, sig.q_ready.at(2 * uu + j + 1))
                        if rms:
                            nc.scalar.activation(q_sq[:, :, 2 * j:2 * j + 2, :].rearrange("p b h s -> p h b s"),
                                                 bank[j][:, :].rearrange("p (h b s) -> p h b s", h=2, b=UB),
                                                 ACT.Square).then_inc(sig.squared.sem, 1)
                            nc.scalar.mul(q_t[:, 2 * j:2 * j + 2, :].rearrange("p h s -> p (h s)"),
                                          bank[j][:, :], q_w[:, 0:1]).then_inc(sig.q_done.sem, 1)
                        else:
                            nc.scalar.copy(q_t[:, 2 * j:2 * j + 2, :].rearrange("p h s -> p (h s)"),
                                           bank[j][:, :]).then_inc(sig.q_done.sem, 1)

                def keys_out(i, n):
                    kr = k_round(i, n)
                    if rms:
                        act.wait_ge(sig.k_ready.sem, sig.k_ready.at(kr + 1))
                        for tt in range(2):
                            if tt == 1:
                                act.wait_ge(sig.act_step.sem, sig.act_step.at(2 * kr + 1))
                            nc.scalar.activation(k_junk[:], bank[2][:, tt * HD:(tt + 1) * HD], ACT.Square,
                                                 accum_out=ssq[:, tt:tt + 1]).then_inc(sig.act_step.sem, 1)
                        return
                    for j in range(kbanks):
                        act.wait_ge(sig.k_ready.sem, sig.k_ready.at(kbanks * kr + j + 1))
                        if both:
                            dst, src = k_t[:, n % UNITS, :], bank[2][:, :]
                        elif kv_heads == 1:
                            dst, src = k_t[:, 0, :], bank[2][:, 0:UT]
                        else:
                            dst = k_t[:, 2 * j:2 * j + 2, :].rearrange("p h s -> p (h s)")
                            src = bank[2 + j][:, :]
                        nc.scalar.copy(dst, src).then_inc(sig.k_done.sem, 1)

                def turned_keys(i, n):
                    uu = BODY * i + n
                    act.wait_ge(sig.keys_turned.sem, sig.keys_turned.at(uu + 1))
                    nc.scalar.mul(k_t[:, 0, :], bank[2][:, 0:UT], k_w[:, 0:1]).then_inc(sig.keys_taken.sem, 1)

                def outputs(i, n):
                    uu = BODY * i + n
                    for b2 in range(2):
                        act.wait_ge(sig.o_ready.sem, sig.o_ready.at(2 * uu + b2 + 1))
                        nc.scalar.copy(o_part(HIGH, b2), o_bank(b2)).then_inc(sig.o_high.sem, 1)

                def exponentials(i, n):
                    uu = BODY * i + n
                    for half in range(halves):
                        act.wait_ge(sig.shifted.sem, sig.shifted.at(halves * uu + half + 1))
                        nc.scalar.activation(probs[:, half, :], shifted[:, half, :], ACT.Exp,
                                             scale=1.0 if (bias is not None or rms) else scale).then_inc(
                            sig.exp_done.sem, 1)


                def split_q_high(group, halves=range(2)):
                    if not isinstance(group, int) or group:
                        act.wait_ge(sig.qo_in.sem, sig.qo_in.at(32 * group))
                    for j in halves:
                        nc.scalar.copy(wqo[:, HIGH, q_half(j)], raw[:, q_half(j)]).then_inc(sig.wq_high.sem, 1)

                def split_o_high(group):
                    act.wait_ge(sig.qo_in.sem, sig.qo_in.at(32 * group + 16))
                    act.wait_ge(sig.added.sem, sig.added.at(2 * UNITS * group))
                    nc.scalar.copy(wqo[:, HIGH, wq_cols:], raw[:]).then_inc(sig.wo_high.sem, 1)

                def step(front, back):
                    if front:
                        i, n = front
                        if rms:
                            keys_out(i, n)
                        queries(i, n)
                        next_group = 2 * i + n // UNITS + 1
                        very_last = n == BODY - 1 and isinstance(i, int)
                        if n % UNITS == UNITS - 1 and not very_last:
                            split_q_high(next_group)
                        if not rms and (n < UNITS or not both):
                            keys_out(i, n)
                        new_kv = kv_split and n % UNITS == UNITS - 1 and not very_last
                        if new_kv:
                            split_kv_high(next_group, 0)
                        if kv_split and not very_last:
                            split_own_high(n + 1)
                        if not kv_split and not back:
                            for u in range(1, UNITS):
                                split_own_high(u)
                    if back:
                        outputs(*back)
                    if front and kv_split and not very_last:
                        split_context_high(n + 1, BODY * i + n + 1)
                    if front:
                        if rms:
                            turned_keys(i, n)
                        exponentials(i, n)
                        if n % UNITS == 0:
                            split_o_high(2 * i + n // UNITS)
                        if new_kv:
                            split_kv_high(next_group, 1)

                def split_own_high(n):
                    nc.scalar.copy(own_part(HIGH, n), feat[:, SELF, :, units_batches(n % UNITS), :]).then_inc(
                        sig.own_high.sem, 1)

                def split_context_high(n, done):
                    if done is not None:
                        act.wait_ge(sig.v_ready.sem, sig.v_ready.at(kbanks * done))
                    nc.scalar.copy(context[:, HIGH, :, :, :],
                                   feat[:, CTX, :, units_batches(n % UNITS), :]).then_inc(sig.context_high.sem, 1)

                def split_kv_high(group, value):
                    if not isinstance(group, int) or group:
                        act.wait_ge(sig.kv_raw_in.sem, sig.kv_raw_in.at(16 * group))
                        if value:
                            act.wait_ge(sig.v_ready.sem, sig.v_ready.at(kbanks * UNITS * group))
                    cols = slice(value * CH * kdim, (value + 1) * CH * kdim)
                    nc.scalar.copy(kv_parts[:, HIGH, cols], wkv[0][:, cols]).then_inc(sig.kv_high.sem, 1)

                act.wait_ge(g.home_in[g.stage.home], g.stage.arrived)
                split_q_high(0, range(1))
                split_own_high(0)
                split_q_high(0, range(1, 2))
                if kv_split:
                    split_context_high(0, None)
                    split_kv_high(0, 0)
                    split_kv_high(0, 1)
                if rms or key_mask is not None or mask is not None:
                    act.wait_ge(sig.small_in.sem, sig.small_in.at(small_loads))
                pipeline(act, step)
                if not last:
                    norm_scalar(nc, act, g, (0, 1))

            @block.vector
            def _(dve):
                head_steps = Steps(sig.dve_step)
                def split_own_low(n, done):
                    dve.wait_ge(sig.own_high.sem, sig.own_high.at(done + 1))
                    nc.vector.tensor_tensor(own_part(LOW, n), feat[:, SELF, :, units_batches(n % UNITS), :],
                                            own_part(HIGH, n), ALU.subtract).then_inc(sig.own_low.sem, 1)

                def split_context_low(n, done):
                    dve.wait_ge(sig.context_high.sem, sig.context_high.at(done + 1))
                    nc.vector.tensor_tensor(context[:, LOW, :, :, :], feat[:, CTX, :, units_batches(n % UNITS), :],
                                            context[:, HIGH, :, :, :], ALU.subtract).then_inc(sig.context_low.sem, 1)

                def split_kv_low(group, value):
                    cols = slice(value * CH * kdim, (value + 1) * CH * kdim)
                    dve.wait_ge(sig.kv_high.sem, sig.kv_high.at(2 * group + value + 1))
                    nc.vector.tensor_tensor(kv_parts[:, LOW, cols], wkv[0][:, cols], kv_parts[:, HIGH, cols],
                                            ALU.subtract).then_inc(sig.kv_low.sem, 1)

                def split_query_weights_low(group):
                    for j in range(2):
                        dve.wait_ge(sig.wq_high.sem, sig.wq_high.at(2 * group + j + 1))
                        nc.vector.tensor_tensor(wqo[:, LOW, q_half(j)], raw[:, q_half(j)], wqo[:, HIGH, q_half(j)],
                                                ALU.subtract).then_inc(sig.q_split.sem, 1)

                split_own_low(0, 0)
                if rms:
                    split_query_weights_low(0)
                if kv_split:
                    split_context_low(0, 0)
                    split_kv_low(0, 0)
                    split_kv_low(0, 1)
                if key_mask is not None:
                    dve.wait_ge(sig.small_in.sem, sig.small_in.at(small_loads))
                    nc.vector.tensor_copy(km_one, km_u8).then_inc(head_steps.count(), 1)
                    dve.wait_ge(sig.dve_step.sem, head_steps.so_far())
                    nc.vector.tensor_scalar(km_neg, km_one, 1.0, -NEG, ALU.subtract, ALU.mult).then_inc(
                        head_steps.count(), 1)
                    dve.wait_ge(sig.dve_step.sem, head_steps.so_far())
                if mask is not None:
                    dve.wait_ge(sig.small_in.sem, sig.small_in.at(small_loads))
                if rms:
                    nc.vector.memset(mean_col[:], 1.0 / HD).then_inc(head_steps.count(), 1)
                    dve.wait_ge(sig.dve_step.sem, head_steps.so_far())
                head = head_steps.n
                per_unit = halves * (before_exp + after_exp)

                def turned(i, n):
                    uu = BODY * i + n
                    for half in range(halves):
                        dve.wait_ge(sig.pt_ready.sem, sig.pt_ready.at(halves * uu + half + 1))
                        nc.vector.tensor_copy(p_t[:, half, :], bank[5][:, :]).then_inc(sig.pt_done.sem, 1)

                def values(i, n):
                    kr = k_round(i, n)
                    for j in range(kbanks):
                        dve.wait_ge(sig.v_ready.sem, sig.v_ready.at(kbanks * kr + j + 1))
                        if both:
                            dst, src = v[:, n % UNITS, :, :].rearrange("p b d -> p (b d)"), value_bank[:, :]
                        elif kbanks == 2:
                            dst, src = v[:, n % 2, j, :], bank[2 + j][:, :]
                        else:
                            dst, src = v[:, n % 2, :, :].rearrange("p t d -> p (t d)"), bank[3][:, 0:2 * HD]
                        nc.vector.tensor_copy(dst, src).then_inc(sig.v_done.sem, 1)

                def rms_keys(i, n):
                    uu = BODY * i + n
                    dve.wait_ge(sig.act_step.sem, sig.act_step.at(2 * uu + 2))
                    nc.vector.tensor_scalar(k_var[:], ssq[:], 1.0 / HD, LN_EPS, ALU.mult, ALU.add).then_inc(
                        sig.rms_var.sem, 1)
                    dve.wait_ge(sig.rms_power.sem, sig.rms_power.at(2 * uu + 1))
                    for tt in range(2):
                        mm = nc.vector.tensor_scalar(k_rows[:, tt, :], bank[2][:, tt * HD:(tt + 1) * HD],
                                                     k_rstd[:, tt:tt + 1], None, ALU.mult)
                    mm.then_inc(sig.rms_done.sem, 1)

                def rms_queries(i, n):
                    uu = BODY * i + n
                    dve.wait_ge(sig.rms_sum.sem, sig.rms_sum.at(uu + 1))
                    nc.vector.tensor_scalar(q_var[:], bank[5][:, 0:8], LN_EPS, 1.0 / scale ** 2, ALU.add,
                                            ALU.mult).then_inc(sig.rms_var.sem, 1)

                def softmax(i, n):
                    uu = BODY * i + n
                    for half in range(halves):
                        steps = Steps(sig.dve_step, head + per_unit * uu + before_exp * half)
                        dve.wait_ge(sig.s_ready.sem, sig.s_ready.at(halves * uu + half + 1))
                        scored = score_banks[half][:, :]
                        sh = shifted[:, half, :]
                        rows = scored.rearrange("p (g k) -> p g k", k=klen)
                        sh_rows = sh.rearrange("p (g k) -> p g k", k=klen)
                        m = mx[:, half, :]
                        if bias is not None:
                            if bias_cols == BATCH * GH // 2 * SEQ:
                                u = n % UNITS
                                b_ap = bias_sb[:, n // UNITS, u * 512:(u + 1) * 512]
                                nc.vector.scalar_tensor_tensor(sh, scored, scale, b_ap, ALU.mult,
                                                               ALU.add).then_inc(sig.s_read.sem, 1)
                            else:
                                b_ap = over(bias_sb[:, n // UNITS, :], (1, 2))
                                nc.vector.scalar_tensor_tensor(
                                    sh.rearrange("p (a c) -> p a c", a=2), scored.rearrange("p (a c) -> p a c", a=2),
                                    scale, b_ap, ALU.mult, ALU.add).then_inc(sig.s_read.sem, 1)
                            dve.wait_ge(sig.s_read.sem, sig.s_read.at(uu + 1))
                            if key_mask is not None:
                                u = n % UNITS
                                km = km_neg[:, UB * u:UB * u + UB, :].rearrange("p (a b) s -> p a (b s)", a=2)
                                four = sh.rearrange("p (a j c) -> p a j c", a=2, j=2)
                                nc.vector.tensor_tensor(four, four, over(km, (2, 2)), ALU.add).then_inc(
                                    steps.count(), 1)
                                dve.wait_ge(sig.dve_step.sem, steps.so_far())
                            nc.vector.tensor_reduce(m, sh_rows, AX.X, ALU.max).then_inc(steps.count(), 1)
                            dve.wait_ge(sig.dve_step.sem, steps.so_far())
                            nc.vector.tensor_tensor(sh_rows, sh_rows, over(m, (2, klen)), ALU.subtract).then_inc(
                                sig.shifted.sem, 1)
                        elif rms:
                            dve.wait_ge(sig.rms_power.sem, sig.rms_power.at(2 * uu + 2))
                            nc.vector.tensor_tensor(sh_rows, rows, over(q_rstd[:], (2, klen)), ALU.mult).then_inc(
                                sig.s_read.sem, 1)
                            dve.wait_ge(sig.s_read.sem, sig.s_read.at(uu + 1))
                            nc.vector.tensor_tensor(sh_rows, sh_rows, over(mask_sb[:], (1, ngr)),
                                                    ALU.add).then_inc(steps.count(), 1)
                            dve.wait_ge(sig.dve_step.sem, steps.so_far())
                            nc.vector.tensor_reduce(m, sh_rows, AX.X, ALU.max).then_inc(steps.count(), 1)
                            dve.wait_ge(sig.dve_step.sem, steps.so_far())
                            nc.vector.tensor_tensor(sh_rows, sh_rows, over(m, (2, klen)), ALU.subtract).then_inc(
                                sig.shifted.sem, 1)
                        else:
                            nc.vector.tensor_reduce(m, rows, AX.X, ALU.max).then_inc(steps.count(), 1)
                            dve.wait_ge(sig.dve_step.sem, steps.so_far())
                            nc.vector.tensor_tensor(sh_rows, rows, over(m, (2, klen)), ALU.subtract).then_inc(
                                sig.shifted.sem, 1)
                    for half in range(halves):
                        steps = Steps(sig.dve_step, head + per_unit * uu + before_exp * halves + after_exp * half)
                        pr_rows = probs[:, half, :].rearrange("p (g k) -> p g k", k=klen)
                        t, r = total[:, half, :], recip[:, half, :]
                        dve.wait_ge(sig.exp_done.sem, sig.exp_done.at(halves * uu + half + 1))
                        nc.vector.tensor_reduce(t, pr_rows, AX.X, ALU.add).then_inc(steps.count(), 1)
                        dve.wait_ge(sig.dve_step.sem, steps.so_far())
                        nc.vector.reciprocal(r, t).then_inc(steps.count(), 1)
                        dve.wait_ge(sig.dve_step.sem, steps.so_far())
                        if key_mask is not None:
                            u = n % UNITS
                            nc.vector.tensor_tensor(pr_rows, pr_rows, over(r, (2, klen)), ALU.mult).then_inc(
                                steps.count(), 1)
                            dve.wait_ge(sig.dve_step.sem, steps.so_far())
                            km = km_one[:, UB * u:UB * u + UB, :].rearrange("p (a b) s -> p a (b s)", a=2)
                            four = probs[:, half, :].rearrange("p (a j c) -> p a j c", a=2, j=2)
                            nc.vector.tensor_tensor(four, four, over(km, (2, 2)), ALU.mult).then_inc(
                                sig.p_ready.sem, 1)
                        else:
                            nc.vector.tensor_tensor(pr_rows, pr_rows, over(r, (2, klen)), ALU.mult).then_inc(
                                sig.p_ready.sem, 1)

                def outputs_low(i, n):
                    uu = BODY * i + n
                    for b2 in range(2):
                        dve.wait_ge(sig.o_high.sem, sig.o_high.at(2 * uu + b2 + 1))
                        nc.vector.tensor_tensor(o_part(LOW, b2), o_bank(b2), o_part(HIGH, b2),
                                                ALU.subtract).then_inc(sig.o_done.sem, 1)

                def add(i, n):
                    uu, u = BODY * i + n, n % UNITS
                    for tt in range(2):
                        dve.wait_ge(sig.y_ready.sem, sig.y_ready.at(2 * uu + tt + 1))
                        t = 2 * u + tt
                        nc.vector.tensor_tensor(x[:, t, :], x[:, t, :], bank[6 + tt][:, :], ALU.add).then_inc(
                            sig.added.sem, 1)
                    if n >= UNITS and isinstance(i, int):
                        for tt in range(2):
                            norm_tile(nc, dve, g, 2 * u + tt, 2 * uu + 2, scale=not rms)

                def step(front, back):
                    if front and rms:
                        rms_keys(*front)
                    if back:
                        turned(*back)
                    if front and (front[1] < UNITS or not both):
                        values(*front)
                    very_last = front and front[1] == BODY - 1 and isinstance(front[0], int)
                    new_kv = kv_split and front and front[1] % UNITS == UNITS - 1 and not very_last
                    if rms and front and front[1] % UNITS == UNITS - 1 and not very_last:
                        split_query_weights_low(2 * front[0] + front[1] // UNITS + 1)
                    if new_kv:
                        split_kv_low(2 * front[0] + front[1] // UNITS + 1, 0)
                    if kv_split and front and not very_last:
                        done = BODY * front[0] + front[1] + 1
                        split_own_low(front[1] + 1, done)
                    if not kv_split and front and not back:
                        for u in range(1, UNITS):
                            split_own_low(u, u)
                    if back:
                        outputs_low(*back)
                    if front:
                        if rms:
                            rms_queries(*front)
                        if kv_split and not very_last:
                            split_context_low(front[1] + 1, done)
                        softmax(*front)
                    if g.x_pending and not back:
                        dve.wait_ge(g.x_in, g.x_pending)
                    if back:
                        add(*back)
                    if new_kv:
                        split_kv_low(2 * front[0] + front[1] // UNITS + 1, 1)

                pipeline(dve, step)
                for t in range(0 if rms else TILES - 1, TILES):
                    norm_scale(nc, dve, g, t)



def narrow_attention(nc, g, name, last, keys, scale, bias=None, rope=False, out_proj=True):
    sig, feat, x, bank = g.sig, g.feat, g.x, g.bank
    nbody = 2
    rounds = TILES // nbody
    blocks = KV // 2
    wk_at, wv_at, wo_at = CH * DIM, CH * (DIM + P), CH * (DIM + 2 * P)
    vcols = 2 * (ND + 1)
    consts_at = wo_at + (NR * DIM if out_proj else 0)
    consts = g.home[:, consts_at:HOME]
    with ExitStack() as ctx:
        def sb(what, shape, dt=F32):
            return ctx.enter_context(nc.sbuf_tensor(f"{name}_{what}", shape, dt))
        w = g.home
        ks = sb("ks", [P, 2, CH, P])
        q_t = sb("q_t", [P, 2, NR, P])
        k_t = sb("k_t", [P, P])
        k_diag = sb("k_diag", [P, 2, 2, KV, SEQ])
        v_diag = sb("v_diag", [P, 2, 2, blocks, 2, ND + 1])
        v_sum = sb("v_sum", [P, 2 * P])
        head_of = consts[:, 0:KV]
        half_of = consts[:, KV:KV + 2]
        shifted = sb("shifted", [P, 2, 512])
        probs = sb("probs", [P, 2, 512])
        p_t = sb("p_t", [P, 512])
        mx = sb("mx", [P, 2, KV])
        recip = sb("recip", [P, HEADS])
        attn = sb("attn", [P, HEADS, ND])
        attn_t = sb("attn_t", [P, NR, P])
        if bias is not None:
            bias_sb = sb("bias", [P, NR, 512])
        if rope:
            at = KV + 2
            rot = consts[:, at:at + P]
            cos, sin = consts[:, at + P:at + P + SEQ], consts[:, at + P + SEQ:at + P + 2 * SEQ]
            at += P + 2 * SEQ
            q_bias, k_bias, v_bias = consts[:, at:at + NR], consts[:, at + NR:at + NR + 1], \
                consts[:, at + NR + 1:at + NR + 1 + P]
            turned_q = sb("turned_q", [P, NR * P])
            turned_k = sb("turned_k", [P, P])
        score_bank_free = sig.s_read if bias is not None else sig.shifted
        o_banks = (bank[3], bank[7])

        def o_block(r, jj):
            n = r * blocks + jj
            return (o_banks[0], n) if r < NR - 1 else (o_banks[1], n - (NR - 1) * blocks)

        def pipeline(engine, step):
            step(None, (0, 0), None)
            step((0, 0), (0, 1), None)
            with engine.Fori(0, rounds - 1) as i:
                step((i, 1), (i + 1, 0), (i, 0))
                step((i + 1, 0), (i + 1, 1), (i, 1))
            step((rounds - 1, 1), None, (rounds - 1, 0))
            step(None, None, (rounds - 1, 1))

        def own_batches(i, n):
            return bass.ds(2 * (nbody * i + n), 2)

        with nc.Block() as block:
            @block.sync
            def _(sp):
                if bias is not None:
                    sp.dma_start(bias_sb[:].rearrange("p r c -> p (r c)"), bias).then_inc(sig.small_in.sem, 16)
                load_ahead(sp, g)
                if last:
                    norm_sync(nc, sp, g)

            @block.gpsimd
            def _(pool):
                norm_pool(nc, pool, g)

            @block.tensor
            def _(pe):
                def project_v(i, n, b):
                    uu = nbody * i + n
                    if b == 0:
                        pe.wait_ge(sig.staged.sem, sig.staged.at(uu + 1))
                        pe.wait_ge(sig.kd_done.sem, sig.kd_done.at(uu))
                        pe.wait_ge(sig.v_done.sem, sig.v_done.at(uu))
                        if rope:
                            pe.wait_ge(sig.q_done.sem, sig.q_done.at(uu + 1))
                    for c in range(CH):
                        for dup in range(2):
                            mm = nc.tensor.matmul(
                                bank[2][dup * SEQ:(dup + 1) * SEQ, (2 + b) * P:(3 + b) * P],
                                ks[:, n % 2, c, b * SEQ:(b + 1) * SEQ],
                                w[:, wv_at + c * P:wv_at + (c + 1) * P], start=(c == 0), stop=(c == CH - 1))
                    if b == 1:
                        mm.then_inc(sig.v_ready.sem, 1)

                def project_k(i, n):
                    uu = nbody * i + n
                    pe.wait_ge(sig.kd_done.sem, sig.kd_done.at(uu))
                    pe.wait_ge(sig.v_done.sem, sig.v_done.at(uu))
                    for c in range(CH):
                        mm = nc.tensor.matmul(bank[2][:, 0:P].rearrange("p (b s) -> p b s", b=2),
                                              w[:, wk_at + c * P:wk_at + (c + 1) * P],
                                              feat[:, keys, c, own_batches(i, n), :],
                                              start=(c == 0), stop=(c == CH - 1))
                    mm.then_inc(sig.k_ready.sem, 1)

                def project_q(i, n, chunks):
                    uu = nbody * i + n
                    if chunks[0] == 0:
                        if out_proj:
                            pe.wait_ge(sig.added.sem, sig.added.at(uu - 1))
                        if rope:
                            pe.wait_ge(sig.kd_done.sem, sig.kd_done.at(uu))
                        pe.wait_ge(sig.q_done.sem, sig.q_done.at(uu))
                    for r in chunks:
                        for c in range(CH):
                            mm = nc.tensor.matmul(bank[0][:, r * P:(r + 1) * P].rearrange("p (b s) -> p b s", b=2),
                                                  w[:, c * DIM + r * P:c * DIM + (r + 1) * P],
                                                  feat[:, SELF, c, own_batches(i, n), :],
                                                  start=(c == 0), stop=(c == CH - 1))
                    if chunks[-1] == NR - 1:
                        mm.then_inc(sig.q_ready.sem, 1)

                def rotate(i, n):
                    uu = nbody * i + n
                    pe.wait_ge(sig.q_done.sem, sig.q_done.at(uu + 1))
                    nc.tensor.matmul(bank[1][:, :], rot, q_t[:, n % 2, :, :].rearrange("p r s -> p (r s)"),
                                     start=True, stop=True)
                    nc.tensor.matmul(bank[0][:, 0:P], rot, k_t[:], start=True, stop=True).then_inc(
                        sig.rotated.sem, 1)

                def scores(i, n, r):
                    uu = nbody * i + n
                    if r == 0:
                        pe.wait_ge(sig.kd_done.sem, sig.kd_done.at(uu + 1))
                        if not rope:
                            pe.wait_ge(sig.q_done.sem, sig.q_done.at(uu + 1))
                    ss = NR * uu + r
                    pe.wait_ge(score_bank_free.sem, score_bank_free.at(ss - 1))
                    for b in range(2):
                        mm = nc.tensor.matmul(bank[4 + r % 2][b * SEQ:(b + 1) * SEQ, :],
                                              q_t[:, n % 2, r, b * SEQ:(b + 1) * SEQ],
                                              k_diag[:, n % 2, b, :, :].rearrange("p h k -> p (h k)"),
                                              start=True, stop=True)
                    mm.then_inc(sig.s_ready.sem, 1)

                def turn_probs(i, n, r):
                    ss = NR * (nbody * i + n) + r
                    pe.wait_ge(sig.exp_done.sem, sig.exp_done.at(ss + 1))
                    pe.wait_ge(sig.pt_done.sem, sig.pt_done.at(ss))
                    for jj in range(blocks):
                        mm = nc.tensor.transpose(bank[6][:, jj * P:(jj + 1) * P],
                                                 probs[:, r % 2, jj * P:(jj + 1) * P], g.ident[:])
                    mm.then_inc(sig.pt_ready.sem, 1)

                def weighted_values(i, n, r):
                    uu = nbody * i + n
                    ss = NR * uu + r
                    if r == 0:
                        pe.wait_ge(sig.v_done.sem, sig.v_done.at(uu + 1))
                        pe.wait_ge(sig.o_done.sem, sig.o_done.at(uu))
                    pe.wait_ge(sig.pt_done.sem, sig.pt_done.at(ss + 1))
                    for jj in range(blocks):
                        ob, at_block = o_block(r, jj)
                        for b in range(2):
                            mm = nc.tensor.matmul(
                                ob[b * SEQ:(b + 1) * SEQ, at_block * vcols:(at_block + 1) * vcols],
                                p_t[:, jj * P + b * SEQ:jj * P + (b + 1) * SEQ],
                                v_diag[:, n % 2, b, jj, :, :].rearrange("p h d -> p (h d)"),
                                start=True, stop=True)
                    if r == NR - 1:
                        mm.then_inc(sig.o_ready.sem, 1)

                def turn_output(i, n):
                    uu = nbody * i + n
                    pe.wait_ge(sig.o_done.sem, sig.o_done.at(uu + 1))
                    pe.wait_ge(sig.attn_taken.sem, sig.attn_taken.at(uu))
                    for r in range(NR):
                        mm = nc.tensor.transpose(bank[1][:, r * P:(r + 1) * P],
                                                 attn[:, r * KV:(r + 1) * KV, :].rearrange("p h d -> p (h d)"),
                                                 g.ident[:])
                    mm.then_inc(sig.attn_turned.sem, 1)

                def project_out(i, n, queries_too):
                    uu = nbody * i + n
                    pe.wait_ge(sig.attn_taken.sem, sig.attn_taken.at(uu + 1))
                    if queries_too:
                        pe.wait_ge(sig.q_done.sem, sig.q_done.at(uu + 2))
                    for r in range(NR):
                        mm = nc.tensor.matmul(bank[0][:, :], attn_t[:, r, :],
                                              w[:, wo_at + r * DIM:wo_at + (r + 1) * DIM],
                                              start=(r == 0), stop=(r == NR - 1))
                    mm.then_inc(sig.y_ready.sem, 1)

                pe.wait_ge(g.home_in[g.stage.home], g.stage.arrived)

                def step(unit, ahead, back):
                    late = not rope
                    if unit:
                        scores(*unit, 0)
                        scores(*unit, 1)
                    if back and out_proj:
                        turn_output(*back)
                    if ahead:
                        if late:
                            project_v(*ahead, 0)
                            project_v(*ahead, 1)
                        project_k(*ahead)
                    if unit:
                        turn_probs(*unit, 0)
                        scores(*unit, 2)
                        weighted_values(*unit, 0)
                    if back and out_proj:
                        project_out(*back, unit is not None)
                    if ahead and not late:
                        project_q(*ahead, range(NR))
                    if unit:
                        turn_probs(*unit, 1)
                        scores(*unit, 3)
                        weighted_values(*unit, 1)
                    if ahead and not late:
                        rotate(*ahead)
                    for r in (2, 3):
                        if unit:
                            turn_probs(*unit, r)
                        if ahead and late:
                            project_q(*ahead, range((r - 2) * NR // 2, (r - 1) * NR // 2))
                        if ahead and not late:
                            project_v(*ahead, r - 2)
                        if unit:
                            weighted_values(*unit, r)

                pipeline(pe, step)
                if not last:
                    norm_tensor(nc, pe, g, (4, 5))

            @block.scalar
            def _(act):
                def stage(i, n):
                    nc.scalar.copy(ks[:, n % 2, :, :].rearrange("p c (b s) -> p c b s", s=SEQ),
                                   feat[:, keys, :, own_batches(i, n), :]).then_inc(sig.staged.sem, 1)

                def queries(i, n):
                    uu = nbody * i + n
                    act.wait_ge(sig.q_ready.sem, sig.q_ready.at(uu + 1))
                    if not rope:
                        nc.scalar.copy(q_t[:, n % 2, :, :].rearrange("p r s -> p (r s)"), bank[0][:, :]).then_inc(
                            sig.q_done.sem, 1)
                        return
                    for r in range(NR):
                        nc.scalar.activation(q_t[:, n % 2, r, :], bank[0][:, r * P:(r + 1) * P], ACT.Identity,
                                             bias=q_bias[:, r:r + 1])
                    nc.scalar.activation(k_t[:], bank[2][:, 0:P], ACT.Identity, bias=k_bias).then_inc(
                        sig.q_done.sem, 1)

                def exponentials(i, n, r):
                    ss = NR * (nbody * i + n) + r
                    act.wait_ge(sig.shifted.sem, sig.shifted.at(ss + 1))
                    nc.scalar.activation(probs[:, r % 2, :], shifted[:, r % 2, :], ACT.Exp,
                                         scale=1.0 if bias is not None else scale).then_inc(sig.exp_done.sem, 1)

                def turned(i, n, r):
                    ss = NR * (nbody * i + n) + r
                    act.wait_ge(sig.pt_ready.sem, sig.pt_ready.at(ss + 1))
                    nc.scalar.copy(p_t[:], bank[6][:, :]).then_inc(sig.pt_done.sem, 1)

                def output(i, n):
                    uu = nbody * i + n
                    act.wait_ge(sig.attn_turned.sem, sig.attn_turned.at(uu + 1))
                    nc.scalar.copy(attn_t[:].rearrange("p r s -> p (r s)"), bank[1][:, :]).then_inc(
                        sig.attn_taken.sem, 1)

                act.wait_ge(g.home_in[g.stage.home], g.stage.arrived)

                def step(unit, ahead, back):
                    if ahead:
                        stage(*ahead)
                    if unit:
                        exponentials(*unit, 0)
                    if back and out_proj:
                        output(*back)
                    if unit:
                        exponentials(*unit, 1)
                        turned(*unit, 0)
                        exponentials(*unit, 2)
                    if ahead and rope:
                        queries(*ahead)
                    if unit:
                        turned(*unit, 1)
                        exponentials(*unit, 3)
                        turned(*unit, 2)
                        turned(*unit, 3)
                    if ahead and not rope:
                        queries(*ahead)

                pipeline(act, step)
                if not last:
                    norm_scalar(nc, act, g, (4, 5))

            @block.vector
            def _(dve):
                def spread_values(i, n):
                    uu = nbody * i + n
                    dve.wait_ge(sig.v_ready.sem, sig.v_ready.at(uu + 1))
                    if not rope:
                        dve.wait_ge(sig.k_ready.sem, sig.k_ready.at(uu + 1))
                    vals = bank[2][:, 2 * P:4 * P]
                    if rope:
                        steps = Steps(sig.rope_step, 7 * uu + 6)
                        nc.vector.tensor_tensor(v_sum[:].rearrange("p (b c) -> p b c", b=2),
                                                vals.rearrange("p (b c) -> p b c", b=2), over(v_bias, (1, 2)),
                                                ALU.add).then_inc(steps.count(), 1)
                        dve.wait_ge(sig.rope_step.sem, steps.so_far())
                        vals = v_sum[:]
                    nc.vector.tensor_tensor(
                        v_diag[:, n % 2, :, :, :, 0:ND].rearrange("p b j h d -> p (b j) h d"),
                        vals.rearrange("p (bj h d) -> p bj h d", h=2, d=ND),
                        over(half_of, (1, 2 * blocks), (3, ND)), ALU.mult).then_inc(sig.v_done.sem, 1)

                def spread_keys(i, n):
                    uu = nbody * i + n
                    key = bank[2][:, 0:P]
                    dve.wait_ge(sig.k_ready.sem, sig.k_ready.at(uu + 1))
                    if rope:
                        steps = Steps(sig.rope_step, 7 * uu)
                        own_q = q_t[:, n % 2, :, :]
                        dve.wait_ge(sig.rotated.sem, sig.rotated.at(uu + 1))
                        nc.vector.tensor_tensor(turned_q[:].rearrange("p (a s) -> p a s", s=SEQ),
                                                bank[1][:, :].rearrange("p (a s) -> p a s", s=SEQ),
                                                over(sin, (1, 2 * NR)), ALU.mult).then_inc(steps.count(), 1)
                        nc.vector.tensor_tensor(turned_k[:].rearrange("p (a s) -> p a s", s=SEQ),
                                                bank[0][:, 0:P].rearrange("p (a s) -> p a s", s=SEQ),
                                                over(sin, (1, 2)), ALU.mult).then_inc(steps.count(), 1)
                        q_rows = own_q.rearrange("p r (b s) -> p (r b) s", s=SEQ)
                        k_rows = k_t[:].rearrange("p (b s) -> p b s", s=SEQ)
                        nc.vector.tensor_tensor(q_rows, q_rows, over(cos, (1, 2 * NR)), ALU.mult).then_inc(
                            steps.count(), 1)
                        nc.vector.tensor_tensor(k_rows, k_rows, over(cos, (1, 2)), ALU.mult).then_inc(
                            steps.count(), 1)
                        dve.wait_ge(sig.rope_step.sem, steps.so_far())
                        q_flat = own_q.rearrange("p r s -> p (r s)")
                        nc.vector.tensor_tensor(q_flat, q_flat, turned_q[:], ALU.add).then_inc(steps.count(), 1)
                        nc.vector.tensor_tensor(k_t[:], k_t[:], turned_k[:], ALU.add).then_inc(steps.count(), 1)
                        dve.wait_ge(sig.rope_step.sem, steps.so_far())
                        key = k_t[:]
                    for b in range(2):
                        ins = nc.vector.tensor_tensor(k_diag[:, n % 2, b, :, :],
                                                      over(key[:, b * SEQ:(b + 1) * SEQ], (1, KV)),
                                                      over(head_of, (2, SEQ)), ALU.mult)
                    ins.then_inc(sig.kd_done.sem, 1)

                def softmax(i, n, r):
                    ss = NR * (nbody * i + n) + r
                    dve.wait_ge(sig.s_ready.sem, sig.s_ready.at(ss + 1))
                    raw = bank[4 + r % 2][:, :]
                    sh = shifted[:, r % 2, :]
                    m = mx[:, r % 2, :]
                    src = raw
                    if bias is not None:
                        if isinstance(i, int) and i == 0 and n == 0 and r == 0:
                            dve.wait_ge(sig.small_in.sem, sig.small_in.at(16))
                        nc.vector.scalar_tensor_tensor(sh, raw, scale, bias_sb[:, r, :], ALU.mult, ALU.add).then_inc(
                            sig.s_read.sem, 1)
                        dve.wait_ge(sig.s_read.sem, sig.s_read.at(ss + 1))
                        src = sh
                    rows = src.rearrange("p (h k) -> p h k", k=SEQ)
                    nc.vector.tensor_reduce(m, rows, AX.X, ALU.max).then_inc(sig.row_max.sem, 1)
                    dve.wait_ge(sig.row_max.sem, sig.row_max.at(ss + 1))
                    nc.vector.tensor_tensor(sh.rearrange("p (h k) -> p h k", k=SEQ), rows, over(m, (2, SEQ)),
                                            ALU.subtract).then_inc(sig.shifted.sem, 1)

                def normalise(i, n):
                    uu = nbody * i + n
                    steps = Steps(sig.row_sum, 2 * uu)
                    dve.wait_ge(sig.o_ready.sem, sig.o_ready.at(uu + 1))
                    first = (NR - 1) * KV
                    parts = [(o_banks[0][:, 0:first * (ND + 1)], 0, first),
                             (o_banks[1][:, 0:KV * (ND + 1)], first, HEADS)]
                    for ob, lo, hi in parts:
                        rows = ob.rearrange("p (h d) -> p h d", d=ND + 1)
                        nc.vector.reciprocal(recip[:, lo:hi], rows[:, :, ND]).then_inc(steps.count(), 1)
                    dve.wait_ge(sig.row_sum.sem, steps.so_far())
                    for ob, lo, hi in parts:
                        rows = ob.rearrange("p (h d) -> p h d", d=ND + 1)
                        ins = nc.vector.tensor_tensor(attn[:, lo:hi, :], rows[:, :, 0:ND],
                                                      over(recip[:, lo:hi], (2, ND)), ALU.mult)
                    ins.then_inc(sig.o_done.sem, 1)
                    if not out_proj:
                        dve.wait_ge(sig.o_done.sem, sig.o_done.at(uu + 1))
                        tile = x[:, bass.ds(uu, 1), :].rearrange("p t (k r d) -> p (t r) k d", k=KV, r=NR)
                        nc.vector.tensor_tensor(tile, tile, attn[:].rearrange("p (r k) d -> p r k d", r=NR),
                                                ALU.add).then_inc(sig.added.sem, 1)

                def add(i, n):
                    uu = nbody * i + n
                    dve.wait_ge(sig.y_ready.sem, sig.y_ready.at(uu + 1))
                    tile = x[:, bass.ds(uu, 1), :].rearrange("p t c -> p (t c)")
                    nc.vector.tensor_tensor(tile, tile, bank[0][:, :], ALU.add).then_inc(sig.added.sem, 1)

                head = Steps(sig.dve_step)
                dve.wait_ge(g.home_in[g.stage.home], g.stage.arrived)
                nc.vector.memset(v_diag[:], 0.0).then_inc(head.count(), 1)
                dve.wait_ge(sig.dve_step.sem, head.so_far())
                for par in range(2):
                    for h in range(2):
                        nc.vector.tensor_copy(v_diag[:, par, :, :, h, ND:ND + 1].rearrange("p b j d -> p (b j) d"),
                                              over(half_of[:, h:h + 1], (1, 2 * blocks))).then_inc(head.count(), 1)
                dve.wait_ge(sig.dve_step.sem, head.so_far())

                def step(unit, ahead, back):
                    if not unit and not ahead:
                        for t in range(TILES - 3):
                            norm_tile(nc, dve, g, t, t + 1)
                    if back:
                        normalise(*back)
                    if unit:
                        softmax(*unit, 0)
                        softmax(*unit, 1)
                    if ahead and not rope:
                        spread_values(*ahead)
                        spread_keys(*ahead)
                    if unit:
                        softmax(*unit, 2)
                    if back and out_proj:
                        add(*back)
                    if unit:
                        softmax(*unit, 3)
                    if ahead and rope:
                        spread_keys(*ahead)
                        spread_values(*ahead)

                pipeline(dve, step)
                for t in range(TILES - 3, TILES):
                    norm_tile(nc, dve, g, t, t + 1)
                norm_scale(nc, dve, g, TILES - 1)


def in_home(g, *widths):
    at, pieces = 0, []
    for width in widths:
        pieces.append(g.home[:, at:at + width])
        at += width
    return pieces



def routed_ffn(nc, g, name, last, experts, rank, chosen, scaling, expert_bias=False, out_bias=False):
    sig, feat, x, bank = g.sig, g.feat, g.x, g.bank
    er = experts * rank
    cols = DIM + experts + er
    per_bank = 512 // er
    with ExitStack() as ctx:
        def sb(what, shape, dt=F32):
            return ctx.enter_context(nc.sbuf_tensor(f"{name}_{what}", shape, dt))
        w, up, before, e_bias, o_bias = in_home(g, CH * cols, DIM, experts * experts, experts * expert_bias,
                                                DIM * out_bias)
        w = w.rearrange("p (c n) -> p c n", c=CH)
        up = up[0:er, :]
        before = before.rearrange("p (a b) -> p a b", a=experts)
        logits = sb("logits", [P, TILES, experts])
        larger = sb("larger", [P, TILES, experts, experts])
        equal = sb("equal", [P, TILES, experts, experts])
        place = sb("place", [P, TILES, experts])
        weight = sb("weight", [P, TILES, experts])
        powers = sb("powers", [P, TILES, experts])
        top = sb("top", [P, TILES])
        z = sb("z", [P, 2, er])
        z_t = sb("z_t", [er, 2, P])
        turn_banks = (bank[0], bank[7])

        with nc.Block() as block:
            @block.sync
            def _(sp):
                load_ahead(sp, g)
                if last:
                    norm_sync(nc, sp, g)

            @block.gpsimd
            def _(pool):
                if out_bias:
                    pool.wait_ge(g.home_in[g.stage.home], g.stage.arrived)
                    nc.gpsimd.tensor_tensor(x[:], x[:], over(o_bias, (1, TILES)), ALU.add).then_inc(
                        sig.prepared.sem, 1)
                norm_pool(nc, pool, g)

            @block.tensor
            def _(pe):
                def features(t, c):
                    return feat[:, SELF, c, 2 * t:2 * t + 2, :].rearrange("p b s -> p (b s)")

                def base(t):
                    if t >= 4:
                        pe.wait_ge(sig.added.sem, sig.added.at(t - 3))
                    for c in range(CH):
                        nc.tensor.matmul(bank[3 + t % 4][:, :], features(t, c), w[:, c, 0:DIM],
                                         start=(c == 0), stop=False)

                pe.wait_ge(g.home_in[g.stage.home], g.stage.arrived)
                for t in range(TILES):
                    for c in range(CH):
                        mm = nc.tensor.matmul(bank[0][:, t * experts:(t + 1) * experts], features(t, c),
                                              w[:, c, DIM:DIM + experts], start=(c == 0), stop=(c == CH - 1))
                mm.then_inc(sig.logits_ready.sem, 1)
                for t in range(TILES):
                    at = t % per_bank * er
                    for c in range(CH):
                        mm = nc.tensor.matmul(bank[1 + t // per_bank][:, at:at + er], features(t, c),
                                              w[:, c, DIM + experts:cols], start=(c == 0), stop=(c == CH - 1))
                mm.then_inc(sig.z_ready.sem, 1)
                base(0)
                base(1)
                for t in range(TILES):
                    pe.wait_ge(sig.z_weighted.sem, t + 1)
                    if t >= 2:
                        pe.wait_ge(sig.z_turned.sem, t - 1)
                    nc.tensor.transpose(turn_banks[t % 2][0:er, 0:P], z[:, t % 2, :], g.ident[:]).then_inc(
                        sig.z_turning.sem, 1)
                    if t + 2 < TILES:
                        base(t + 2)
                    pe.wait_ge(sig.z_turned.sem, t + 1)
                    nc.tensor.matmul(bank[3 + t % 4][:, :], z_t[:, t % 2, :], up, start=False,
                                     stop=True).then_inc(sig.y_ready.sem, 1)
                if not last:
                    norm_tensor(nc, pe, g, (0, 1))

            @block.scalar
            def _(act):
                if chosen > 1:
                    act.wait_ge(sig.shifted.sem, sig.shifted.at(1))
                    nc.scalar.activation(powers[:], powers[:], ACT.Exp).then_inc(sig.exp_done.sem, 1)
                for t in range(TILES):
                    act.wait_ge(sig.z_turning.sem, t + 1)
                    nc.scalar.copy(z_t[:, t % 2, :], turn_banks[t % 2][0:er, 0:P]).then_inc(sig.z_turned.sem, 1)
                if not last:
                    norm_scalar(nc, act, g, (0, 1))

            @block.vector
            def _(dve):
                steps = Steps(sig.dve_step)
                dve.wait_ge(g.home_in[g.stage.home], g.stage.arrived)
                dve.wait_ge(sig.logits_ready.sem, 1)
                raw = bank[0][:, 0:TILES * experts].rearrange("p (t e) -> p t e", e=experts)
                if expert_bias:
                    nc.vector.tensor_tensor(logits[:], raw, over(e_bias, (1, TILES)), ALU.add).then_inc(
                        steps.count(), 1)
                else:
                    nc.vector.tensor_copy(logits[:], raw).then_inc(steps.count(), 1)
                dve.wait_ge(sig.dve_step.sem, steps.so_far())
                if chosen > 1:
                    nc.vector.tensor_reduce(top[:], logits[:], AX.X, ALU.max).then_inc(steps.count(), 1)
                    dve.wait_ge(sig.dve_step.sem, steps.so_far())
                    nc.vector.tensor_tensor(powers[:], logits[:], over(top[:], (2, experts)),
                                            ALU.subtract).then_inc(sig.shifted.sem, 1)
                other, own = over(logits[:], (2, experts)), over(logits[:], (3, experts))
                nc.vector.tensor_tensor(larger[:], other, own, ALU.is_gt).then_inc(steps.count(), 1)
                nc.vector.tensor_tensor(equal[:], other, own, ALU.is_equal).then_inc(steps.count(), 1)
                dve.wait_ge(sig.dve_step.sem, steps.so_far())
                nc.vector.tensor_tensor(equal[:], equal[:], over(before, (1, TILES)), ALU.mult).then_inc(
                    steps.count(), 1)
                dve.wait_ge(sig.dve_step.sem, steps.so_far())
                nc.vector.tensor_tensor(larger[:], larger[:], equal[:], ALU.add).then_inc(steps.count(), 1)
                dve.wait_ge(sig.dve_step.sem, steps.so_far())
                nc.vector.tensor_reduce(place[:], larger[:], AX.X, ALU.add).then_inc(steps.count(), 1)
                dve.wait_ge(sig.dve_step.sem, steps.so_far())
                nc.vector.tensor_scalar(weight[:], place[:], float(chosen), None, ALU.is_lt).then_inc(
                    steps.count(), 1)
                dve.wait_ge(sig.dve_step.sem, steps.so_far())
                if chosen > 1:
                    dve.wait_ge(sig.exp_done.sem, 1)
                    nc.vector.tensor_tensor(weight[:], weight[:], powers[:], ALU.mult).then_inc(steps.count(), 1)
                    dve.wait_ge(sig.dve_step.sem, steps.so_far())
                    nc.vector.tensor_reduce(top[:], weight[:], AX.X, ALU.add).then_inc(steps.count(), 1)
                    dve.wait_ge(sig.dve_step.sem, steps.so_far())
                    nc.vector.reciprocal(top[:], top[:]).then_inc(steps.count(), 1)
                    dve.wait_ge(sig.dve_step.sem, steps.so_far())
                    nc.vector.scalar_tensor_tensor(weight[:], weight[:], scaling, over(top[:], (2, experts)),
                                                   ALU.mult, ALU.mult).then_inc(steps.count(), 1)
                    dve.wait_ge(sig.dve_step.sem, steps.so_far())
                dve.wait_ge(sig.z_ready.sem, 1)

                def weigh(t):
                    if t >= 2:
                        dve.wait_ge(sig.z_turning.sem, t - 1)
                    at = t % per_bank * er
                    nc.vector.tensor_tensor(
                        z[:, t % 2, :].rearrange("p (e r) -> p e r", e=experts),
                        bank[1 + t // per_bank][:, at:at + er].rearrange("p (e r) -> p e r", e=experts),
                        over(weight[:, t, :], (2, rank)), ALU.mult).then_inc(sig.z_weighted.sem, 1)

                weigh(0)
                weigh(1)
                if out_bias:
                    dve.wait_ge(sig.prepared.sem, 1)
                for t in range(TILES):
                    if t + 2 < TILES:
                        weigh(t + 2)
                    dve.wait_ge(sig.y_ready.sem, t + 1)
                    nc.vector.tensor_tensor(x[:, t, :], x[:, t, :], bank[3 + t % 4][:, :], ALU.add).then_inc(
                        sig.added.sem, 1)
                    norm_tile(nc, dve, g, t, t + 1)
                norm_scale(nc, dve, g, TILES - 1)



def unlike_attention(nc, g, name, last, eta):
    sig, feat, x, bank = g.sig, g.feat, g.x, g.bank
    per_bank = 512 // P
    with ExitStack() as ctx:
        def sb(what, shape, dt=F32):
            return ctx.enter_context(nc.sbuf_tensor(f"{name}_{what}", shape, dt))
        eta_sb = sb("eta", [P, 1])
        twice = sb("twice", [P, TILES, DIM])
        least = sb("least", [P, TILES])
        probs = sb("probs", [P, TILES, P])
        p_t = sb("p_t", [P, 2, P])
        total = sb("total", [P, TILES])
        factor = sb("factor", [P, TILES])
        turn_banks = (bank[2], bank[3])
        out_banks = bank[4:8]

        def block_of(h):
            return slice(h * SEQ, (h + 1) * SEQ)

        with nc.Block() as block:
            @block.sync
            def _(sp):
                sp.dma_start(eta_sb[:], eta).then_inc(sig.small_in.sem, 16)
                load_ahead(sp, g)
                if last:
                    norm_sync(nc, sp, g)

            @block.gpsimd
            def _(pool):
                nc.gpsimd.memset(probs[:], 0.0).then_inc(sig.zeroed.sem, 1)
                nc.gpsimd.tensor_tensor(twice[:], x[:], x[:], ALU.add).then_inc(sig.prepared.sem, 1)
                norm_pool(nc, pool, g)

            @block.tensor
            def _(pe):
                for t in range(TILES):
                    for c in range(CH):
                        f = feat[:, SELF, c, 2 * t:2 * t + 2, :].rearrange("p b s -> p (b s)")
                        mm = nc.tensor.matmul(bank[t // per_bank][:, t % per_bank * P:(t % per_bank + 1) * P], f, f,
                                              start=(c == 0), stop=(c == CH - 1))
                    if t % per_bank == per_bank - 1:
                        mm.then_inc(sig.s_ready.sem, 1)
                for t in range(TILES):
                    pe.wait_ge(sig.exp_done.sem, 2 * (t + 1))
                    if t >= 2:
                        pe.wait_ge(sig.pt_done.sem, sig.pt_done.at(t - 1))
                    nc.tensor.transpose(turn_banks[t % 2][:, 0:P], probs[:, t, :], g.ident[:]).then_inc(
                        sig.pt_ready.sem, 1)
                    if t >= 4:
                        pe.wait_ge(sig.added.sem, sig.added.at(t - 3))
                    pe.wait_ge(sig.pt_done.sem, sig.pt_done.at(t + 1))
                    nc.tensor.matmul(out_banks[t % 4][:, :], p_t[:, t % 2, :], x[:, t, :], start=True,
                                     stop=True).then_inc(sig.y_ready.sem, 1)
                if not last:
                    norm_tensor(nc, pe, g, (0, 1))

            @block.scalar
            def _(act):
                def turned(t):
                    act.wait_ge(sig.pt_ready.sem, t + 1)
                    if t >= 2:
                        act.wait_ge(sig.y_ready.sem, t - 1)
                    nc.scalar.copy(p_t[:, t % 2, :], turn_banks[t % 2][:, 0:P]).then_inc(sig.pt_done.sem, 1)

                act.wait_ge(sig.zeroed.sem, 1)
                for t in range(TILES):
                    if t % per_bank == 0:
                        act.wait_ge(sig.least.sem, t // per_bank + 1)
                    at = t % per_bank * P
                    for h in range(2):
                        rows = block_of(h)
                        nc.scalar.activation(probs[rows, t, rows],
                                             bank[t // per_bank][rows, at + h * SEQ:at + (h + 1) * SEQ], ACT.Exp,
                                             bias=least[rows, t:t + 1], scale=-1.0,
                                             accum_out=total[rows, t:t + 1]).then_inc(sig.exp_done.sem, 1)
                    if t >= 2:
                        turned(t - 2)
                turned(TILES - 2)
                turned(TILES - 1)
                if not last:
                    norm_scalar(nc, act, g, (0, 1))

            @block.vector
            def _(dve):
                steps = Steps(sig.dve_step)
                for n in range(TILES // per_bank):
                    dve.wait_ge(sig.s_ready.sem, n + 1)
                    for h in range(2):
                        rows = block_of(h)
                        src = bank[n][rows, :].rearrange("p (t k) -> p t k", k=P)[:, :, rows]
                        mm = nc.vector.tensor_reduce(least[rows, n * per_bank:(n + 1) * per_bank], src, AX.X,
                                                     ALU.min)
                    mm.then_inc(sig.least.sem, 1)
                for t in range(TILES):
                    if t == 0:
                        dve.wait_ge(sig.exp_done.sem, 2 * TILES)
                        nc.vector.reciprocal(factor[:], total[:]).then_inc(steps.count(), 1)
                        dve.wait_ge(sig.small_in.sem, 16)
                        dve.wait_ge(sig.dve_step.sem, steps.so_far())
                        nc.vector.tensor_scalar(factor[:], factor[:], eta_sb[:, 0:1], None, ALU.mult).then_inc(
                            steps.count(), 1)
                        dve.wait_ge(sig.dve_step.sem, steps.so_far())
                        dve.wait_ge(sig.prepared.sem, 1)
                    dve.wait_ge(sig.y_ready.sem, t + 1)
                    nc.vector.scalar_tensor_tensor(x[:, t, :], out_banks[t % 4][:, :], factor[:, t:t + 1],
                                                   twice[:, t, :], ALU.mult, ALU.add).then_inc(sig.added.sem, 1)
                    norm_tile(nc, dve, g, t, t + 1)
                norm_scale(nc, dve, g, TILES - 1)



BOTTLE, ROUTE, SLOTS, TOP, VALUE = 64, 48, 128, 8, 32
TAU_LOW, TAU_HIGH, EARLY_EXIT = 0.5, 2.0, 0.05
GELU_CUBE, GELU_SCALE = 0.044715, math.sqrt(2.0 / math.pi)


def memory_ffn(nc, g, name, last):
    sig, feat, x, bank = g.sig, g.feat, g.x, g.bank
    hidden = P
    four = 512 // SLOTS
    groups = TILES // four
    wcols = BOTTLE + hidden + VALUE + SLOTS
    with ExitStack() as ctx:
        def sb(what, shape, dt=F32):
            return ctx.enter_context(nc.sbuf_tensor(f"{name}_{what}", shape, dt))
        w, small, w_vu, log_rel, cols = in_home(g, CH * wcols, ROUTE + SLOTS, DIM, SLOTS, 5)
        w = w.rearrange("p (c n) -> p c n", c=CH)
        small = small[0:BOTTLE, :]
        w_vu = w_vu[0:VALUE, :]
        q_t = sb("q_t", [BOTTLE, TOKENS])
        rq_t = sb("rq_t", [ROUTE, TOKENS])
        rk_t = sb("rk_t", [ROUTE, SLOTS])
        down = sb("down", [VALUE, SLOTS])
        slot_values = sb("slot_values", [SLOTS, DIM])
        y = sb("y", [P, TOKENS])
        inner = sb("inner", [P, TOKENS])
        th = sb("th", [P, TOKENS])
        route = sb("route", [P, four, SLOTS])
        rest = sb("rest", [P, four, SLOTS])
        top = sb("top", [P, four, TOP])
        scores = sb("scores", [P, four, SLOTS])
        mx = sb("mx", [P, four])
        probs = sb("probs", [P, groups, four, SLOTS])
        p_t = sb("p_t", [P, groups, four * P])
        total = sb("total", [P, TILES])
        stats = sb("stats", [P, TILES, 6])
        mv = sb("mv", [P, TILES, 2])
        log_var = sb("log_var", [P, TILES])
        log_sum = sb("log_sum", [P, 1])
        ones = sb("ones", [P, P])
        mean = sb("mean", [P, 1])
        u = sb("u", [P, TILES])
        gate = sb("gate", [P, TILES])
        w_q = (0, BOTTLE)
        w_u1 = (BOTTLE, BOTTLE + hidden)
        w_vd = (BOTTLE + hidden, BOTTLE + hidden + VALUE)
        values = (BOTTLE + hidden + VALUE, wcols)
        out_banks = (bank[7], bank[0], bank[4])

        with nc.Block() as block:
            @block.sync
            def _(sp):
                load_ahead(sp, g)
                if last:
                    norm_sync(nc, sp, g)

            @block.gpsimd
            def _(pool):
                for n in range(2):
                    part = slice(n * 512, (n + 1) * 512)
                    pool.wait_ge(sig.y_squared.sem, n + 1)
                    nc.gpsimd.tensor_scalar(inner[:, part], inner[:, part], GELU_CUBE, 1.0, ALU.mult,
                                            ALU.add).then_inc(sig.pool_step.sem, 1)
                    pool.wait_ge(sig.pool_step.sem, n + 1)
                    nc.gpsimd.tensor_tensor(inner[:, part], inner[:, part], y[:, part], ALU.mult).then_inc(
                        sig.inner_done.sem, 1)
                pool.wait_ge(sig.x_read.sem, 1)
                nc.gpsimd.tensor_tensor(x[:], x[:], x[:], ALU.add).then_inc(sig.prepared.sem, 1)
                norm_pool(nc, pool, g)

            @block.tensor
            def _(pe):
                def tokens_at(n, c):
                    return feat[:, SELF, c, n * 8:(n + 1) * 8, :].rearrange("p b s -> p (b s)")

                def project(dst, which, n):
                    for c in range(CH):
                        mm = nc.tensor.matmul(dst, w[:, c, which[0]:which[1]], tokens_at(n, c), start=(c == 0),
                                              stop=(c == CH - 1))
                    return mm

                pe.wait_ge(g.home_in[g.stage.home], g.stage.arrived)
                for n in range(2):
                    project(bank[n][0:BOTTLE, :], w_q, n).then_inc(sig.q_ready.sem, 1)
                nc.tensor.matmul(bank[6][0:ROUTE, 0:SLOTS], small[:, 0:ROUTE], small[:, ROUTE:ROUTE + SLOTS],
                                 start=True, stop=True)
                for c in range(CH):
                    mm = nc.tensor.matmul(bank[6][0:VALUE, SLOTS:2 * SLOTS], w[:, c, w_vd[0]:w_vd[1]],
                                          w[:, c, values[0]:values[1]], start=(c == 0), stop=(c == CH - 1))
                mm.then_inc(sig.k_ready.sem, 1)
                for n in range(2):
                    pe.wait_ge(sig.q_done.sem, sig.q_done.at(n + 1))
                    nc.tensor.matmul(bank[4 + n][0:ROUTE, :], small[:, 0:ROUTE], q_t[:, n * 512:(n + 1) * 512],
                                     start=True, stop=True).then_inc(sig.rq_ready.sem, 1)
                pe.wait_ge(sig.k_done.sem, sig.k_done.at(2))
                nc.tensor.matmul(bank[7][:, :], down[:], w_vu, start=True, stop=True).then_inc(
                    sig.v_ready.sem, 1)
                for n in range(2):
                    project(bank[2 + n][:, :], w_u1, n).then_inc(sig.hidden_ready.sem, 1)
                pe.wait_ge(sig.rq_done.sem, groups)
                for n in range(groups):
                    for tt in range(four):
                        t = n * four + tt
                        nc.tensor.matmul(bank[n][:, tt * SLOTS:(tt + 1) * SLOTS], rq_t[:, t * P:(t + 1) * P],
                                         rk_t[:], start=True, stop=True)
                        mm = nc.tensor.matmul(bank[4 + n][:, tt * SLOTS:(tt + 1) * SLOTS],
                                              q_t[:, t * P:(t + 1) * P], small[:, ROUTE:ROUTE + SLOTS],
                                              start=True, stop=True)
                    mm.then_inc(sig.s_ready.sem, 1)
                pe.wait_ge(sig.log_summed.sem, 1)
                nc.tensor.matmul(bank[6][:, TILES:TILES + 1], ones[:], log_sum[:], start=True, stop=True)
                pe.wait_ge(sig.gelu_done.sem, 2)
                for t in range(TILES):
                    mm = nc.tensor.matmul(bank[6][:, t:t + 1], y[:, t * P:(t + 1) * P], cols[:, 1:2], start=True,
                                          stop=True)
                mm.then_inc(sig.learned_ready.sem, 1)
                for n in range(groups):
                    pe.wait_ge(sig.exp_done.sem, four * (n + 1))
                    for tt in range(four):
                        mm = nc.tensor.transpose(bank[2 + n][:, tt * P:(tt + 1) * P], probs[:, n, tt, :],
                                                 g.ident[:])
                    mm.then_inc(sig.pt_ready.sem, 1)
                    pe.wait_ge(sig.pt_done.sem, sig.pt_done.at(n + 1))
                    for tt in range(four):
                        t = n * four + tt
                        if t == 0:
                            pe.wait_ge(sig.v_done.sem, sig.v_done.at(1))
                        if t >= 3:
                            pe.wait_ge(sig.added.sem, sig.added.at(t - 2))
                        nc.tensor.matmul(out_banks[t % 3][:, :], p_t[:, n, tt * P:(tt + 1) * P], slot_values[:],
                                         start=True, stop=True).then_inc(sig.y_ready.sem, 1)
                if not last:
                    norm_tensor(nc, pe, g, (1, 5))

            @block.scalar
            def _(act):
                for n in range(2):
                    act.wait_ge(sig.q_ready.sem, n + 1)
                    nc.scalar.copy(q_t[:, n * 512:(n + 1) * 512], bank[n][0:BOTTLE, :]).then_inc(sig.q_done.sem, 1)
                act.wait_ge(sig.k_ready.sem, 1)
                nc.scalar.copy(rk_t[:], bank[6][0:ROUTE, 0:SLOTS]).then_inc(sig.k_done.sem, 1)
                nc.scalar.copy(down[:], bank[6][0:VALUE, SLOTS:2 * SLOTS]).then_inc(sig.k_done.sem, 1)
                for n in range(2):
                    act.wait_ge(sig.rq_ready.sem, n + 1)
                    nc.scalar.copy(rq_t[:, n * 512:(n + 1) * 512], bank[4 + n][0:ROUTE, :]).then_inc(
                        sig.rq_done.sem, 1)
                act.wait_ge(sig.v_ready.sem, 1)
                nc.scalar.copy(slot_values[:], bank[7][:, :]).then_inc(sig.v_done.sem, 1)
                act.wait_ge(g.home_in[g.stage.home], g.stage.arrived)
                for n in range(2):
                    part = slice(n * 512, (n + 1) * 512)
                    act.wait_ge(sig.hidden_ready.sem, n + 1)
                    nc.scalar.activation(y[:, part], bank[2 + n][:, :], ACT.Identity, bias=cols[:, 0:1])
                    nc.scalar.activation(inner[:, part], bank[2 + n][:, :], ACT.Square,
                                         bias=cols[:, 0:1]).then_inc(sig.y_squared.sem, 1)
                for n in range(2):
                    part = slice(n * 512, (n + 1) * 512)
                    act.wait_ge(sig.inner_done.sem, n + 1)
                    nc.scalar.activation(th[:, part], inner[:, part], ACT.Tanh, scale=GELU_SCALE).then_inc(
                        sig.tanh_done.sem, 1)
                act.wait_ge(sig.x_read.sem, 1)
                nc.scalar.activation(log_var[:], log_var[:], ACT.Ln).then_inc(sig.log_done.sem, 1)
                for n in range(groups):
                    act.wait_ge(sig.shifted.sem, sig.shifted.at(n + 1))
                    for tt in range(four):
                        t = n * four + tt
                        nc.scalar.activation(probs[:, n, tt, :], probs[:, n, tt, :], ACT.Exp,
                                             accum_out=total[:, t:t + 1]).then_inc(sig.exp_done.sem, 1)
                    act.wait_ge(sig.logistic_in.sem, n + 1)
                    nc.scalar.activation(gate[:], gate[:], ACT.Tanh, scale=0.5).then_inc(sig.logistic.sem, 1)
                    act.wait_ge(sig.pt_ready.sem, n + 1)
                    nc.scalar.copy(p_t[:, n, :], bank[2 + n][:, :]).then_inc(sig.pt_done.sem, 1)
                if not last:
                    norm_scalar(nc, act, g, (1, 5))

            @block.vector
            def _(dve):
                steps = Steps(sig.dve_step)

                def settle():
                    dve.wait_ge(sig.dve_step.sem, steps.so_far())

                nc.vector.memset(ones[:], 1.0)
                for t in range(TILES):
                    nc.vector.bn_stats(stats[:, t, :], x[:, t, :]).then_inc(steps.count(), 1)
                settle()
                for t in range(TILES):
                    nc.vector.bn_aggr(mv[:, t, :], stats[:, t, :]).then_inc(steps.count(), 1)
                settle()
                nc.vector.tensor_scalar(log_var[:], mv[:, :, 1], 1.0, None, ALU.add).then_inc(sig.x_read.sem, 1)
                for n in range(2):
                    part = slice(n * 512, (n + 1) * 512)
                    dve.wait_ge(sig.tanh_done.sem, n + 1)
                    nc.vector.scalar_tensor_tensor(y[:, part], th[:, part], 1.0, y[:, part], ALU.add,
                                                   ALU.mult).then_inc(sig.gelu_done.sem, 1)
                dve.wait_ge(sig.log_done.sem, 1)
                nc.vector.tensor_reduce(log_sum[:], log_var[:], AX.X, ALU.add).then_inc(sig.log_summed.sem, 1)
                dve.wait_ge(g.home_in[g.stage.home], g.stage.arrived)

                def choose(n):
                    dve.wait_ge(sig.s_ready.sem, n + 1)
                    rel = over(log_rel, (1, four))
                    nc.vector.scalar_tensor_tensor(route[:], bank[n][:, :].rearrange("p (t k) -> p t k", t=four),
                                                   ROUTE ** -0.5, rel, ALU.mult, ALU.add).then_inc(steps.count(), 1)
                    nc.vector.scalar_tensor_tensor(scores[:],
                                                   bank[4 + n][:, :].rearrange("p (t k) -> p t k", t=four),
                                                   BOTTLE ** -0.5, rel, ALU.mult, ALU.add).then_inc(steps.count(), 1)
                    settle()
                    for tt in range(four):
                        nc.vector.max(top[:, tt, :], route[:, tt, :]).then_inc(steps.count(), 1)
                    settle()
                    for tt in range(four):
                        nc.vector.match_replace(rest[:, tt, :], top[:, tt, :], route[:, tt, :], NEG).then_inc(
                            steps.count(), 1)
                    settle()
                    nc.vector.tensor_tensor(rest[:], rest[:], route[:], ALU.is_equal).then_inc(steps.count(), 1)
                    settle()
                    nc.vector.scalar_tensor_tensor(scores[:], rest[:], NEG, scores[:], ALU.mult,
                                                   ALU.add).then_inc(steps.count(), 1)
                    settle()
                    nc.vector.tensor_reduce(mx[:], scores[:], AX.X, ALU.max).then_inc(steps.count(), 1)
                    settle()
                    nc.vector.tensor_tensor(probs[:, n, :, :], scores[:], over(mx[:], (2, SLOTS)),
                                            ALU.subtract).then_inc(sig.shifted.sem, 1)

                def logistic(n):
                    dve.wait_ge(sig.logistic.sem, n + 1)
                    nc.vector.tensor_scalar(gate[:], gate[:], 1.0, 0.5, ALU.add, ALU.mult).then_inc(
                        steps.count(), 1)
                    settle()

                choose(0)
                dve.wait_ge(sig.learned_ready.sem, 1)
                nc.vector.tensor_scalar(mean[:], bank[6][:, TILES:TILES + 1], 1.0 / TOKENS, 1e-6, ALU.mult,
                                        ALU.add).then_inc(steps.count(), 1)
                nc.vector.tensor_scalar(gate[:], bank[6][:, 0:TILES], 0.5, cols[:, 2:3], ALU.mult,
                                        ALU.add).then_inc(sig.logistic_in.sem, 1)
                settle()
                nc.vector.reciprocal(mean[:], mean[:]).then_inc(steps.count(), 1)
                settle()
                nc.vector.tensor_scalar(u[:], log_var[:], mean[:, 0:1], 0.5, ALU.mult, ALU.mult).then_inc(
                    steps.count(), 1)
                settle()
                choose(1)
                logistic(0)
                nc.vector.scalar_tensor_tensor(u[:], gate[:], 2.5, u[:], ALU.mult, ALU.add).then_inc(
                    steps.count(), 1)
                settle()
                nc.vector.tensor_scalar(u[:], u[:], 0.0, 5.0, ALU.max, ALU.min).then_inc(steps.count(), 1)
                settle()
                nc.vector.tensor_scalar(u[:], u[:], TAU_LOW, 1.0 / (TAU_HIGH - TAU_LOW), ALU.subtract,
                                        ALU.mult).then_inc(steps.count(), 1)
                settle()
                nc.vector.tensor_scalar(u[:], u[:], 0.0, 1.0, ALU.max, ALU.min).then_inc(steps.count(), 1)
                settle()
                nc.vector.tensor_scalar(gate[:], u[:], cols[:, 3:4], cols[:, 4:5], ALU.mult, ALU.add).then_inc(
                    sig.logistic_in.sem, 1)
                logistic(1)
                nc.vector.scalar_tensor_tensor(gate[:], gate[:], EARLY_EXIT, gate[:], ALU.is_ge,
                                               ALU.mult).then_inc(steps.count(), 1)
                dve.wait_ge(sig.exp_done.sem, TILES)
                nc.vector.reciprocal(total[:], total[:]).then_inc(steps.count(), 1)
                settle()
                nc.vector.tensor_tensor(gate[:], gate[:], total[:], ALU.mult).then_inc(steps.count(), 1)
                settle()
                dve.wait_ge(sig.prepared.sem, 1)
                for t in range(TILES):
                    dve.wait_ge(sig.y_ready.sem, t + 1)
                    nc.vector.scalar_tensor_tensor(x[:, t, :], out_banks[t % 3][:, :], gate[:, t:t + 1], x[:, t, :],
                                                   ALU.mult, ALU.add).then_inc(sig.added.sem, 1)
                    norm_tile(nc, dve, g, t, t + 1)
                norm_scale(nc, dve, g, TILES - 1)



MIX, MIX_RANK, MIX_KEY = 8, 64, 128


def mixed_ffn(nc, g, name, last):
    sig, feat, x, bank = g.sig, g.feat, g.x, g.bank
    pairs = MIX * MIX_RANK // P
    half_b = BATCH // 2
    wcols = 2 * DIM + MIX_KEY
    with ExitStack() as ctx:
        def sb(what, shape, dt=F32):
            return ctx.enter_context(nc.sbuf_tensor(f"{name}_{what}", shape, dt))
        w, keys = in_home(g, CH * wcols, MIX)
        w = w.rearrange("p (c n) -> p c n", c=CH)
        up = g.other[:, 0:pairs * DIM].rearrange("p (j n) -> p j n", j=pairs)
        sums = sb("sums", [P, CH, BATCH])
        q_t = sb("q_t", [MIX_KEY, BATCH])
        coef = sb("coef", [BATCH, MIX])
        spread = sb("spread", [BATCH, MIX, MIX_RANK])
        stat = sb("stat", [BATCH, 2])
        rows = sb("rows", [P, pairs, BATCH])
        h_t = sb("h_t", [P, pairs, TOKENS])
        came = 2 * CH * DIM
        down_at, q_at = DIM, 2 * DIM
        y_banks = (bank[4], bank[5], bank[6])

        with nc.Block() as block:
            @block.sync
            def _(sp):
                sp.dma_start(g.home[:, came:CH * wcols + MIX], g.t[name + "_w"][:, came:]).then_inc(
                    sig.small_in.sem, 16)
                if last:
                    norm_sync(nc, sp, g)

            @block.gpsimd
            def _(pool):
                norm_pool(nc, pool, g)

            @block.tensor
            def _(pe):
                def down(u):
                    half, j = u // pairs, u % pairs
                    if u >= 4:
                        pe.wait_ge(sig.h_done.sem, u - 3)
                    for c in range(CH):
                        mm = nc.tensor.matmul(
                            bank[u % 4][:, :], w[:, c, down_at + j * P:down_at + (j + 1) * P],
                            feat[:, SELF, c, half * half_b:(half + 1) * half_b, :].rearrange("p b s -> p (b s)"),
                            start=(c == 0), stop=(c == CH - 1))
                    mm.then_inc(sig.h_ready.sem, 1)

                def base(t):
                    if t >= 3:
                        pe.wait_ge(sig.added.sem, sig.added.at(t - 2))
                    for c in range(CH):
                        nc.tensor.matmul(y_banks[t % 3][:, :],
                                         feat[:, SELF, c, 2 * t:2 * t + 2, :].rearrange("p b s -> p (b s)"),
                                         w[:, c, 0:DIM], start=(c == 0), stop=False)

                def mix(t):
                    if t % 4 == 0:
                        pe.wait_ge(sig.h_done.sem, pairs * (t // 4 + 1))
                    for j in range(pairs):
                        mm = nc.tensor.matmul(y_banks[t % 3][:, :], h_t[:, j, t * P:(t + 1) * P], up[:, j, :],
                                              start=False, stop=(j == pairs - 1))
                    mm.then_inc(sig.y_ready.sem, 1)

                pe.wait_ge(g.home_in[g.stage.home], g.stage.arrived)
                pe.wait_ge(sig.small_in.sem, 16)
                down(0)
                down(1)
                pe.wait_ge(sig.sums_done.sem, 1)
                for c in range(CH):
                    mm = nc.tensor.matmul(bank[7][:, 0:BATCH], w[:, c, q_at:q_at + MIX_KEY], sums[:, c, :],
                                          start=(c == 0), stop=(c == CH - 1))
                mm.then_inc(sig.q_ready.sem, 1)
                down(2)
                pe.wait_ge(sig.q_done.sem, sig.q_done.at(1))
                nc.tensor.matmul(bank[7][0:BATCH, BATCH:BATCH + MIX], q_t[:], keys, start=True,
                                 stop=True).then_inc(sig.s_ready.sem, 1)
                down(3)
                base(0)
                pe.wait_ge(sig.coef_done.sem, 1)
                for j in range(pairs):
                    mm = nc.tensor.matmul(bank[7][:, (2 + j) * BATCH:(3 + j) * BATCH],
                                          spread[:, 2 * j:2 * j + 2, :].rearrange("b e r -> b (e r)"),
                                          g.ident[0:BATCH, 0:BATCH], start=True, stop=True)
                mm.then_inc(sig.rows_ready.sem, 1)
                base(1)
                base(2)
                mix(0)
                for u in range(4, 8):
                    down(u)
                mix(1)
                mix(2)
                for t in range(3, TILES):
                    base(t)
                    mix(t)
                if not last:
                    norm_tensor(nc, pe, g, (0, 1))

            @block.scalar
            def _(act):
                act.wait_ge(sig.q_ready.sem, 1)
                nc.scalar.mul(q_t[:], bank[7][:, 0:BATCH], 1.0 / SEQ).then_inc(sig.q_done.sem, 1)
                act.wait_ge(sig.shifted.sem, sig.shifted.at(1))
                nc.scalar.activation(coef[:], coef[:], ACT.Exp, scale=MIX_KEY ** -0.5,
                                     accum_out=stat[:, 1:2]).then_inc(sig.exp_done.sem, 1)
                if not last:
                    norm_scalar(nc, act, g, (0, 1))

            @block.vector
            def _(dve):
                steps = Steps(sig.dve_step)
                nc.vector.tensor_reduce(sums[:], feat[:, SELF, :, :, :], AX.X, ALU.add).then_inc(
                    sig.sums_done.sem, 1)
                dve.wait_ge(sig.s_ready.sem, 1)
                raw = bank[7][0:BATCH, BATCH:BATCH + MIX]
                nc.vector.tensor_reduce(stat[:, 0:1], raw, AX.X, ALU.max).then_inc(steps.count(), 1)
                dve.wait_ge(sig.dve_step.sem, steps.so_far())
                nc.vector.tensor_scalar(coef[:], raw, stat[:, 0:1], None, ALU.subtract).then_inc(
                    sig.shifted.sem, 1)
                dve.wait_ge(sig.exp_done.sem, 1)
                nc.vector.reciprocal(stat[:, 1:2], stat[:, 1:2]).then_inc(steps.count(), 1)
                dve.wait_ge(sig.dve_step.sem, steps.so_far())
                nc.vector.tensor_scalar(spread[:], over(coef[:], (2, MIX_RANK)), stat[:, 1:2], None,
                                        ALU.mult).then_inc(sig.coef_done.sem, 1)
                dve.wait_ge(sig.rows_ready.sem, 1)
                nc.vector.tensor_copy(rows[:], bank[7][:, 2 * BATCH:(2 + pairs) * BATCH].rearrange(
                    "p (j b) -> p j b", b=BATCH)).then_inc(steps.count(), 1)
                dve.wait_ge(sig.dve_step.sem, steps.so_far())

                def scale(u):
                    half, j = u // pairs, u % pairs
                    dve.wait_ge(sig.h_ready.sem, u + 1)
                    nc.vector.tensor_tensor(
                        h_t[:, j, half * 512:(half + 1) * 512].rearrange("p (b s) -> p b s", s=SEQ),
                        bank[u % 4][:, :].rearrange("p (b s) -> p b s", s=SEQ),
                        over(rows[:, j, half * half_b:(half + 1) * half_b], (2, SEQ)), ALU.mult).then_inc(
                        sig.h_done.sem, 1)

                def add(t):
                    dve.wait_ge(sig.y_ready.sem, t + 1)
                    nc.vector.tensor_tensor(x[:, t, :], x[:, t, :], y_banks[t % 3][:, :], ALU.add).then_inc(
                        sig.added.sem, 1)

                for u in range(4):
                    scale(u)
                add(0)
                for u in range(4, 8):
                    scale(u)
                norm_tile(nc, dve, g, 0, 1)
                for t in range(1, TILES):
                    add(t)
                    norm_tile(nc, dve, g, t, t + 1)
                norm_scale(nc, dve, g, TILES - 1)



def build(nc, t, out):
    with ExitStack() as ctx:
        g = Record()
        g.out, g.t = out, t
        g.x = ctx.enter_context(nc.sbuf_tensor("x", [P, TILES, DIM], F32))
        g.feat = ctx.enter_context(nc.sbuf_tensor("feat", [P, 2, CH, BATCH, SEQ], F32))
        g.ident = ctx.enter_context(nc.sbuf_tensor("ident", [P, P], F32))
        g.norm = norm_buffers(nc, ctx)
        g.minus_half = ctx.enter_context(nc.sbuf_tensor("minus_half", [P, TILES], F32))
        g.bank = [ctx.enter_context(nc.psum_tensor(f"bank{n}", [P, 512], F32)) for n in range(8)]
        g.out_written = Signal(ctx.enter_context(nc.semaphore("out_written")), 0)
        loaded = ctx.enter_context(nc.semaphore("loaded"))
        g.sig = Signals(nc, ctx)
        numbers = sorted(sem.num for sem in g.sig.all)
        assert numbers == list(range(numbers[0], numbers[-1] + 1))

        g.raw = ctx.enter_context(nc.sbuf_tensor("raw", [P, CH * GH * HD], F32))
        g.homes = [ctx.enter_context(nc.sbuf_tensor(f"home{n}", [P, HOME], F32)) for n in range(2)]
        g.home_in = [ctx.enter_context(nc.semaphore(f"home{n}_in")) for n in range(2)]
        g.x_in = ctx.enter_context(nc.semaphore("x_in"))
        g.context_in = ctx.enter_context(nc.semaphore("context_in"))

        def packed(home, name):
            return [(g.homes[home][:, 0:t[name].shape[1]], t[name])]

        def group(home, name, kv_heads):
            kv_cols = 2 * CH * kv_heads * HD
            return [(g.raw[:], t[name + "_qo"][0][:, 0:CH * GH * HD]),
                    (g.homes[home][:, 0:kv_cols], t[name + "_kv"][0])]

        narrow, wide = ND ** -0.5, HD ** -0.5
        stages = [
            Stage(1, group(1, "l0a", 1), lambda last: wide_attention(
                nc, g, "l0a", last, t["l0a_qo"], t["l0a_kv"], 1, SELF, wide, bias=t["l0a_bias"])),
            Stage(0, packed(0, "l0x_w"), lambda last: narrow_attention(nc, g, "l0x", last, CTX, narrow)),
            Stage(1, packed(1, "l0f_w"), lambda last: routed_ffn(
                nc, g, "l0f", last, 4, 8, 1, 1.0, expert_bias=True)),

            Stage(0, [], lambda last: unlike_attention(nc, g, "l1a", last, t["l1a_eta"])),
            Stage(0, group(0, "l1x", 1), lambda last: wide_attention(
                nc, g, "l1x", last, t["l1x_qo"], t["l1x_kv"], 1, "both", wide)),
            Stage(1, packed(1, "l1f_w"), lambda last: routed_ffn(
                nc, g, "l1f", last, 8, 16, 2, 2.0, out_bias=True)),

            Stage(0, packed(0, "l2a_w"), lambda last: narrow_attention(
                nc, g, "l2a", last, SELF, narrow, rope=True, out_proj=False)),
            Stage(1, group(1, "l2x", 1), lambda last: wide_attention(
                nc, g, "l2x", last, t["l2x_qo"], t["l2x_kv"], 1, CTX, wide, mask=t["l2x_mask"],
                q_norm=t["l2x_qn"], k_norm=t["l2x_kn"])),
            Stage(0, packed(0, "l2f_w"), lambda last: memory_ffn(nc, g, "l2f", last)),

            Stage(1, packed(1, "l3a_w"), lambda last: narrow_attention(
                nc, g, "l3a", last, SELF, narrow, bias=t["l3a_bias"])),
            Stage(0, group(0, "l3x", GH), lambda last: wide_attention(
                nc, g, "l3x", last, t["l3x_qo"], t["l3x_kv"], GH, CTX, wide, bias=t["l3x_bias"],
                key_mask=t["l3x_mask"])),
            Stage(0, [(g.homes[0][:, 0:2 * CH * DIM], t["l3f_w"][:, 0:2 * CH * DIM]),
                      (g.homes[1][:, 0:CH * DIM], t["l3f_up"])], lambda last: mixed_ffn(nc, g, "l3f", last)),
        ]
        totals = [0, 0]
        for stage in stages:
            totals[stage.home] += 16 * len(stage.loads)
            stage.arrived = totals[stage.home]

        with nc.Block() as block:
            @block.sync
            def _(sp):
                sp.dma_start(g.feat[:, SELF, :, :, :].rearrange("p c b s -> p (c b s)"), t["feat"][1]).then_inc(
                    loaded, 16)
                sp.dma_start(g.ident[:], t["ident"]).then_inc(loaded, 16)
                g.ahead = stages[0]
                load_ahead(sp, g)
                sp.wait_ge(loaded, 32)

            @block.vector
            def _(dve):
                nc.vector.memset(g.minus_half[:], -0.5)

        for n, stage in enumerate(stages):
            clear_signals(nc, g)
            g.stage, g.ahead = stage, (stages + [Stage(0, [], None)])[n + 1]
            g.home, g.other = g.homes[stage.home], g.homes[1 - stage.home]
            g.x_pending = 16 * TILES if n == 0 else 0
            stage.run(stage is stages[-1])



def wide_inputs(arrays, name, wq, wk, wv, wo, kv_heads):
    q = wq.reshape(CH, P, GROUPS, GH, HD).transpose(2, 1, 3, 0, 4).reshape(GROUPS, P, -1)
    o = wo.reshape(GROUPS, GH, HD, DIM).transpose(0, 2, 1, 3).reshape(GROUPS, P, -1)
    arrays[name + "_qo"] = np.concatenate([q, o], axis=2)
    n = wk.shape[1] // (kv_heads * HD)
    kv = [w.reshape(CH, P, n, kv_heads * HD).transpose(2, 1, 0, 3).reshape(n, P, -1) for w in (wk, wv)]
    arrays[name + "_kv"] = np.concatenate(kv, axis=2)


def distance_bias():
    slopes = (2.0 ** (-8.0 / HEADS)) ** np.arange(1, HEADS + 1, dtype=np.float32)
    rel = np.arange(SEQ)[:, None] - np.arange(SEQ)[None, :]
    b = -slopes[:, None, None].astype(np.float32) * np.sqrt(np.maximum(rel, 0).astype(np.float32))
    b = np.where(rel[None] >= 0, b, NEG).astype(np.float32)
    b = b.reshape(GROUPS, 2, 2, SEQ, SEQ).transpose(0, 2, 3, 1, 4)
    b = np.repeat(b[:, :, :, :, None, :], 2, axis=4)
    return np.ascontiguousarray(b.reshape(GROUPS, P, 2 * 2 * SEQ), dtype=np.float32)


def packed(*parts):
    return np.concatenate([np.concatenate([m, np.zeros((P - m.shape[0], m.shape[1]), m.dtype)]) for m in parts],
                          axis=1)


def narrow_inputs(wq, wk, wv, wo):
    q = wq.reshape(CH, P, KV, NR, ND).transpose(1, 0, 3, 2, 4).reshape(P, -1)
    kv = [m.reshape(CH, P, P).transpose(1, 0, 2).reshape(P, -1) for m in (wk, wv)]
    parts = [q] + kv
    if wo is not None:
        parts.append(wo.reshape(KV, NR, ND, DIM).transpose(0, 2, 1, 3).reshape(P, -1))
    return np.concatenate(parts, axis=1)


def linear_bias():
    slopes = (2.0 ** (-2.0 ** (-(math.log2(HEADS) - 3)))) ** np.arange(1, HEADS + 1, dtype=np.float64)
    rel = (np.arange(SEQ)[None, :] - np.arange(SEQ)[:, None]).astype(np.float32)
    b = slopes.astype(np.float32)[:, None, None] * rel[None]
    b = np.where(rel[None] <= 0, b, np.float32(NEG)).astype(np.float32)
    b = b.reshape(KV, NR, SEQ, SEQ).transpose(2, 1, 0, 3).reshape(SEQ, -1)
    return np.concatenate([b, b], axis=0)


def rope_tables():
    half = ND // 2
    turn = np.zeros((P, P), np.float32)
    for h in range(KV):
        for d in range(half):
            turn[h * ND + half + d, h * ND + d] = -1.0
            turn[h * ND + d, h * ND + half + d] = 1.0
    inv = (1.0 / 10000.0 ** (np.arange(0, ND, 2, dtype=np.float32) / ND)).astype(np.float32)
    ang = np.arange(SEQ, dtype=np.float32)[None, :] * inv[:, None]
    ang = np.tile(np.concatenate([ang, ang], axis=0), (KV, 1))
    return turn, np.cos(ang).astype(np.float32), np.sin(ang).astype(np.float32)


def chunked(*parts):
    m = np.concatenate(parts, axis=1)
    return m.reshape(CH, P, m.shape[1]).transpose(1, 0, 2).reshape(P, -1)


def rows(v):
    return np.broadcast_to(v.reshape(1, -1), (P, v.size))


def ffn_inputs(a, i):
    def before(experts):
        return rows(np.tril(np.ones((experts, experts), np.float32), -1))

    a["l0f_w"] = packed(chunked(i["L0_ffn_W_up"].T, i["L0_ffn_gate_w"].T, i["L0_ffn_lora_A"].reshape(-1, DIM).T),
                        i["L0_ffn_lora_B"].transpose(0, 2, 1).reshape(-1, DIM), before(4),
                        rows(i["L0_ffn_expert_bias"]))
    a["l1a_eta"] = rows(i["L1_attn_eta"])
    a["l1f_w"] = packed(chunked(i["L1_ffn_W_base"].T, i["L1_ffn_W_router"].T, i["L1_ffn_A"].reshape(-1, DIM).T),
                        i["L1_ffn_B"].transpose(0, 2, 1).reshape(-1, DIM), before(8), rows(i["L1_ffn_b_base"]))
    a["l2f_w"] = packed(chunked(i["L2_ffn_Wq"].T, i["L2_ffn_Wu1"].T, i["L2_ffn_Wvd"].T, i["L2_ffn_aux_values"].T),
                        i["L2_ffn_Wr"].T, i["L2_ffn_aux_keys"].T, i["L2_ffn_Wvu"].T, rows(i["L2_ffn_log_rel"]),
                        i["L2_ffn_bu1"].reshape(P, 1), i["L2_ffn_Wu2"].reshape(P, 1),
                        *[rows(i["L2_ffn_" + n]) for n in ("bu2", "gate_w1", "gate_bias")])
    down = i["L3_ffn_lora_down"].transpose(1, 0, 2).reshape(DIM, -1)
    a["l3f_w"] = packed(chunked(i["L3_ffn_W_org"].T, down, i["L3_ffn_Wq"].T), i["L3_ffn_lora_keys"].T)
    a["l3f_up"] = chunked(i["L3_ffn_lora_up"].reshape(-1, DIM))


def lay_out(i):
    i = {k: np.asarray(v) for k, v in i.items()}
    a = {}
    x = i["x"].reshape(TOKENS, DIM)
    a["x"] = x.reshape(TILES, P, DIM)
    feats = [f.reshape(BATCH, SEQ, CH, P).transpose(3, 2, 0, 1) for f in (i["ctx_4096"], i["x"])]
    a["feat"] = np.stack(feats, axis=0).reshape(2, P, -1)
    a["ident"] = np.eye(P, dtype=np.float32)
    w = i["L0_attn_w_qkv"]
    wide_inputs(a, "l0a", w[:, :HEADS * HD], w[:, HEADS * HD:HEADS * HD + GROUPS * HD],
                w[:, HEADS * HD + GROUPS * HD:], i["L0_attn_w_o"], 1)
    a["l0a_bias"] = distance_bias()
    wide_inputs(a, "l1x", i["L1_xattn_Wq"], i["L1_xattn_Wk"], i["L1_xattn_Wv"], i["L1_xattn_Wo"], 1)
    wide_inputs(a, "l2x", i["L2_xattn_q_proj_w"].T, i["L2_xattn_k_proj_w"].T, i["L2_xattn_v_proj_w"].T,
                i["L2_xattn_o_proj_w"].T, 1)
    a["l2x_mask"] = i["mask_1x1xSxS2_ff0"].reshape(SEQ, SEQ)
    a["l2x_qn"] = i["L2_xattn_q_norm_w"].reshape(P, 1)
    a["l2x_kn"] = i["L2_xattn_k_norm_w"].reshape(P, 1)
    wide_inputs(a, "l3x", i["L3_xattn_Wq"], i["L3_xattn_Wk"], i["L3_xattn_Wv"], i["L3_xattn_Wo"], GH)
    b = i["fside_Bx32xSxS2_0"].reshape(UNITS, 2, 2, GROUPS, 2, 2, SEQ, SEQ)
    a["l3x_bias"] = b.transpose(3, 5, 6, 0, 1, 4, 2, 7).reshape(GROUPS, P, -1)
    m = i["mask_BxSxS2_bk0"].transpose(1, 0, 2)
    a["l3x_mask"] = np.concatenate([m, m], axis=0)
    own = [np.repeat(np.eye(KV, dtype=np.float32), ND, axis=0), np.repeat(np.eye(2, dtype=np.float32), SEQ, axis=0)]
    a["l0x_w"] = packed(narrow_inputs(i["L0_xattn_Wq"], i["L0_xattn_Wk"], i["L0_xattn_Wv"], i["L0_xattn_Wo"]), *own)
    bq = i["L2_attn_bq"].reshape(KV, NR, ND).transpose(0, 2, 1).reshape(P, NR)
    a["l2a_w"] = packed(narrow_inputs(i["L2_attn_wq"], i["L2_attn_wk"], i["L2_attn_wv"], None), *own,
                        *rope_tables(), bq, i["L2_attn_bk"].reshape(P, 1), rows(i["L2_attn_bv"]))
    w = i["L3_attn_Wqkv"]
    wk, wv = (np.tile(w[:, DIM + n * ND:DIM + (n + 1) * ND], (1, KV)) for n in range(2))
    a["l3a_w"] = packed(narrow_inputs(w[:, :DIM], wk, wv, i["L3_attn_Wo"]), *own)
    a["l3a_bias"] = linear_bias()
    ffn_inputs(a, i)
    return {k: np.ascontiguousarray(v) for k, v in a.items()}


def kernel(**inputs):
    import concourse.bacc as bacc
    from concourse.bass_utils import run_bass_kernel_spmd

    arrays = lay_out(inputs)
    nc = bacc.Bacc("TRN2", target_bir_lowering=False, num_devices=1)
    t = {k: nc.dram_tensor("in_" + k, v.shape, mybir.dt.from_np(v.dtype), kind="ExternalInput").ap()
         for k, v in arrays.items()}
    out = nc.dram_tensor("out_0_dram", (TOKENS, DIM), F32, kind="ExternalOutput").ap()
    build(nc, t, out)
    r = run_bass_kernel_spmd(nc, [{"in_" + k: v for k, v in arrays.items()}], core_ids=[0])
    return r.results[0]["out_0_dram"].reshape(BATCH, SEQ, DIM)
```
